# Optimizing a Trainium2 kernel written in Bass

```python
import numpy as np
import jax
import jax.numpy as jnp

def _softmax(x, axis=-1):
    return jax.nn.softmax(x, axis=axis)

def _gelu(x):
    return jax.nn.gelu(x, approximate=True)

def _silu(x):
    return jax.nn.silu(x)

def _sigmoid(x):
    return jax.nn.sigmoid(x)

def _layernorm(x, axis=-1, eps=1e-05):
    m = jnp.mean(x, axis=axis, keepdims=True)
    v = jnp.var(x, axis=axis, keepdims=True)
    return (x - m) / jnp.sqrt(v + eps)

def _scatter_add(tgt, idx, src, axis=0):
    return tgt.at[idx].add(src)

def _segment_sum(src, seg, n):
    return jax.ops.segment_sum(src, seg, n)
kernel_name = 'mk_sandwich_d2_jaxref_r8_995158'

def setup_inputs(seed: int=0):
    np.random.seed(seed)
    _w = jnp.asarray

    def _L0_attn_setup():
        import jax, jax.numpy as jnp
        import numpy as np
        D_MODEL = 128
        D_STATE = 16
        D_CONV = 4
        EXPAND = 2
        D_INNER = D_MODEL * EXPAND
        DT_RANK = max(1, D_MODEL // 16)
        BSZ, SEQ = (2, 256)
        LN_EPS = 1e-05

        def _silu(v):
            return v * jax.nn.sigmoid(v)

        def _selective_scan(u, delta, A, B_s, C_s, D):
            b, l, d = u.shape
            n = A.shape[1]
            h0 = jnp.zeros((b, d, n), dtype=u.dtype)
            sw = lambda a: jnp.swapaxes(a, 0, 1)

            def step(h, inp):
                dt_t, u_t, b_t, c_t = inp
                dA = jnp.exp(dt_t[..., None] * A)
                h = dA * h + dt_t[..., None] * b_t[:, None, :] * u_t[..., None]
                y = jnp.einsum('bdn,bn->bd', h, c_t)
                return (h, y)
            _, ys = jax.lax.scan(step, h0, (sw(delta), sw(u), sw(B_s), sw(C_s)))
            return jnp.swapaxes(ys, 0, 1) + u * D[None, None, :]
        key = jax.random.key(seed)
        ks = jax.random.split(key, 9)
        x = jax.random.normal(ks[0], (BSZ, SEQ, D_MODEL), dtype=jnp.float32)
        W_in = jax.random.normal(ks[1], (2 * D_INNER + 2 * D_STATE + DT_RANK, D_MODEL), dtype=jnp.float32) * 0.02
        W_dt = jax.random.normal(ks[2], (D_INNER, DT_RANK), dtype=jnp.float32) * 0.1
        b_dt = jax.random.uniform(ks[3], (D_INNER,), minval=-4.0, maxval=-1.0, dtype=jnp.float32)
        A_log = jnp.log(jnp.broadcast_to(jnp.arange(1, D_STATE + 1, dtype=jnp.float32), (D_INNER, D_STATE)))
        D = jnp.ones((D_INNER,), dtype=jnp.float32)
        conv_w = jax.random.normal(ks[4], (D_INNER, 1, D_CONV), dtype=jnp.float32) * 0.3
        conv_b = jax.random.normal(ks[5], (D_INNER,), dtype=jnp.float32) * 0.1
        W_out = jax.random.normal(ks[6], (D_MODEL, D_INNER), dtype=jnp.float32) * 0.02
        ln_g = jnp.ones((D_MODEL,), dtype=jnp.float32)
        ln_b = jnp.zeros((D_MODEL,), dtype=jnp.float32)
        return {'x': x, 'W_in': W_in, 'W_dt': W_dt, 'b_dt': b_dt, 'A_log': A_log, 'D': D, 'conv_w': conv_w, 'conv_b': conv_b, 'W_out': W_out, 'ln_g': ln_g, 'ln_b': ln_b}
    _L0_attn_in = _L0_attn_setup()

    def _L0_ffn_setup():
        import jax, jax.numpy as jnp
        import numpy as np
        D_MODEL = 128
        DEPTH = 8
        M = 2 ** DEPTH
        N_INTERNAL = M - 1
        B, T = (8, 512)

        def _leaf_probs(gate):
            BT = gate.shape[0]
            lp = jnp.ones((BT, M), dtype=gate.dtype)
            for level in range(DEPTH):
                n = 2 ** level
                half = M // (2 * n)
                g = gate[:, n - 1:2 * n - 1]
                f = jnp.stack([1.0 - g, g], axis=-1)
                f = jnp.broadcast_to(f[..., None], (BT, n, 2, half))
                lp = lp * f.reshape(BT, M)
            return lp
        key = jax.random.key(seed)
        ks = jax.random.split(key, 7)
        x = jax.random.normal(ks[0], (B, T, D_MODEL), dtype=jnp.float32)
        Wq = jax.random.normal(ks[1], (D_MODEL, D_MODEL), dtype=jnp.float32) * 0.02
        routers = jax.random.normal(ks[2], (N_INTERNAL, D_MODEL), dtype=jnp.float32) * 0.02
        leaf_keys = jax.random.normal(ks[3], (M, D_MODEL), dtype=jnp.float32) * 0.02
        leaf_values = jax.random.normal(ks[4], (M, D_MODEL), dtype=jnp.float32) * 0.02
        Wout_w = jax.random.normal(ks[5], (D_MODEL, D_MODEL), dtype=jnp.float32) * 0.02
        Wout_b = jax.random.normal(ks[6], (D_MODEL,), dtype=jnp.float32) * 0.02
        return {'x': x, 'Wq': Wq, 'routers': routers, 'leaf_keys': leaf_keys, 'leaf_values': leaf_values, 'Wout_w': Wout_w, 'Wout_b': Wout_b}
    _L0_ffn_in = _L0_ffn_setup()

    def _L1_attn_setup():
        import jax, jax.numpy as jnp
        import numpy as np
        L, D, F, H = (4, 128, 256, 8)
        DH = D // H
        EPS = 1e-05

        def _layer_norm(x, scale, bias):
            mu = x.mean(-1, keepdims=True)
            var = x.var(-1, keepdims=True)
            return (x - mu) * jax.lax.rsqrt(var + EPS) * scale + bias

        def _rotate(x, cos, sin):
            x1, x2 = (x[..., 0::2], x[..., 1::2])
            r1 = x1 * cos - x2 * sin
            r2 = x1 * sin + x2 * cos
            return jnp.stack([r1, r2], axis=-1).reshape(x.shape)

        def _decay_matrix(S):
            gammas = 1.0 - jnp.exp(jnp.linspace(np.log(1 / 32), np.log(1 / 64), H)).astype(jnp.float32)
            n = jnp.arange(S)
            diff = (n[:, None] - n[None, :]).astype(jnp.float32)
            pw = jnp.exp(jnp.clip(diff, 0.0)[None] * jnp.log(gammas)[:, None, None])
            return jnp.where(diff[None] >= 0, pw, 0.0)

        def _retention(x, Wq, Wk, Wv, Wg, Wo, gn_s, gn_b, Dm, cos, sin):
            B, S, _ = x.shape
            Q = (x @ Wq).reshape(B, S, H, DH)
            K = (x @ Wk).reshape(B, S, H, DH)
            V = (x @ Wv).reshape(B, S, H, DH)
            Q = _rotate(Q, cos, sin)
            K = _rotate(K, cos, -sin)
            att = jnp.einsum('bnhd,bmhd->bhnm', Q, K) * Dm
            Y = jnp.einsum('bhnm,bmhd->bnhd', att, V)
            mu = Y.mean(-1, keepdims=True)
            var = Y.var(-1, keepdims=True)
            Y = (Y - mu) * jax.lax.rsqrt(var + EPS)
            Y = Y.reshape(B, S, D) * gn_s + gn_b
            G = jax.nn.swish(x @ Wg)
            return G * Y @ Wo
        key = jax.random.key(seed)
        ks = jax.random.split(key, 8)
        B, S = (4, 128)
        sd = 1.0 / np.sqrt(D)
        sf = 1.0 / np.sqrt(F)
        return {'X': jax.random.normal(ks[0], (B, S, D), jnp.float32), 'Wq': jax.random.normal(ks[1], (L, D, D), jnp.float32) * sd, 'Wk': jax.random.normal(ks[2], (L, D, D), jnp.float32) * sd, 'Wv': jax.random.normal(ks[3], (L, D, D), jnp.float32) * sd, 'Wg': jax.random.normal(ks[4], (L, D, D), jnp.float32) * sd, 'Wo': jax.random.normal(ks[5], (L, D, D), jnp.float32) * sd, 'W1': jax.random.normal(ks[6], (L, D, F), jnp.float32) * sd, 'W2': jax.random.normal(ks[7], (L, F, D), jnp.float32) * sf, 'ln_scale': jnp.ones((D,), jnp.float32), 'ln_bias': jnp.zeros((D,), jnp.float32), 'gn_scale': jnp.ones((L, D), jnp.float32), 'gn_bias': jnp.zeros((L, D), jnp.float32)}
    _L1_attn_in = _L1_attn_setup()

    def _L1_ffn_setup():
        import jax, jax.numpy as jnp
        import numpy as np
        H = 128
        I = 128
        E = 8
        key = jax.random.key(seed)
        ks = jax.random.split(key, 8)
        s = 0.02
        x = jax.random.normal(ks[0], (4, 256, H), dtype=jnp.float32)
        Wg = jax.random.normal(ks[1], (H, E), dtype=jnp.float32) * s
        bg = jnp.zeros((E,), dtype=jnp.float32)
        W1 = jax.random.normal(ks[2], (E, H, I), dtype=jnp.float32) * s
        b1 = jnp.zeros((E, I), dtype=jnp.float32)
        W2 = jax.random.normal(ks[3], (E, I, H), dtype=jnp.float32) * s
        b2 = jnp.zeros((E, H), dtype=jnp.float32)
        return {'x': x, 'Wg': Wg, 'bg': bg, 'W1': W1, 'b1': b1, 'W2': W2, 'b2': b2}
    _L1_ffn_in = _L1_ffn_setup()
    _d = {'L0_attn_x': _L0_attn_in['x'], 'L0_attn_W_in': _L0_attn_in['W_in'], 'L0_attn_W_dt': _L0_attn_in['W_dt'], 'L0_attn_b_dt': _L0_attn_in['b_dt'], 'L0_attn_A_log': _L0_attn_in['A_log'], 'L0_attn_D': _L0_attn_in['D'], 'L0_attn_conv_w': _L0_attn_in['conv_w'], 'L0_attn_conv_b': _L0_attn_in['conv_b'], 'L0_attn_W_out': _L0_attn_in['W_out'], 'L0_attn_ln_g': _L0_attn_in['ln_g'], 'L0_attn_ln_b': _L0_attn_in['ln_b'], 'L0_ffn_Wq': _L0_ffn_in['Wq'], 'L0_ffn_routers': _L0_ffn_in['routers'], 'L0_ffn_leaf_keys': _L0_ffn_in['leaf_keys'], 'L0_ffn_leaf_values': _L0_ffn_in['leaf_values'], 'L0_ffn_Wout_w': _L0_ffn_in['Wout_w'], 'L0_ffn_Wout_b': _L0_ffn_in['Wout_b'], 'L1_attn_Wq': _L1_attn_in['Wq'], 'L1_attn_Wk': _L1_attn_in['Wk'], 'L1_attn_Wv': _L1_attn_in['Wv'], 'L1_attn_Wg': _L1_attn_in['Wg'], 'L1_attn_Wo': _L1_attn_in['Wo'], 'L1_attn_W1': _L1_attn_in['W1'], 'L1_attn_W2': _L1_attn_in['W2'], 'L1_attn_ln_scale': _L1_attn_in['ln_scale'], 'L1_attn_ln_bias': _L1_attn_in['ln_bias'], 'L1_attn_gn_scale': _L1_attn_in['gn_scale'], 'L1_attn_gn_bias': _L1_attn_in['gn_bias'], 'L1_ffn_Wg': _L1_ffn_in['Wg'], 'L1_ffn_bg': _L1_ffn_in['bg'], 'L1_ffn_W1': _L1_ffn_in['W1'], 'L1_ffn_b1': _L1_ffn_in['b1'], 'L1_ffn_W2': _L1_ffn_in['W2'], 'L1_ffn_b2': _L1_ffn_in['b2']}
    _x0 = _d['L0_attn_x']
    _d['L0_attn_x'] = jax.random.normal(jax.random.fold_in(jax.random.key(seed), 1), (8, 256, 128), dtype=_x0.dtype)
    del _x0
    return _d

def reference(L0_attn_x, L0_attn_W_in, L0_attn_W_dt, L0_attn_b_dt, L0_attn_A_log, L0_attn_D, L0_attn_conv_w, L0_attn_conv_b, L0_attn_W_out, L0_attn_ln_g, L0_attn_ln_b, L0_ffn_Wq, L0_ffn_routers, L0_ffn_leaf_keys, L0_ffn_leaf_values, L0_ffn_Wout_w, L0_ffn_Wout_b, L1_attn_Wq, L1_attn_Wk, L1_attn_Wv, L1_attn_Wg, L1_attn_Wo, L1_attn_W1, L1_attn_W2, L1_attn_ln_scale, L1_attn_ln_bias, L1_attn_gn_scale, L1_attn_gn_bias, L1_ffn_Wg, L1_ffn_bg, L1_ffn_W1, L1_ffn_b1, L1_ffn_W2, L1_ffn_b2):

    def _L0_attn_ref(x, W_in, W_dt, b_dt, A_log, D, conv_w, conv_b, W_out, ln_g, ln_b):
        import jax, jax.numpy as jnp
        import numpy as np
        D_MODEL = 128
        D_STATE = 16
        D_CONV = 4
        EXPAND = 2
        D_INNER = D_MODEL * EXPAND
        DT_RANK = max(1, D_MODEL // 16)
        BSZ, SEQ = (2, 256)
        LN_EPS = 1e-05

        def _silu(v):
            return v * jax.nn.sigmoid(v)

        def _selective_scan(u, delta, A, B_s, C_s, D):
            b, l, d = u.shape
            n = A.shape[1]
            h0 = jnp.zeros((b, d, n), dtype=u.dtype)
            sw = lambda a: jnp.swapaxes(a, 0, 1)

            def step(h, inp):
                dt_t, u_t, b_t, c_t = inp
                dA = jnp.exp(dt_t[..., None] * A)
                h = dA * h + dt_t[..., None] * b_t[:, None, :] * u_t[..., None]
                y = jnp.einsum('bdn,bn->bd', h, c_t)
                return (h, y)
            _, ys = jax.lax.scan(step, h0, (sw(delta), sw(u), sw(B_s), sw(C_s)))
            return jnp.swapaxes(ys, 0, 1) + u * D[None, None, :]
        residual = x
        b, l, _ = x.shape
        proj = jnp.einsum('bld,od->blo', x, W_in)
        x_s, z, B_s, C_s, dt = jnp.split(proj, [D_INNER, 2 * D_INNER, 2 * D_INNER + D_STATE, 2 * D_INNER + 2 * D_STATE], axis=-1)
        xc = jnp.transpose(x_s, (0, 2, 1))
        xc = jax.lax.conv_general_dilated(xc, conv_w, window_strides=(1,), padding=[(D_CONV - 1, D_CONV - 1)], feature_group_count=D_INNER, dimension_numbers=('NCH', 'OIH', 'NCH'))
        xc = xc[..., :l] + conv_b[None, :, None]
        x_s = _silu(jnp.transpose(xc, (0, 2, 1)))
        dt = jax.nn.softplus(jnp.einsum('blr,dr->bld', dt, W_dt) + b_dt)
        A = -jnp.exp(A_log)
        y = _selective_scan(x_s, dt, A, B_s, C_s, D)
        y = y * _silu(z)
        out = residual + jnp.einsum('bld,od->blo', y, W_out)
        mu = jnp.mean(out, axis=-1, keepdims=True)
        var = jnp.mean(jnp.square(out - mu), axis=-1, keepdims=True)
        return (out - mu) * jax.lax.rsqrt(var + LN_EPS) * ln_g + ln_b

    def _L0_ffn_ref(x, Wq, routers, leaf_keys, leaf_values, Wout_w, Wout_b):
        import jax, jax.numpy as jnp
        import numpy as np
        D_MODEL = 128
        DEPTH = 8
        M = 2 ** DEPTH
        N_INTERNAL = M - 1
        B, T = (8, 512)

        def _leaf_probs(gate):
            BT = gate.shape[0]
            lp = jnp.ones((BT, M), dtype=gate.dtype)
            for level in range(DEPTH):
                n = 2 ** level
                half = M // (2 * n)
                g = gate[:, n - 1:2 * n - 1]
                f = jnp.stack([1.0 - g, g], axis=-1)
                f = jnp.broadcast_to(f[..., None], (BT, n, 2, half))
                lp = lp * f.reshape(BT, M)
            return lp
        Bv, Tv, d = x.shape
        q = jnp.einsum('btd,ed->bte', x, Wq)
        q_flat = q.reshape(Bv * Tv, d)
        gate = jax.nn.sigmoid(q_flat @ routers.T)
        leaf_prob = _leaf_probs(gate)
        ret = (leaf_prob @ leaf_values).reshape(Bv, Tv, d)
        return jnp.einsum('btd,ed->bte', ret, Wout_w) + Wout_b

    def _L1_attn_ref(X, Wq, Wk, Wv, Wg, Wo, W1, W2, ln_scale, ln_bias, gn_scale, gn_bias):
        import jax, jax.numpy as jnp
        import numpy as np
        L, D, F, H = (4, 128, 256, 8)
        DH = D // H
        EPS = 1e-05

        def _layer_norm(x, scale, bias):
            mu = x.mean(-1, keepdims=True)
            var = x.var(-1, keepdims=True)
            return (x - mu) * jax.lax.rsqrt(var + EPS) * scale + bias

        def _rotate(x, cos, sin):
            x1, x2 = (x[..., 0::2], x[..., 1::2])
            r1 = x1 * cos - x2 * sin
            r2 = x1 * sin + x2 * cos
            return jnp.stack([r1, r2], axis=-1).reshape(x.shape)

        def _decay_matrix(S):
            gammas = 1.0 - jnp.exp(jnp.linspace(np.log(1 / 32), np.log(1 / 64), H)).astype(jnp.float32)
            n = jnp.arange(S)
            diff = (n[:, None] - n[None, :]).astype(jnp.float32)
            pw = jnp.exp(jnp.clip(diff, 0.0)[None] * jnp.log(gammas)[:, None, None])
            return jnp.where(diff[None] >= 0, pw, 0.0)

        def _retention(x, Wq, Wk, Wv, Wg, Wo, gn_s, gn_b, Dm, cos, sin):
            B, S, _ = x.shape
            Q = (x @ Wq).reshape(B, S, H, DH)
            K = (x @ Wk).reshape(B, S, H, DH)
            V = (x @ Wv).reshape(B, S, H, DH)
            Q = _rotate(Q, cos, sin)
            K = _rotate(K, cos, -sin)
            att = jnp.einsum('bnhd,bmhd->bhnm', Q, K) * Dm
            Y = jnp.einsum('bhnm,bmhd->bnhd', att, V)
            mu = Y.mean(-1, keepdims=True)
            var = Y.var(-1, keepdims=True)
            Y = (Y - mu) * jax.lax.rsqrt(var + EPS)
            Y = Y.reshape(B, S, D) * gn_s + gn_b
            G = jax.nn.swish(x @ Wg)
            return G * Y @ Wo
        B, S, _ = X.shape
        pos = jnp.arange(S, dtype=jnp.float32)
        inv_freq = 1.0 / 10000.0 ** (jnp.arange(0, DH, 2, dtype=jnp.float32) / DH)
        ang = pos[:, None] * inv_freq[None, :]
        cos = jnp.cos(ang)[None, :, None, :]
        sin = jnp.sin(ang)[None, :, None, :]
        Dm = _decay_matrix(S)
        for i in range(L):
            Yr = _retention(_layer_norm(X, ln_scale, ln_bias), Wq[i], Wk[i], Wv[i], Wg[i], Wo[i], gn_scale[i], gn_bias[i], Dm, cos, sin) + X
            X = jax.nn.gelu(_layer_norm(Yr, ln_scale, ln_bias) @ W1[i]) @ W2[i] + Yr
        return X

    def _L1_ffn_ref(x, Wg, bg, W1, b1, W2, b2):
        import jax, jax.numpy as jnp
        import numpy as np
        H = 128
        I = 128
        E = 8
        B, S, Hd = x.shape
        xf = x.reshape(-1, Hd)
        logits = xf @ Wg + bg
        gates = jax.nn.softmax(logits, axis=-1)
        idx = jnp.argmax(gates, axis=-1)
        h = jax.nn.gelu(jnp.einsum('th,ehi->tei', xf, W1) + b1, approximate=False)
        y = jnp.einsum('tei,eih->teh', h, W2) + b2
        out = jnp.take_along_axis(y, idx[:, None, None], axis=1)[:, 0, :]
        return out.reshape(B, S, Hd)
    x = L0_attn_x
    x = x + _layernorm(_L0_attn_ref(_layernorm(x, axis=-1), L0_attn_W_in, L0_attn_W_dt, L0_attn_b_dt, L0_attn_A_log, L0_attn_D, L0_attn_conv_w, L0_attn_conv_b, L0_attn_W_out, L0_attn_ln_g, L0_attn_ln_b), axis=-1)
    x = x + _layernorm(_L0_ffn_ref(_layernorm(x, axis=-1), L0_ffn_Wq, L0_ffn_routers, L0_ffn_leaf_keys, L0_ffn_leaf_values, L0_ffn_Wout_w, L0_ffn_Wout_b), axis=-1)
    x = x + _layernorm(_L1_attn_ref(_layernorm(x, axis=-1), L1_attn_Wq, L1_attn_Wk, L1_attn_Wv, L1_attn_Wg, L1_attn_Wo, L1_attn_W1, L1_attn_W2, L1_attn_ln_scale, L1_attn_ln_bias, L1_attn_gn_scale, L1_attn_gn_bias), axis=-1)
    x = x + _layernorm(_L1_ffn_ref(_layernorm(x, axis=-1), L1_ffn_Wg, L1_ffn_bg, L1_ffn_W1, L1_ffn_b1, L1_ffn_W2, L1_ffn_b2), axis=-1)
    return x

_drawn_inputs = setup_inputs


def setup_inputs(seed=0):
    import zlib

    import numpy as np

    out = dict(_drawn_inputs(seed))
    spreads = {'L0_attn_D': (1.0, 0.6),
     'L0_attn_ln_g': (1.0, 0.2),
     'L0_attn_ln_b': (0.0, 0.1),
     'L1_attn_ln_scale': (1.0, 0.2),
     'L1_attn_ln_bias': (0.0, 0.1),
     'L1_attn_gn_scale': (1.0, 0.2),
     'L1_attn_gn_bias': (0.0, 0.1),
     'L1_ffn_bg': (0.0, 0.1),
     'L1_ffn_b1': (0.0, 0.1),
     'L1_ffn_b2': (0.0, 0.1)}
    factors = {'L0_attn_W_in': 3.469,
     'L0_attn_W_dt': 8.0,
     'L0_attn_b_dt': 7.719,
     'L0_attn_A_log': 8.0,
     'L0_attn_conv_w': 4.462,
     'L0_attn_conv_b': 4.471,
     'L0_attn_W_out': 3.833,
     'L0_ffn_Wq': 7.676,
     'L0_ffn_routers': 7.657}
    for name, (base, spread) in spreads.items():
        noise = np.random.default_rng([zlib.crc32(name.encode()), seed]).standard_normal(out[name].shape)
        drawn = base * np.exp(spread * noise) if base else spread * noise
        out[name] = jnp.asarray(drawn.astype(out[name].dtype))
    for name, factor in factors.items():
        out[name] = (out[name] * factor).astype(out[name].dtype)
    return out
```

```python
from contextlib import ExitStack

import numpy as np

import concourse.bass as bass
from concourse import mybir

F32 = mybir.dt.float32
BF16 = mybir.dt.bfloat16
ALU = mybir.AluOpType
ACT = mybir.ActivationFunctionType
AX = mybir.AxisListType.X

P = 128
D = 128
B, S = 8, 256
T = B * S // P
G = 4
GT = T // G
GC = GT * P
EPS = 1e-5
NSTATE = 16
HALVES = 2
TAPS = 4
RANK = 8
DEPTH = 8
LEAVES = 1 << DEPTH
LAYERS = 4
HEADS, DH = 8, 16
SCW = 3 * P
EXPERTS = 8


def offsets(*parts):
    at, out = 0, {}
    for name, width in parts:
        out[name] = slice(at, at + width)
        at += width
    return out, at


WA, WA_W = offsets(("x", 256), ("z", 256), ("bc", 32), ("dtin", P), ("dtw", 256), ("tap", TAPS * 256),
                   ("out", 256), ("conv_b", 2), ("b_dt", 2), ("alog", 2 * NSTATE), ("dskip", 2),
                   ("ln_g", D), ("ln_b", D))
WB, WB_W = offsets(("q", D), ("routers", LEAVES), ("values", LEAVES), ("wout", D), ("bias", D))
WD, WD_W = offsets(("w1", EXPERTS * D), ("w2", EXPERTS * D), ("b1", EXPERTS), ("gate", EXPERTS),
                   ("bg", EXPERTS), ("b2", D))
WL, WL_W = offsets(("qk", 4 * P), ("vg", 2 * P), ("wo", P), ("gn", 2 * P), ("w1", 2 * P), ("w2", 2 * P))
CS, CS_W = offsets(("ident", P), ("dup", P), ("mask", SCW), ("tq", 2 * S), ("tk", 2 * S), ("rank", EXPERTS))
PER_LAYER_VECTOR = 2 * G * (3 * GT - 1) + 3 * G
PER_LAYER_POOL = 4 * G


def constants():
    c = np.zeros((P, CS_W), np.float32)
    c[:, CS["ident"]] = np.eye(P)
    k = np.arange(P)
    c[:, CS["dup"]] = (k[:, None] // 32 == k[None] // 32) & (k[:, None] % 16 == k[None] % 16)
    later = (k[None] >= k[:, None]).astype(np.float32)
    c[:, CS["mask"]] = np.concatenate([later, np.ones((P, P), np.float32), later], 1)
    pos = np.arange(S, dtype=np.float32)
    freq = (1.0 / 10000.0 ** (np.arange(0, DH, 2, dtype=np.float32) / DH)).astype(np.float32)
    ang = (pos[:, None] * freq[None]).astype(np.float64)
    decay = 1.0 - np.exp(np.linspace(np.log(1 / 32), np.log(1 / 64), HEADS)).astype(np.float32)
    decay = np.log(decay.astype(np.float32)).astype(np.float64)
    tq, tk = np.zeros((P, 2, S)), np.zeros((P, 2, S))
    for ab in range(2):
        for r in range(P):
            j, i = r // 32, r % 32
            m = i % 16 // 2
            grow = np.exp(np.arange(S) * decay[4 * ab + j])
            if i < 16:
                q = k_ = np.cos(ang[:, m])
            else:
                q = np.sin(ang[:, m]) * (-1 if i % 2 == 0 else 1)
                k_ = -q
            tq[r, ab], tk[r, ab] = q * grow, k_ / grow
    c[:, CS["tq"]] = tq.reshape(P, -1)
    c[:, CS["tk"]] = tk.reshape(P, -1)
    c[:, CS["rank"]] = np.arange(EXPERTS, 0, -1)
    return c


def selectors():
    sel = np.zeros((P, 2 * NSTATE, P), np.float32)
    for s in range(2 * NSTATE):
        for part in range(3):
            sel[s + 32 * part, s] = 1.0
    return sel.reshape(P, -1)


class Steps:

    def __init__(self, eng, sem):
        self.eng, self.sem, self.n, self.turns = eng, sem, 0, None

    def put(self, ins):
        ins.then_inc(self.sem, 1)
        self.n += 1

    def settle(self):
        self.eng.wait_ge(self.sem, self.n if self.turns is None else self.turns + self.n)

    def enter(self, turn, per):
        self.start, self.per = self.n, per
        self.turns, self.n = turn * per + self.n, 0

    def leave(self, turns):
        assert self.n == self.per, (self.n, self.per)
        self.turns, self.n = None, self.start + turns * self.per


class Counter:

    def __init__(self):
        self.n, self.turns = 0, None

    def next(self):
        self.n += 1
        return self.n if self.turns is None else self.turns + self.n

    def enter(self, turn, per):
        self.start, self.per = self.n, per
        self.turns, self.n = turn * per + self.n, 0

    def leave(self, turns):
        assert self.n == self.per, (self.n, self.per)
        self.turns, self.n = None, self.start + turns * self.per


def four_blocks(nc, x, wa, wb, wl, wd, lnc, const, sel, out):
    with ExitStack() as ctx:
        def sbuf(name, width, dtype=F32):
            return ctx.enter_context(nc.sbuf_tensor(name, [P, width], dtype))

        def sem(name):
            return ctx.enter_context(nc.semaphore(name))

        X = sbuf("X", T * D)
        Wa, Wb, Wl, Wd = sbuf("Wa", WA_W), sbuf("Wb", WB_W), sbuf("Wl", WL_W), sbuf("Wd", WD_W)
        Cs = sbuf("Cs", CS_W)
        Sel = sbuf("Sel", 2 * NSTATE * P, BF16)
        st, mv = sbuf("st", T * 6), sbuf("mv", T * 2)
        ve, rs = sbuf("ve", T), sbuf("rs", T)
        mhalf = sbuf("mhalf", 32)
        eps = sbuf("eps", GT)
        scratch = sbuf("scratch", 1 + HALVES)
        ident, dup, mask = Cs[:, CS["ident"]], Cs[:, CS["dup"]], Cs[:, CS["mask"]]
        st3, mv3 = st[:].rearrange("p (t s) -> p t s", s=6), mv[:].rearrange("p (t s) -> p t s", s=2)
        X3 = X[:].rearrange("p (t d) -> p t d", d=D)
        bank = [ctx.enter_context(nc.psum_tensor(f"bank{i}", [P, 512], F32)) for i in range(8)]

        ARENA = 37400
        arena = sbuf("arena", ARENA)
        top = [0]

        def take(width):
            top[0] += width
            assert top[0] <= ARENA, top[0]
            return arena[:, top[0] - width:top[0]]

        Xn = take(T * D)
        Xt = take(B * (S + TAPS - 1))
        Xt3 = Xt.rearrange("p (b s) -> p b s", b=B)
        U = take(HALVES * 2048).rearrange("p (h c) -> p h c", h=HALVES)
        Z = take(HALVES * 2048).rearrange("p (h c) -> p h c", h=HALVES)
        Dt = take(HALVES * 2048).rearrange("p (h c) -> p h c", h=HALVES)
        Dtu = take(HALVES * 2048).rearrange("p (h c) -> p h c", h=HALVES)
        Da = take(HALVES * 1024).rearrange("p (h c) -> p h c", h=HALVES)
        Dbu = take(HALVES * 1024).rearrange("p (h c) -> p h c", h=HALVES)
        Hs = take(HALVES * 1024).rearrange("p (h c) -> p h c", h=HALVES)
        Hc = take(HALVES * 1024).rearrange("p (h c) -> p h c", h=HALVES)
        Bc = take(1024).bitcast(BF16)
        Rest, Mid = take(GC), take(GC // 2).bitcast(BF16)
        T1 = take(T * D)
        Wk = take(TAPS * 256).rearrange("p (k c) -> p k c", k=TAPS)
        Wdt, DiagD, Aneg = take(256), take(256), take(2 * NSTATE)
        T13 = T1.rearrange("p (t d) -> p t d", d=D)
        Xn3 = Xn.rearrange("p (t d) -> p t d", d=D)

        top[0] = 0
        Bn, Bt = take(T * D), take(T * D)
        Gates = take(T * LEAVES).rearrange("p (t n) -> p t n", t=T)
        LpA = take(T * LEAVES).rearrange("p (t n) -> p t n", t=T)
        LpB = take(T * LEAVES).rearrange("p (t n) -> p t n", t=T)
        LpT = take(G * 2 * GC).rearrange("p (g h c) -> p g h c", g=G, h=2)
        Wrq, Wlv = take(LEAVES), take(2 * D)
        T2 = take(T * D)
        Bn3, T23 = Bn.rearrange("p (t d) -> p t d", d=D), T2.rearrange("p (t d) -> p t d", d=D)

        top[0] = 0
        R, Hn, Ht = take(T * D), take(T * D), take(T * D)
        Tq = take(2 * 2048).rearrange("p (a c) -> p a c", a=2)
        Tk = take(2 * 2048).rearrange("p (a c) -> p a c", a=2)
        Kr = take(2 * 2048).rearrange("p (a c) -> p a c", a=2)
        V, Th, Sg = take(T * D), take(T * D), take(T * D)
        Att = take(2 * HEADS * SCW).rearrange("p (r w) -> p r w", w=SCW)
        Yc, Ys = take(T * D), take(2 * GC)
        Gyt, Ft = take(2 * GC), take(2 * 2 * GC)
        gst = take(G * 96)
        Lnc = take(2)
        R3, Hn3 = R.rearrange("p (t d) -> p t d", d=D), Hn.rearrange("p (t d) -> p t d", d=D)

        top[0] = 0
        Dn, Dtr, T3 = take(T * D), take(T * D), take(T * D)
        Hid = take(2 * GC)
        lg, ex, oh, tmp = take(T * EXPERTS), take(T * EXPERTS), take(T * EXPERTS), take(T * EXPERTS)
        red = take(4 * T)
        Oht = take(2048)
        Dn3, T33 = Dn.rearrange("p (t d) -> p t d", d=D), T3.rearrange("p (t d) -> p t d", d=D)

        x_in = [sem(f"x_in{g}") for g in range(G)]
        wa_in, wb_in, wd_in = sem("wa_in"), sem("wb_in"), sem("wd_in")
        const_in, sel_in, lnc_in, stored = sem("const_in"), sem("sel_in"), sem("lnc_in"), sem("stored")
        qkvg_in, out_in, ffn_in = sem("qkvg_in"), sem("out_in"), sem("ffn_in")
        vec, pol, act_steps = sem("vector_steps"), sem("pool_steps"), sem("scalar_steps")
        var_ready, rstd_ready = sem("var_ready"), sem("rstd_ready")
        conv_w, dt_w, dt_wc, a_neg, d_diag = sem("conv_w"), sem("dt_w"), sem("dt_w_copied"), sem("a_neg"), sem("d_diag")
        pads = sem("pads")
        a_normed, a_turned, a_rows = sem("a_normed"), sem("a_turned"), sem("a_rows")
        conv_done, z_done, bc_done, dt_done = sem("conv_done"), sem("z_done"), sem("bc_done"), sem("dt_done")
        u_ready, z_ready, bc_hi, bc_rest, bc_mid, bc_lo, bc_ready = (
            sem("u_ready"), sem("z_ready"), sem("bc_hi"), sem("bc_rest"), sem("bc_mid"), sem("bc_lo"), sem("bc_ready"))
        dtx_ready, exp_ready, ln_ready, log_rest, dt_ready, dtu_ready = (
            sem("dtx_ready"), sem("exp_ready"), sem("ln_ready"), sem("log_rest"), sem("dt_ready"), sem("dtu_ready"))
        b_rows, c_rows, b_used = sem("b_rows"), sem("c_rows"), sem("b_used")
        da_ready, scanned, hc_ready, hc_used = sem("da_ready"), sem("scanned"), sem("hc_ready"), sem("hc_used")
        y_gated, y_proj, t1_ready = sem("y_gated"), sem("y_proj"), sem("t1_ready")
        g_normed, g_scaled, o_normed, xa_ready = sem("g_normed"), sem("g_scaled"), sem("o_normed"), sem("xa_ready")
        tree_w, tree_wc = sem("tree_w"), sem("tree_w_copied")
        b_normed, b_turned, b_rows_t, logits, gated, leaves = (
            sem("b_normed"), sem("b_turned"), sem("b_rows_turned"), sem("logits"), sem("gated"), sem("leaves"))
        lp_turned, lp_rows, b_proj, t2_ready, t2_normed, xb_ready = (
            sem("lp_turned"), sem("lp_rows"), sem("b_proj"), sem("t2_ready"), sem("t2_normed"), sem("xb_ready"))
        c_normed, c_turned, c_rows_t, proj, rotated, vg, v_ready, th_ready, sg_ready = (
            sem("c_normed"), sem("c_turned"), sem("c_rows_turned"), sem("proj"), sem("rotated"), sem("vg"),
            sem("v_ready"), sem("th_ready"), sem("sg_ready"))
        kdup, k_ready, scores, masked, heads_out, centred, squared, y_unit, gy_ready = (
            sem("kdup"), sem("k_ready"), sem("scores"), sem("masked"), sem("heads_out"), sem("centred"),
            sem("squared"), sem("y_unit"), sem("gy_ready"))
        gy_turned, gy_rows, wo_done, r_mid, f_normed, f_turned, f_rows = (
            sem("gy_turned"), sem("gy_rows"), sem("wo_done"), sem("r_mid"), sem("f_normed"), sem("f_turned"),
            sem("f_rows"))
        w1_done, gelu_ready, w2_done, r_new, r_normed, xc_ready = (
            sem("w1_done"), sem("gelu_ready"), sem("w2_done"), sem("r_new"), sem("r_normed"),
            sem("xc_ready"))
        d_normed, d_turned, d_rows, gate_done, shifted, exps, chosen, oh_turned, oh_rows = (
            sem("d_normed"), sem("d_turned"), sem("d_rows"), sem("gate_done"), sem("shifted"), sem("exps"),
            sem("chosen"), sem("oh_turned"), sem("oh_rows"))
        hidden, h_ready, expert_out, mixed, t3_normed, xd_ready = (
            sem("hidden"), sem("h_ready"), sem("expert_out"), sem("mixed"), sem("t3_normed"), sem("xd_ready"))

        def group(g):
            return slice(g * GC, (g + 1) * GC)

        def tile(t):
            return slice(t * P, (t + 1) * P)

        block = ctx.enter_context(nc.Block())

        @block.sync
        def _(sync):
            x_tiles = x.rearrange("b (h p) d -> p (b h) d", p=P)
            for g in range(G):
                sync.dma_start(X3[:, g * GT:(g + 1) * GT, :], x_tiles[:, g * GT:(g + 1) * GT, :]).then_inc(x_in[g], 16)
                if g == 0:
                    sync.dma_start(Cs[:], const).then_inc(const_in, 16)
                    sync.dma_start(Wa[:], wa).then_inc(wa_in, 16)
            sync.dma_start(Sel[:], sel).then_inc(sel_in, 16)
            sync.dma_start(Wb[:], wb).then_inc(wb_in, 16)
            sync.dma_start(Wd[:], wd).then_inc(wd_in, 16)
            parts = ((slice(WL["qk"].start, WL["vg"].stop), qkvg_in), (slice(WL["wo"].start, WL["gn"].stop), out_in),
                     (slice(WL["w1"].start, WL["w2"].stop), ffn_in))
            for cols, landed in parts:
                sync.dma_start(Wl[:, cols], wl[0, :, cols]).then_inc(landed, 16)
            sync.wait_ge(xb_ready, G)
            sync.dma_start(Lnc, lnc).then_inc(lnc_in, 16)
            with sync.Fori(0, LAYERS - 1) as layer:
                nxt = wl[bass.ds(layer + 1, 1)].rearrange("a p c -> (a p) c")
                sync.wait_ge(vg, layer * G * 2 + 2 * G)
                sync.dma_start(Wl[:, parts[0][0]], nxt[:, parts[0][0]]).then_inc(qkvg_in, 16)
                sync.wait_ge(wo_done, layer * G + G)
                sync.wait_ge(gy_ready, layer * G + G)
                sync.dma_start(Wl[:, parts[1][0]], nxt[:, parts[1][0]]).then_inc(out_in, 16)
                sync.wait_ge(w2_done, layer * G + G)
                sync.dma_start(Wl[:, parts[2][0]], nxt[:, parts[2][0]]).then_inc(ffn_in, 16)
            out_tiles = out.rearrange("b (h p) d -> p (b h) d", p=P)
            for g in range(G):
                sync.wait_ge(xd_ready, g + 1)
                sync.dma_start(out_tiles[:, g * GT:(g + 1) * GT, :], X3[:, g * GT:(g + 1) * GT, :]).then_inc(stored, 16)
            sync.wait_ge(stored, 16 * G)

        @block.gpsimd
        def _(pool):
            own = Steps(pool, pol)
            norms = Counter()

            def rstd(g):
                pool.wait_ge(var_ready, norms.next())
                own.put(pool.tensor_tensor(ve[:, g * GT:(g + 1) * GT], mv3[:, g * GT:(g + 1) * GT, 1], eps[:, 0:GT], ALU.add))
                own.settle()
                pool.tensor_tensor(rs[:, g * GT:(g + 1) * GT], ve[:, g * GT:(g + 1) * GT], mhalf[:, 0:GT],
                                   ALU.pow).then_inc(rstd_ready, 1)

            own.put(pool.memset(mhalf[:], -0.5))
            own.put(pool.memset(eps[:], EPS))
            pool.memset(Xt3[:, :, 0:TAPS - 1], 0.0).then_inc(pads, 1)
            for h in range(HALVES):
                pool.memset(Da[:, h].rearrange("p (b s) -> p b s", s=S)[:, :, 0:1], 0.0).then_inc(scanned, 1)
            pool.memset(Bc[:, :], 0.0).then_inc(pads, 1)
            own.settle()
            pool.wait_ge(wa_in, 16)
            for k in range(TAPS):
                last = pool.tensor_tensor(Wk[:, k, :], Wa[:, WA["x"]],
                                          Wa[:, WA["tap"]].rearrange("p (k c) -> p k c", k=TAPS)[:, k, :], ALU.mult)
                if k < TAPS - 1:
                    own.put(last)
            last.then_inc(conv_w, 1)
            pool.wait_ge(const_in, 16)
            for h in range(HALVES):
                pool.tensor_scalar(DiagD[:, tile(h)], ident, Wa[:, WA["dskip"]][:, h:h + 1], None,
                                   ALU.mult).then_inc(d_diag, 1)
            for g in range(G):
                rstd(g)
            for half in range(4):
                q, h = divmod(half, HALVES)
                pool.wait_ge(exp_ready, half + 1)
                if q:
                    pool.wait_ge(hc_used, 2 + 2 * NSTATE)
                own.put(pool.tensor_scalar(Hc[:, h], Dbu[:, h], 1.0, -1.0, ALU.add, ALU.add))
                own.settle()
                pool.tensor_tensor(Hc[:, h], Dbu[:, h], Hc[:, h], ALU.subtract).then_inc(log_rest, 1)
                if h == 1:
                    for g in (2 * q, 2 * q + 1):
                        rstd(g)
                        pool.wait_ge(g_normed, g + 1)
                        t = T13[:, g * GT:(g + 1) * GT, :]
                        for col, op in (("ln_g", ALU.mult), ("ln_b", ALU.add)):
                            row = Wa[:, WA[col]].unsqueeze(1).broadcast_to((P, GT, D))
                            ins = pool.tensor_tensor(t, t, row, op)
                            if op == ALU.mult:
                                own.put(ins)
                                own.settle()
                        ins.then_inc(g_scaled, 1)
                        rstd(g)
                        pool.wait_ge(o_normed, g + 1)
                        xg = X3[:, g * GT:(g + 1) * GT, :]
                        pool.tensor_tensor(xg, xg, t, ALU.add).then_inc(xa_ready, 1)

            for g in range(G):
                rstd(g)
            for g in range(G):
                rstd(g)
                pool.wait_ge(t2_normed, g + 1)
                xg = X3[:, g * GT:(g + 1) * GT, :]
                pool.tensor_tensor(xg, xg, T23[:, g * GT:(g + 1) * GT, :], ALU.add).then_inc(xb_ready, 1)

            for g in range(G):
                rstd(g)
            pool.wait_ge(lnc_in, 16)
            with pool.Fori(0, LAYERS) as layer:
                own.enter(layer, PER_LAYER_POOL)
                norms.enter(layer, 3 * G)
                for g in range(G):
                    rstd(g)
                for g in range(G):
                    cols = slice(g * 96 + 64, g * 96 + 96)
                    pool.wait_ge(var_ready, norms.next())
                    pool.tensor_tensor(gst[:, cols], gst[:, cols], mhalf[:], ALU.pow).then_inc(rstd_ready, 1)
                    pool.wait_ge(y_unit, layer * G + g + 1)
                    if g == 0:
                        pool.wait_ge(out_in, layer * 16 + 16)
                    y = Yc[:, group(g)].rearrange("p (t d) -> p t d", d=D)
                    gn = Wl[:, WL["gn"]].rearrange("p (a d) -> p a d", a=2)
                    own.put(pool.tensor_tensor(y, y, gn[:, 0:1, :].broadcast_to((P, GT, D)), ALU.mult))
                    own.settle()
                    own.put(pool.tensor_tensor(y, y, gn[:, 1:2, :].broadcast_to((P, GT, D)), ALU.add))
                    own.settle()
                    pool.wait_ge(sg_ready, layer * 2 * G + 2 * g + 2)
                    pool.tensor_tensor(Yc[:, group(g)], Yc[:, group(g)], Sg[:, group(g)], ALU.mult).then_inc(gy_ready, 1)
                for g in range(G):
                    rstd(g)
                own.leave(LAYERS)
                norms.leave(LAYERS)
            for g in range(G):
                rstd(g)
                pool.wait_ge(r_normed, g + 1)
                xg = X3[:, g * GT:(g + 1) * GT, :]
                pool.tensor_tensor(xg, xg, Hn3[:, g * GT:(g + 1) * GT, :], ALU.add).then_inc(xc_ready, 1)

            for g in range(G):
                rstd(g)
            for g in range(G):
                rstd(g)
                pool.wait_ge(t3_normed, g + 1)
                xg = X3[:, g * GT:(g + 1) * GT, :]
                pool.tensor_tensor(xg, xg, T33[:, g * GT:(g + 1) * GT, :], ALU.add).then_inc(xd_ready, 1)

        @block.scalar
        def _(act):
            own = Steps(act, act_steps)
            act.wait_ge(wa_in, 16)
            own.put(act.activation(Aneg, Wa[:, WA["alog"]], ACT.Exp))
            own.settle()
            act.mul(Aneg, Aneg, -1.0).then_inc(a_neg, 1)

            act.wait_ge(pads, 2)
            for g in range(G):
                act.wait_ge(a_turned, g + 1)
                act.copy(Xt3[:, 2 * g:2 * g + 2, TAPS - 1:], bank[g % 2][:].rearrange("p (b s) -> p b s", b=2)).then_inc(a_rows, 1)
                for h in range(HALVES):
                    act.wait_ge(conv_done, 2 * g + h + 1)
                    act.activation(U[:, h, group(g)], bank[2 + h][:], ACT.Silu,
                                   bias=Wa[:, WA["conv_b"]][:, h:h + 1]).then_inc(u_ready, 1)
                for h in range(HALVES):
                    act.wait_ge(z_done, 2 * g + h + 1)
                    act.activation(Z[:, h, group(g)], bank[4 + h][:], ACT.Silu).then_inc(z_ready, 1)
                act.wait_ge(bc_done, g + 1)
                act.copy(Bc[0:32, group(g)], bank[g % 2][0:32, :]).then_inc(bc_hi, 1)
                act.wait_ge(bc_rest, g + 1)
                act.copy(Mid[0:32, :], Rest[0:32, :]).then_inc(bc_mid, 1)
                act.wait_ge(bc_mid, g + 1)
                act.copy(Bc[32:64, group(g)], Mid[0:32, :]).then_inc(bc_ready, 1)

            act.preload_act_table_set("natural_log_exp_and_others")
            for q in range(2):
                cols = slice(q * 1024, (q + 1) * 1024)
                for h in range(HALVES):
                    act.wait_ge(dtx_ready, 4 * q + 2 + h + 1)
                    if q:
                        act.wait_ge(scanned, 2 + 2 * NSTATE)
                        act.wait_ge(hc_ready, 2 + 2 * NSTATE)
                    own.put(act.activation(Hs[:, h], Dt[:, h, cols], ACT.Abs))
                    own.settle()
                    act.activation(Dbu[:, h], Hs[:, h], ACT.Exp, scale=-1.0).then_inc(exp_ready, 1)
                    act.wait_ge(exp_ready, 2 * q + h + 1)
                    act.activation(Hs[:, h], Dbu[:, h], ACT.Ln, bias=1.0).then_inc(ln_ready, 1)
                act.wait_ge(dtu_ready, 2 * q + 2)
                with act.Fori(0, NSTATE) as n:
                    for h in range(HALVES):
                        act.wait_ge(scanned, n * 2 + (2 * NSTATE * q + 2))
                        seq = "p (b s) -> p b s"
                        act.activation(Da[:, h].rearrange(seq, s=S)[:, :, 1:], Dt[:, h, cols].rearrange(seq, s=S)[:, :, 1:],
                                       ACT.Exp, scale=Aneg[:, bass.ds(n + h * NSTATE, 1)]).then_inc(da_ready, 1)

            for g in range(G):
                act.wait_ge(b_turned, g + 1)
                act.copy(Bt[:, group(g)], bank[g % 2][:]).then_inc(b_rows_t, 1)
            for t in range(T // 2):
                act.wait_ge(logits, t + 1)
                act.activation(Gates[:, 2 * t:2 * t + 2, :], bank[2 + t % 2][:], ACT.Sigmoid).then_inc(gated, 1)
            for g in range(G):
                for h in range(2):
                    act.wait_ge(lp_turned, 2 * g + h + 1)
                    act.copy(LpT[:, g, h, :], bank[4 + h][:]).then_inc(lp_rows, 1)

            act.wait_ge(lnc_in, 16)
            act.preload_act_table(ACT.Gelu_apprx_tanh)
            with act.Fori(0, LAYERS) as layer:
                for g in range(G):
                    act.wait_ge(c_turned, layer * G + g + 1)
                    act.activation(Ht[:, group(g)], bank[g % 2][:], ACT.Identity, bias=Lnc[:, 1:2],
                                   scale=Lnc[:, 0:1]).then_inc(c_rows_t, 1)
                for g in range(G + 1):
                    if g < G:
                        for k in range(2):
                            act.wait_ge(vg, layer * 2 * G + 2 * g + k + 1)
                            vgt = bank[6 + k][:].rearrange("p (t c) -> p t c", t=2)
                            tiles = slice(GT * g + 2 * k, GT * g + 2 * k + 2)
                            act.copy(V.rearrange("p (t d) -> p t d", d=D)[:, tiles, :], vgt[:, :, 0:D]).then_inc(v_ready, 1)
                            act.activation(Th.rearrange("p (t d) -> p t d", d=D)[:, tiles, :], vgt[:, :, D:],
                                           ACT.Tanh, scale=0.5).then_inc(th_ready, 1)
                    if g >= 1:
                        for k in range(2):
                            act.wait_ge(kdup, layer * 2 * G + 2 * (g - 1) + k + 1)
                            act.copy(Kr[:, k, group(g - 1)], bank[k][:]).then_inc(k_ready, 1)
                for g in range(G):
                    act.wait_ge(centred, layer * G + g + 1)
                    act.square(Ys[:, group(g % 2)], Yc[:, group(g)]).then_inc(squared, 1)
                for g in range(G):
                    act.wait_ge(gy_turned, layer * G + g + 1)
                    if g >= 2:
                        act.wait_ge(wo_done, layer * G + g - 1)
                    act.mul(Gyt[:, group(g % 2)], bank[g % 2][:], 0.5).then_inc(gy_rows, 1)
                for g in range(G):
                    act.wait_ge(f_turned, layer * G + g + 1)
                    act.activation(Ht[:, group(g)], bank[g % 2][:], ACT.Identity, bias=Lnc[:, 1:2],
                                   scale=Lnc[:, 0:1]).then_inc(f_rows, 1)
                    for k in range(2):
                        act.wait_ge(w1_done, layer * 2 * G + 2 * g + k + 1)
                        if g >= 2:
                            act.wait_ge(w2_done, layer * G + g - 1)
                        act.activation(Ft[:, group(2 * (g % 2) + k)], bank[4 + k][:],
                                       ACT.Gelu_apprx_tanh).then_inc(gelu_ready, 1)

            for g in range(G):
                act.wait_ge(d_turned, g + 1)
                act.copy(Dtr[:, group(g)], bank[g % 2][:]).then_inc(d_rows, 1)
            act.wait_ge(shifted, 1)
            act.activation(ex, lg, ACT.Exp).then_inc(exps, 1)
            for g in range(G):
                act.wait_ge(oh_turned, g + 1)
                act.copy(Oht[0:EXPERTS, group(g)], bank[g % 2][0:EXPERTS, :]).then_inc(oh_rows, 1)
            for g in range(G):
                for e in range(EXPERTS):
                    i = g * EXPERTS + e
                    act.wait_ge(hidden, i + 1)
                    if i >= 2:
                        act.wait_ge(expert_out, (i - 2) // EXPERTS * (EXPERTS + 1) + (i - 2) % EXPERTS + 2)
                    act.activation(Hid[:, group(i % 2)], bank[2 + i % 2][:], ACT.Gelu,
                                   bias=Wd[:, WD["b1"]][:, e:e + 1]).then_inc(h_ready, 1)

        @block.vector
        def _(dve):
            own = Steps(dve, vec)
            norms = Counter()

            def stats(src3, g, waits=()):
                tiles = range(g * GT, (g + 1) * GT)
                for t in tiles:
                    own.put(dve.bn_stats(st3[:, t, :], src3[:, t, :]))
                own.settle()
                own.put(dve.memset(scratch[:, 0:1], 0.0))
                for t in tiles:
                    ins = dve.bn_aggr(mv3[:, t, :], st3[:, t, :])
                    if t < tiles[-1]:
                        own.put(ins)
                ins.then_inc(var_ready, 1)

            def normalise(dst3, src3, g, done):
                dve.wait_ge(rstd_ready, norms.next())
                tiles = range(g * GT, (g + 1) * GT)
                for t in tiles:
                    ins = dve.tensor_scalar(dst3[:, t, :], src3[:, t, :], mv3[:, t, 0:1], rs[:, t:t + 1], ALU.subtract, ALU.mult)
                    if t < tiles[-1]:
                        own.put(ins)
                ins.then_inc(done, 1)

            dve.wait_ge(wa_in, 16)
            dve.wait_ge(const_in, 16)
            dve.wait_ge(dt_w, 1)
            dve.tensor_copy(Wdt, bank[7][:, 0:256]).then_inc(dt_wc, 1)
            for g in range(G + 1):
                if g < G:
                    dve.wait_ge(x_in[g], 16)
                    stats(X3, g)
                if g >= 1:
                    normalise(Xn3, X3, g - 1, a_normed)
            for g in range(G):
                dve.wait_ge(bc_hi, g + 1)
                if g:
                    dve.wait_ge(bc_lo, g)
                dve.tensor_tensor(Rest[0:32, :], bank[g % 2][0:32, :], Bc[0:32, group(g)], ALU.subtract).then_inc(bc_rest, 1)
                dve.wait_ge(bc_mid, g + 1)
                dve.tensor_tensor(Bc[64:96, group(g)], Rest[0:32, :], Mid[0:32, :], ALU.subtract).then_inc(bc_lo, 1)
                for h in range(HALVES):
                    dve.wait_ge(dt_done, 2 * g + h + 1)
                    dve.tensor_scalar(Dt[:, h, group(g)], bank[6 + h][:], Wa[:, WA["b_dt"]][:, h:h + 1], None,
                                      ALU.add).then_inc(dtx_ready, 1)

            for h in range(HALVES):
                dve.memset(scratch[:, 1 + h:2 + h], 0.0).then_inc(hc_ready, 1)
            for q in range(2):
                cols = slice(q * 1024, (q + 1) * 1024)
                for h in range(HALVES):
                    dve.wait_ge(ln_ready, 2 * q + h + 1)
                    dve.wait_ge(dtx_ready, 8)
                    own.put(dve.scalar_tensor_tensor(Dt[:, h, cols], Dt[:, h, cols], 0.0, Hs[:, h], ALU.max, ALU.add))
                    dve.wait_ge(log_rest, 2 * q + h + 1)
                    own.settle()
                    dve.tensor_tensor(Dt[:, h, cols], Dt[:, h, cols], Hc[:, h], ALU.add).then_inc(dt_ready, 1)
                    dve.wait_ge(dt_ready, 2 * q + h + 1)
                    dve.wait_ge(u_ready, 8)
                    dve.tensor_tensor(Dtu[:, h, cols], Dt[:, h, cols], U[:, h, cols], ALU.mult).then_inc(dtu_ready, 1)
                dve.wait_ge(dtu_ready, 2 * q + 2)
                with dve.Fori(0, NSTATE) as n:
                    own.enter(n, 4)
                    base = q * 2 * NSTATE
                    dve.wait_ge(hc_ready, n * 2 + (base + 2))
                    dve.wait_ge(b_rows, n + (q * NSTATE + 1))
                    for h in range(HALVES):
                        for c in range(2):
                            ins = dve.tensor_tensor(Dbu[:, h, group(c)], Dtu[:, h, slice(q * 1024 + c * GC, q * 1024 + (c + 1) * GC)],
                                                    bank[4 + c][:], ALU.mult)
                            if c == 0:
                                own.put(ins)
                        ins.then_inc(b_used, 1)
                    for h in range(HALVES):
                        dve.wait_ge(b_used, n * 2 + (base + h + 1))
                        dve.wait_ge(da_ready, n * 2 + (base + h + 1))
                        dve.tensor_tensor_scan(Hs[:, h], Da[:, h], Dbu[:, h], 0.0, ALU.mult, ALU.add).then_inc(scanned, 1)
                    dve.wait_ge(c_rows, n + (q * NSTATE + 1))
                    for h in range(HALVES):
                        dve.wait_ge(scanned, n * 2 + (base + h + 3))
                        if h == 0:
                            dve.wait_ge(hc_used, n * 2 + (2 + q * (2 * NSTATE + 2)))
                        for c in range(2):
                            ins = dve.tensor_tensor(Hc[:, h, group(c)], Hs[:, h, group(c)], bank[6 + c][:], ALU.mult)
                            if c == 0:
                                own.put(ins)
                        ins.then_inc(hc_ready, 1)
                    own.leave(NSTATE)
                dve.wait_ge(hc_used, (q + 1) * (2 * NSTATE + 2))
                dve.wait_ge(z_ready, 8)
                for h in range(HALVES):
                    for c in range(2):
                        zz = Z[:, h, slice(q * 1024 + c * GC, q * 1024 + (c + 1) * GC)]
                        dve.tensor_tensor(zz, bank[2 * h + c][:], zz, ALU.mult).then_inc(y_gated, 1)
                for c in range(2):
                    g = 2 * q + c
                    dve.wait_ge(y_proj, g + 1)
                    dve.tensor_tensor(T1[:, group(g)], bank[4 + c][:], Xn[:, group(g)], ALU.add).then_inc(t1_ready, 1)
                    dve.wait_ge(t1_ready, g + 1)
                    stats(T13, g)
                    normalise(T13, T13, g, g_normed)
                    dve.wait_ge(g_scaled, g + 1)
                    stats(T13, g)
                    normalise(T13, T13, g, o_normed)

            dve.wait_ge(tree_w, 1)
            own.put(dve.tensor_copy(Wrq, bank[7][:, 0:256]))
            dve.tensor_copy(Wlv, bank[7][:, 256:512]).then_inc(tree_wc, 1)
            for g in range(G + 1):
                if g < G:
                    dve.wait_ge(xa_ready, g + 1)
                    stats(X3, g)
                if g >= 1:
                    normalise(Bn3, X3, g - 1, b_normed)
            for g in range(G):
                tiles = slice(g * GT, (g + 1) * GT)
                dve.wait_ge(gated, 2 * g + 2)
                first = Gates[:, tiles, 0:1]
                own.put(dve.tensor_scalar(LpA[:, tiles, 0:1], first, -1.0, 1.0, ALU.mult, ALU.add))
                own.put(dve.tensor_copy(LpA[:, tiles, 1:2], first))
                own.settle()
                now, then = LpA, LpB
                for level in range(1, DEPTH):
                    n = 1 << level
                    right, left = then[:, tiles, 1:2 * n:2], then[:, tiles, 0:2 * n:2]
                    own.put(dve.tensor_tensor(right, now[:, tiles, 0:n], Gates[:, tiles, n - 1:2 * n - 1], ALU.mult))
                    own.settle()
                    ins = dve.tensor_tensor(left, now[:, tiles, 0:n], right, ALU.subtract)
                    if level < DEPTH - 1:
                        own.put(ins)
                        own.settle()
                    now, then = then, now
                ins.then_inc(leaves, 1)
            for g in range(G):
                dve.wait_ge(b_proj, g + 1)
                bias = Wb[:, WB["bias"]].unsqueeze(1).broadcast_to((P, GT, D))
                dve.tensor_tensor(T23[:, g * GT:(g + 1) * GT, :], bank[6 + g % 2][:].rearrange("p (t d) -> p t d", d=D),
                                  bias, ALU.add).then_inc(t2_ready, 1)
                dve.wait_ge(t2_ready, g + 1)
                stats(T23, g)
                if g >= 1:
                    normalise(T23, T23, g - 1, t2_normed)
            normalise(T23, T23, G - 1, t2_normed)

            for g in range(G + 1):
                if g < G:
                    dve.wait_ge(xb_ready, g + 1)
                    stats(X3, g)
                if g >= 1:
                    normalise(R3, X3, g - 1, r_new)
            dve.wait_ge(r_new, G)
            with dve.Fori(0, LAYERS) as layer:
                own.enter(layer, PER_LAYER_VECTOR)
                norms.enter(layer, 3 * G)
                for g in range(G + 1):
                    if g < G:
                        dve.wait_ge(r_new, layer * G + G)
                        stats(R3, g)
                    if g >= 1:
                        normalise(Hn3, R3, g - 1, c_normed)
                for g in range(G + 1):
                    if g < G:
                        for k in range(4):
                            dve.wait_ge(proj, layer * 4 * G + 4 * g + k + 1)
                            dst = (Tq, Tk)[k // 2][:, k % 2, group(g)].rearrange("p (b s) -> p b s", b=2)
                            table = Cs[:, CS[("tq", "tk")[k // 2]]].rearrange("p (a s) -> p a s", a=2)
                            dve.tensor_tensor(dst, bank[2 + k][:].rearrange("p (b s) -> p b s", b=2),
                                              table[:, k % 2:k % 2 + 1, :].broadcast_to((P, 2, S)), ALU.mult).then_inc(rotated, 1)
                        for k in range(2):
                            dve.wait_ge(th_ready, layer * 2 * G + 2 * g + k + 1)
                            tiles = slice(GT * g + 2 * k, GT * g + 2 * k + 2)
                            as3 = "p (t d) -> p t d"
                            dve.scalar_tensor_tensor(Sg.rearrange(as3, d=D)[:, tiles, :], Th.rearrange(as3, d=D)[:, tiles, :],
                                                     1.0, bank[6 + k][:].rearrange("p (t c) -> p t c", t=2)[:, :, D:],
                                                     ALU.add, ALU.mult).then_inc(sg_ready, 1)
                for b in range(B + 2):
                    if b < B:
                        for h in range(HEADS):
                            i = b * HEADS + h
                            dve.wait_ge(scores, layer * B * HEADS + i + 1)
                            if h == 0 and b >= 2:
                                dve.wait_ge(heads_out, layer * B + b - 1)
                            dve.tensor_tensor(Att[:, (b % 2) * HEADS + h, :], bank[2 + i % 4][:, 0:SCW], mask,
                                              ALU.mult).then_inc(masked, 1)
                    if b % 2 == 0 and b >= 2:
                        g = b // 2 - 1
                        as3 = "p (m i) -> p m i"
                        sums, var = gst[:, g * 96:g * 96 + 32], gst[:, g * 96 + 64:g * 96 + 96]
                        mean = gst[:, g * 96 + 32:g * 96 + 64]
                        dve.wait_ge(heads_out, layer * B + 2 * g + 2)
                        own.put(dve.tensor_reduce(sums, bank[6 + g % 2][:].rearrange(as3, i=DH), AX, ALU.add))
                        own.settle()
                        own.put(dve.tensor_scalar(mean, sums, 1.0 / DH, None, ALU.mult))
                        own.settle()
                        dve.tensor_tensor(Yc[:, group(g)].rearrange(as3, i=DH), bank[6 + g % 2][:].rearrange(as3, i=DH),
                                          mean.unsqueeze(2).broadcast_to((P, 32, DH)), ALU.subtract).then_inc(centred, 1)
                        dve.wait_ge(squared, layer * G + g + 1)
                        own.put(dve.tensor_reduce(var, Ys[:, group(g % 2)].rearrange(as3, i=DH), AX, ALU.add))
                        own.settle()
                        dve.tensor_scalar(var, var, 1.0 / DH, EPS, ALU.mult, ALU.add).then_inc(var_ready, 1)
                for g in range(G):
                    as3 = "p (m i) -> p m i"
                    dve.wait_ge(rstd_ready, norms.next())
                    y = Yc[:, group(g)].rearrange(as3, i=DH)
                    dve.tensor_tensor(y, y, gst[:, g * 96 + 64:g * 96 + 96].unsqueeze(2).broadcast_to((P, 32, DH)),
                                      ALU.mult).then_inc(y_unit, 1)
                for g in range(G + 1):
                    if g < G:
                        dve.wait_ge(wo_done, layer * G + g + 1)
                        dve.tensor_tensor(R[:, group(g)], bank[2 + g % 2][:], R[:, group(g)], ALU.add).then_inc(r_mid, 1)
                        dve.wait_ge(r_mid, layer * G + g + 1)
                        stats(R3, g)
                    if g >= 1:
                        normalise(Hn3, R3, g - 1, f_normed)
                for g in range(G):
                    dve.wait_ge(w2_done, layer * G + g + 1)
                    dve.tensor_tensor(R[:, group(g)], bank[6 + g % 2][:], R[:, group(g)], ALU.add).then_inc(r_new, 1)
                own.leave(LAYERS)
                norms.leave(LAYERS)
            for g in range(G):
                dve.wait_ge(r_new, G + LAYERS * G)
                stats(R3, g)
                if g >= 1:
                    normalise(Hn3, R3, g - 1, r_normed)
            normalise(Hn3, R3, G - 1, r_normed)

            dve.wait_ge(wd_in, 16)
            for g in range(G + 1):
                if g < G:
                    dve.wait_ge(xc_ready, g + 1)
                    stats(X3, g)
                if g >= 1:
                    normalise(Dn3, X3, g - 1, d_normed)
            by_expert = "p (t e) -> p t e"
            dve.wait_ge(gate_done, 1)
            lg3, ex3, oh3, tmp3 = (v.rearrange(by_expert, e=EXPERTS) for v in (lg, ex, oh, tmp))
            most, total, best, first = (red[:, i * T:(i + 1) * T] for i in range(4))

            def step(ins):
                own.put(ins)
                own.settle()

            def spread(v):
                return v.unsqueeze(2).broadcast_to((P, T, EXPERTS))

            step(dve.tensor_tensor(lg3, bank[2][:, 0:T * EXPERTS].rearrange(by_expert, e=EXPERTS),
                                   Wd[:, WD["bg"]].unsqueeze(1).broadcast_to((P, T, EXPERTS)), ALU.add))
            step(dve.tensor_reduce(most, lg3, AX, ALU.max))
            dve.tensor_tensor(lg3, lg3, spread(most), ALU.subtract).then_inc(shifted, 1)
            dve.wait_ge(exps, 1)
            step(dve.tensor_reduce(total, ex3, AX, ALU.add))
            step(dve.reciprocal(total, total))
            step(dve.tensor_tensor(ex3, ex3, spread(total), ALU.mult))
            step(dve.tensor_reduce(best, ex3, AX, ALU.max))
            step(dve.tensor_tensor(oh3, ex3, spread(best), ALU.is_equal))
            step(dve.tensor_tensor(tmp3, oh3, Cs[:, CS["rank"]].unsqueeze(1).broadcast_to((P, T, EXPERTS)), ALU.mult))
            step(dve.tensor_reduce(first, tmp3, AX, ALU.max))
            dve.tensor_tensor(oh3, tmp3, spread(first), ALU.is_equal).then_inc(chosen, 1)
            dve.wait_ge(chosen, 1)
            for g in range(G + 1):
                if g < G:
                    for e in range(EXPERTS + 1):
                        i = g * (EXPERTS + 1) + e
                        dve.wait_ge(expert_out, i + 1)
                        if e == 0:
                            dve.tensor_copy(T3[:, group(g)], bank[4 + i % 2][:]).then_inc(mixed, 1)
                            continue
                        dve.wait_ge(mixed, i)
                        for k in range(GT):
                            t = g * GT + k
                            ins = dve.scalar_tensor_tensor(T33[:, t, :], bank[4 + i % 2][:, tile(k)], oh3[:, t, e - 1:e],
                                                           T33[:, t, :], ALU.mult, ALU.add)
                            if k < GT - 1:
                                own.put(ins)
                        ins.then_inc(mixed, 1)
                    dve.wait_ge(mixed, (g + 1) * (EXPERTS + 1))
                    stats(T33, g)
                if g >= 1:
                    normalise(T33, T33, g - 1, t3_normed)

        @block.tensor
        def _(pe):
            def turn(dst, src3, g, width=P):
                for k in range(GT):
                    ins = pe.transpose(dst[0:width, tile(k)], src3[:, g * GT + k, :], ident)
                return ins

            def tokens(dst, rows, weights, rows_of=lambda k: tile(k), width=D):
                for k in range(GT):
                    for i, (r, w) in enumerate(zip(rows, weights)):
                        ins = pe.matmul(dst[:, k * width:(k + 1) * width], r[:, rows_of(k)], w, start=i == 0,
                                        stop=i == len(rows) - 1)
                return ins

            pe.wait_ge(wa_in, 16)
            pe.matmul(bank[7][:, 0:256], Wa[0:RANK, WA["dtin"]], Wa[0:RANK, WA["dtw"]], start=True, stop=True).then_inc(dt_w, 1)
            pe.wait_ge(const_in, 16)
            pe.wait_ge(conv_w, 1)
            pe.wait_ge(dt_wc, 1)
            pe.wait_ge(pads, 2)
            for g in range(G):
                pe.wait_ge(a_normed, g + 1)
                if g >= 2:
                    pe.wait_ge(bc_rest, g - 1)
                turn(bank[g % 2], Xn3, g).then_inc(a_turned, 1)
                pe.wait_ge(a_rows, g + 1)
                seqs = slice(2 * g, 2 * g + 2)
                for h in range(HALVES):
                    if g:
                        pe.wait_ge(u_ready, 2 * (g - 1) + h + 1)
                    for k in range(TAPS):
                        ins = pe.matmul(bank[2 + h][:], Wk[:, k, tile(h)], Xt3[:, seqs, k:k + S], start=k == 0, stop=k == TAPS - 1)
                    ins.then_inc(conv_done, 1)
                rows = Xt3[:, seqs, TAPS - 1:]
                for h in range(HALVES):
                    if g:
                        pe.wait_ge(z_ready, 2 * (g - 1) + h + 1)
                    pe.matmul(bank[4 + h][:], Wa[:, WA["z"]][:, tile(h)], rows, start=True, stop=True).then_inc(z_done, 1)
                pe.matmul(bank[g % 2][0:32, :], Wa[:, WA["bc"]], rows, start=True, stop=True).then_inc(bc_done, 1)
                for h in range(HALVES):
                    if g:
                        pe.wait_ge(dtx_ready, 2 * (g - 1) + h + 1)
                    pe.matmul(bank[6 + h][:], Wdt[:, tile(h)], rows, start=True, stop=True).then_inc(dt_done, 1)

            pe.wait_ge(sel_in, 16)
            pe.wait_ge(d_diag, HALVES)
            pe.wait_ge(dtx_ready, 8)
            for q in range(2):
                def rows_of_state(first_bank, row, done):
                    for c in range(2):
                        ins = pe.matmul(bank[first_bank + c][:], Sel[:, bass.ds(row * P, P)], Bc[:, group(2 * q + c)],
                                        start=True, stop=True)
                    ins.then_inc(done, 1)

                def add_state(h):
                    for c in range(2):
                        ins = pe.matmul(bank[2 * h + c][:], ident, Hc[:, h, group(c)], start=False, stop=False,
                                        skip_group_check=True)
                    return ins

                pe.wait_ge(u_ready, 8)
                pe.wait_ge(bc_ready, G)
                pe.wait_ge(bc_lo, G)
                if q:
                    pe.wait_ge(y_gated, 4)
                    pe.wait_ge(t1_ready, 2)
                for h in range(HALVES):
                    for c in range(2):
                        ins = pe.matmul(bank[2 * h + c][:], DiagD[:, tile(h)], U[:, h, group(2 * q + c)], start=True,
                                        stop=False, skip_group_check=True)
                    ins.then_inc(hc_used, 1)
                rows_of_state(4, 0, b_rows)
                rows_of_state(6, NSTATE, c_rows)
                base = q * 2 * NSTATE
                with pe.Fori(0, NSTATE - 1) as n:
                    pe.wait_ge(b_used, n * 2 + (base + 2))
                    rows_of_state(4, n + 1, b_rows)
                    pe.wait_ge(hc_ready, n * 2 + (base + 4))
                    rows_of_state(6, n + (1 + NSTATE), c_rows)
                    for h in range(HALVES):
                        add_state(h).then_inc(hc_used, 1)
                pe.wait_ge(hc_ready, 2 + base + 2 * NSTATE)
                for h in range(HALVES):
                    add_state(h).then_inc(hc_used, 1)
                for c in range(2):
                    g = 2 * q + c
                    pe.wait_ge(y_gated, 4 * q + 4)
                    tokens(bank[4 + c], [Z[:, h, group(g)] for h in range(HALVES)],
                           [Wa[:, WA["out"]][:, tile(h)] for h in range(HALVES)]).then_inc(y_proj, 1)

            pe.wait_ge(wb_in, 16)
            pe.wait_ge(t1_ready, G)
            pe.matmul(bank[7][:, 0:256], Wb[:, WB["q"]], Wb[:, WB["routers"]], start=True, stop=True)
            for h in range(2):
                ins = pe.matmul(bank[7][:, 256 + h * P:256 + (h + 1) * P], Wb[:, WB["values"]][:, tile(h)], Wb[:, WB["wout"]],
                                start=True, stop=True)
            ins.then_inc(tree_w, 1)
            for g in range(G):
                pe.wait_ge(b_normed, g + 1)
                if g >= 2:
                    pe.wait_ge(b_rows_t, g - 1)
                turn(bank[g % 2], Bn3, g).then_inc(b_turned, 1)
            pe.wait_ge(tree_wc, 1)
            for g in range(G):
                pe.wait_ge(b_rows_t, g + 1)
                for k in range(GT):
                    t = g * GT + k
                    if k % 2 == 0 and t >= 4:
                        pe.wait_ge(gated, t // 2 - 1)
                    ins = pe.matmul(bank[2 + t // 2 % 2][:, (k % 2) * LEAVES:(k % 2 + 1) * LEAVES], Bt[:, tile(t)], Wrq,
                                    start=True, stop=True)
                    if k % 2:
                        ins.then_inc(logits, 1)
            for g in range(G):
                pe.wait_ge(leaves, g + 1)
                for h in range(2):
                    if g:
                        pe.wait_ge(lp_rows, 2 * (g - 1) + h + 1)
                    for k in range(GT):
                        ins = pe.transpose(bank[4 + h][:, tile(k)], LpB[:, g * GT + k, tile(h)], ident)
                    ins.then_inc(lp_turned, 1)
                pe.wait_ge(lp_rows, 2 * g + 2)
                if g >= 2:
                    pe.wait_ge(t2_ready, g - 1)
                tokens(bank[6 + g % 2], [LpT[:, g, h, :] for h in range(2)], [Wlv[:, tile(h)] for h in range(2)]).then_inc(b_proj, 1)

            with pe.Fori(0, LAYERS) as layer:
                for g in range(G):
                    pe.wait_ge(c_normed, layer * G + g + 1)
                    if g >= 2:
                        pe.wait_ge(c_rows_t, layer * G + g - 1)
                    turn(bank[g % 2], Hn3, g).then_inc(c_turned, 1)
                pe.wait_ge(qkvg_in, layer * 16 + 16)
                for g in range(G + 1):
                    if g < G:
                        pe.wait_ge(c_rows_t, layer * G + g + 1)
                        for k in range(4):
                            if g:
                                pe.wait_ge(rotated, layer * 4 * G + 4 * (g - 1) + k + 1)
                            pe.matmul(bank[2 + k][:], Wl[:, WL["qk"]][:, tile(k)], Ht[:, group(g)], start=True, stop=True).then_inc(proj, 1)
                        for k in range(2):
                            if g:
                                pe.wait_ge(sg_ready, layer * 2 * G + 2 * (g - 1) + k + 1)
                            else:
                                pe.wait_ge(r_new, layer * G + G)
                            for j in range(2):
                                ins = pe.matmul(bank[6 + k][:, j * 256:(j + 1) * 256], Ht[:, tile(g * GT + 2 * k + j)],
                                                Wl[:, WL["vg"]], start=True, stop=True)
                            ins.then_inc(vg, 1)
                    if g >= 1:
                        for k in range(2):
                            pe.wait_ge(rotated, layer * 4 * G + 4 * (g - 1) + 3 + k)
                            if g == 1:
                                pe.wait_ge(c_rows_t, layer * G + G)
                            else:
                                pe.wait_ge(k_ready, layer * 2 * G + 2 * (g - 2) + k + 1)
                            pe.matmul(bank[k][:], dup, Tk[:, k, group(g - 1)], start=True, stop=True).then_inc(kdup, 1)
                for b in range(B + 1):
                    if b < B:
                        g = b // 2
                        pe.wait_ge(k_ready, layer * 2 * G + 2 * g + 2)
                        if b == 0:
                            pe.wait_ge(rotated, layer * 4 * G + 4 * G)
                        for h in range(HEADS):
                            i = b * HEADS + h
                            ab, rows = h // 4, slice(32 * (h % 4), 32 * (h % 4) + 32)
                            if i >= 4:
                                pe.wait_ge(masked, layer * B * HEADS + i - 3)
                            first, second = tile(2 * b), tile(2 * b + 1)
                            pe.matmul(bank[2 + i % 4][:, 0:2 * P], Kr[rows, ab, first], Tq[rows, ab, 2 * b * P:(2 * b + 2) * P],
                                      start=True, stop=True)
                            pe.matmul(bank[2 + i % 4][:, 2 * P:SCW], Kr[rows, ab, second], Tq[rows, ab, second],
                                      start=True, stop=True).then_inc(scores, 1)
                    if b >= 1:
                        c = b - 1
                        g = c // 2
                        if c == 0:
                            pe.wait_ge(sg_ready, layer * 2 * G + 2 * G)
                            pe.wait_ge(v_ready, layer * 2 * G + 2 * G)
                        if c % 2 == 0 and g >= 2:
                            pe.wait_ge(centred, layer * G + g - 1)
                        y = bank[6 + g % 2]
                        for h in range(HEADS):
                            pe.wait_ge(masked, layer * B * HEADS + c * HEADS + h + 1)
                            a = Att[:, (c % 2) * HEADS + h, :]
                            cols = slice(DH * h, DH * (h + 1))
                            at = (c % 2) * 256
                            v0, v1 = (V[:, (2 * c + j) * D:(2 * c + j + 1) * D][:, cols] for j in range(2))
                            pe.matmul(y[:, at:at + D][:, cols], a[:, 0:P], v0, start=True, stop=True)
                            pe.matmul(y[:, at + D:at + 2 * D][:, cols], a[:, P:2 * P], v0, start=True, stop=False)
                            ins = pe.matmul(y[:, at + D:at + 2 * D][:, cols], a[:, 2 * P:], v1, start=False, stop=True)
                        ins.then_inc(heads_out, 1)
                for g in range(G + 1):
                    if g < G:
                        pe.wait_ge(gy_ready, layer * G + g + 1)
                        if g >= 2:
                            pe.wait_ge(gy_rows, layer * G + g - 1)
                        turn(bank[g % 2], Yc.rearrange("p (t d) -> p t d", d=D), g).then_inc(gy_turned, 1)
                    if g >= 1:
                        k = g - 1
                        pe.wait_ge(gy_rows, layer * G + k + 1)
                        pe.wait_ge(out_in, layer * 16 + 16)
                        if k >= 2:
                            pe.wait_ge(r_mid, layer * G + k - 1)
                        tokens(bank[2 + k % 2], [Gyt[:, group(k % 2)]], [Wl[:, WL["wo"]]]).then_inc(wo_done, 1)
                for g in range(G + 1):
                    if g < G:
                        pe.wait_ge(f_normed, layer * G + g + 1)
                        if g >= 2:
                            pe.wait_ge(f_rows, layer * G + g - 1)
                        turn(bank[g % 2], Hn3, g).then_inc(f_turned, 1)
                        if g == 0:
                            pe.wait_ge(ffn_in, layer * 16 + 16)
                        pe.wait_ge(f_rows, layer * G + g + 1)
                        for k in range(2):
                            if g:
                                pe.wait_ge(gelu_ready, layer * 2 * G + 2 * (g - 1) + k + 1)
                            pe.matmul(bank[4 + k][:], Wl[:, WL["w1"]][:, tile(k)], Ht[:, group(g)], start=True, stop=True).then_inc(w1_done, 1)
                    if g >= 1:
                        k = g - 1
                        pe.wait_ge(gelu_ready, layer * 2 * G + 2 * k + 2)
                        if k >= 2:
                            pe.wait_ge(r_new, layer * G + (G + k - 1))
                        tokens(bank[6 + k % 2], [Ft[:, group(2 * (k % 2) + j)] for j in range(2)],
                               [Wl[:, WL["w2"]][:, tile(j)] for j in range(2)]).then_inc(w2_done, 1)

            pe.wait_ge(wd_in, 16)
            for g in range(G):
                pe.wait_ge(d_normed, g + 1)
                if g >= 2:
                    pe.wait_ge(d_rows, g - 1)
                turn(bank[g % 2], Dn3, g).then_inc(d_turned, 1)
            for g in range(G):
                pe.wait_ge(d_rows, g + 1)
                for k in range(GT):
                    t = g * GT + k
                    ins = pe.matmul(bank[2][:, t * EXPERTS:(t + 1) * EXPERTS], Dtr[:, tile(t)], Wd[:, WD["gate"]], start=True, stop=True)
            ins.then_inc(gate_done, 1)
            pe.wait_ge(chosen, 1)
            for g in range(G):
                if g >= 2:
                    pe.wait_ge(oh_rows, g - 1)
                for k in range(GT):
                    ins = pe.transpose(bank[g % 2][0:EXPERTS, tile(k)], oh[:, (g * GT + k) * EXPERTS:(g * GT + k + 1) * EXPERTS], ident)
                ins.then_inc(oh_turned, 1)

            def second(j):
                g, e = divmod(j, EXPERTS + 1)
                if j >= 2:
                    pe.wait_ge(mixed, j - 1)
                if e == 0:
                    pe.wait_ge(oh_rows, g + 1)
                    tokens(bank[4 + j % 2], [Oht[0:EXPERTS, group(g)]], [Wd[0:EXPERTS, WD["b2"]]]).then_inc(expert_out, 1)
                    return
                i = g * EXPERTS + e - 1
                pe.wait_ge(h_ready, i + 1)
                tokens(bank[4 + j % 2], [Hid[:, group(i % 2)]], [Wd[:, WD["w2"]][:, tile(e - 1)]]).then_inc(expert_out, 1)

            for g in range(G):
                for e in range(EXPERTS):
                    i = g * EXPERTS + e
                    if i >= 2:
                        pe.wait_ge(h_ready, i - 1)
                    pe.matmul(bank[2 + i % 2][:], Wd[:, WD["w1"]][:, tile(e)], Dtr[:, group(g)], start=True, stop=True).then_inc(hidden, 1)
                    if e == 0:
                        if g:
                            second(g * (EXPERTS + 1) - 1)
                        second(g * (EXPERTS + 1))
                    else:
                        second(g * (EXPERTS + 1) + e)
            second(G * (EXPERTS + 1) - 1)


def _pack(width, where, parts):
    out = np.zeros((P, width), np.float32)
    for name, a in parts.items():
        a = a.reshape(a.shape[0], -1)
        out[: a.shape[0], where[name].start : where[name].start + a.shape[1]] = a
    return out


def _columns(v):
    return np.ascontiguousarray(v.reshape(-1, P).T)


def _everywhere(v):
    return np.broadcast_to(v.reshape(1, -1), (P, v.size))


def _rotated(w):
    w = w.reshape(D, HEADS, DH)
    swapped = w.reshape(D, HEADS, DH // 2, 2)[..., ::-1].reshape(D, HEADS, DH)
    return np.concatenate([w, swapped], 2).reshape(D, 2, P)


def kernel(**inputs):
    import concourse.bacc as _bacc
    import ml_dtypes
    from concourse.bass_utils import run_bass_kernel_spmd as _run

    a = {k: np.asarray(v) for k, v in inputs.items()}
    win = a["L0_attn_W_in"]
    alog = a["L0_attn_A_log"].reshape(HALVES, P, NSTATE).transpose(1, 0, 2)
    taps = a["L0_attn_conv_w"][:, 0, :].T
    wa = _pack(WA_W, WA, {
        "x": win[:256].T, "z": win[256:512].T, "bc": win[512:544].T, "dtin": win[544:552],
        "dtw": a["L0_attn_W_dt"].T, "tap": _everywhere(taps), "out": a["L0_attn_W_out"].T.reshape(HALVES, P, D).transpose(1, 0, 2),
        "conv_b": _columns(a["L0_attn_conv_b"]), "b_dt": _columns(a["L0_attn_b_dt"]), "alog": alog,
        "dskip": _columns(a["L0_attn_D"]), "ln_g": _everywhere(a["L0_attn_ln_g"]), "ln_b": _everywhere(a["L0_attn_ln_b"])})
    wb = _pack(WB_W, WB, {
        "q": a["L0_ffn_Wq"], "routers": a["L0_ffn_routers"].T, "values": a["L0_ffn_leaf_values"].T,
        "wout": a["L0_ffn_Wout_w"].T, "bias": _everywhere(a["L0_ffn_Wout_b"])})
    wl = np.stack([_pack(WL_W, WL, {
        "qk": np.concatenate([_rotated(a["L1_attn_Wq"][i]), _rotated(a["L1_attn_Wk"][i])], 1),
        "vg": np.concatenate([a["L1_attn_Wv"][i], a["L1_attn_Wg"][i]], 1), "wo": a["L1_attn_Wo"][i],
        "gn": np.concatenate([_everywhere(a["L1_attn_gn_scale"][i]), _everywhere(a["L1_attn_gn_bias"][i])], 1),
        "w1": a["L1_attn_W1"][i], "w2": a["L1_attn_W2"][i].reshape(2, P, D).transpose(1, 0, 2)})
        for i in range(LAYERS)])
    wd = _pack(WD_W, WD, {
        "w1": a["L1_ffn_W1"].transpose(1, 0, 2), "w2": a["L1_ffn_W2"].transpose(1, 0, 2), "b1": a["L1_ffn_b1"].T,
        "gate": a["L1_ffn_Wg"], "bg": _everywhere(a["L1_ffn_bg"]), "b2": a["L1_ffn_b2"]})
    lnc = np.stack([a["L1_attn_ln_scale"], a["L1_attn_ln_bias"]], 1)
    arrays = {"x": a["L0_attn_x"], "wa": wa, "wb": wb, "wl": wl, "wd": wd, "lnc": lnc, "const": constants(),
              "sel": selectors().astype(ml_dtypes.bfloat16)}
    nc = _bacc.Bacc("TRN2", target_bir_lowering=False, num_devices=1)
    named = {}
    for name, v in arrays.items():
        arrays[name] = v = np.ascontiguousarray(v)
        named[name] = nc.dram_tensor(name, v.shape, mybir.dt.from_np(v.dtype), kind="ExternalInput").ap()
    out = nc.dram_tensor("out", (B, S, D), F32, kind="ExternalOutput").ap()
    four_blocks(nc, out=out, **named)
    r = _run(nc, [arrays], core_ids=[0])
    return r.results[0]["out"]
```

```python
from contextlib import ExitStack

import numpy as np

import concourse.bass as bass
from concourse import mybir

F32 = mybir.dt.float32
BF16 = mybir.dt.bfloat16
ALU = mybir.AluOpType
ACT = mybir.ActivationFunctionType
AX = mybir.AxisListType.X

P = 128
D = 128
B, S = 8, 256
T = B * S // P
G = 4
GT = T // G
GC = GT * P
EPS = 1e-5
NSTATE = 16
HALVES = 2
TAPS = 4
RANK = 8
DEPTH = 8
LEAVES = 1 << DEPTH
LAYERS = 4
HEADS, DH = 8, 16
CHUNK = 64
CHUNKS = GC // CHUNK
SEQ_CHUNKS = S // CHUNK
PARITY, PAIR = 2, 4
EXPERTS = 8


def offsets(*parts):
    at, out = 0, {}
    for name, width in parts:
        out[name] = slice(at, at + width)
        at += width
    return out, at


WA, WA_W = offsets(("x", 256), ("z", 256), ("bc", 32), ("dtin", P), ("dtw", 256), ("tap", TAPS * 256),
                   ("out", 256), ("conv_b", 2), ("b_dt", 2), ("alog", 2 * NSTATE), ("dskip", 2),
                   ("ln_g", D), ("ln_b", D))
WB, WB_W = offsets(("q", D), ("routers", LEAVES), ("values", LEAVES), ("wout", D), ("bias", D))
WD, WD_W = offsets(("w1", EXPERTS * D), ("w2", EXPERTS * D), ("b1", EXPERTS), ("gate", EXPERTS),
                   ("bg", EXPERTS), ("b2", D))
WL, WL_W = offsets(("qk", 4 * P), ("v", P), ("g", P), ("wo", P), ("gn", 2 * P), ("w1", 2 * P), ("w2", 2 * P))
CS, CS_W = offsets(("ident", P), ("causal", CHUNK), ("same_head", P), ("parity", PARITY), ("pair", PAIR),
                   ("tq", 2 * S), ("tk", 2 * S), ("rank", EXPERTS))
PER_LAYER_VECTOR = 2 * G * (3 * GT - 1) + 3 * G
PER_LAYER_SCALAR = G * (1 + (PARITY - 1) + (PAIR - 1))
PER_LAYER_POOL = 2 * G + 2 * G


def constants():
    c = np.zeros((P, CS_W), np.float32)
    c[:, CS["ident"]] = np.eye(P)
    k = np.arange(P)
    c[:, CS["causal"]] = np.arange(CHUNK)[None] >= k[:, None] % CHUNK
    c[:, CS["same_head"]] = k[:, None] // DH == k[None] // DH
    c[:, CS["parity"]] = k[:, None] // DH % 2 == np.arange(PARITY)
    c[:, CS["pair"]] = k[:, None] // (2 * DH) == np.arange(PAIR)
    pos = np.arange(S, dtype=np.float32)
    freq = (1.0 / 10000.0 ** (np.arange(0, DH, 2, dtype=np.float32) / DH)).astype(np.float32)
    ang = (pos[:, None] * freq[None]).astype(np.float64)
    decay = 1.0 - np.exp(np.linspace(np.log(1 / 32), np.log(1 / 64), HEADS)).astype(np.float32)
    decay = np.log(decay.astype(np.float32)).astype(np.float64)
    tq, tk = np.zeros((P, 2, S)), np.zeros((P, 2, S))
    for row in range(P):
        h, i = divmod(row, DH)
        grow = np.exp(np.arange(S) * decay[h])
        cos, sin = np.cos(ang[:, i // 2]), np.sin(ang[:, i // 2]) * (-1 if i % 2 == 0 else 1)
        tq[row, 0], tq[row, 1] = cos * grow, sin * grow
        tk[row, 0], tk[row, 1] = cos / grow, -sin / grow
    c[:, CS["tq"]] = tq.reshape(P, -1)
    c[:, CS["tk"]] = tk.reshape(P, -1)
    c[:, CS["rank"]] = np.arange(EXPERTS, 0, -1)
    return c


def selectors():
    sel = np.zeros((P, 2 * NSTATE, P), np.float32)
    for s in range(2 * NSTATE):
        for part in range(3):
            sel[s + 32 * part, s] = 1.0
    return sel.reshape(P, -1)


class Steps:

    def __init__(self, eng, sem):
        self.eng, self.sem, self.n, self.turns = eng, sem, 0, None

    def put(self, ins):
        ins.then_inc(self.sem, 1)
        self.n += 1

    def settle(self):
        self.eng.wait_ge(self.sem, self.n if self.turns is None else self.turns + self.n)

    def enter(self, turn, per):
        self.start, self.per = self.n, per
        self.turns, self.n = turn * per + self.n, 0

    def leave(self, turns):
        assert self.n == self.per, (self.n, self.per)
        self.turns, self.n = None, self.start + turns * self.per


class Counter:

    def __init__(self):
        self.n, self.turns = 0, None

    def next(self):
        self.n += 1
        return self.n if self.turns is None else self.turns + self.n

    def enter(self, turn, per):
        self.start, self.per = self.n, per
        self.turns, self.n = turn * per + self.n, 0

    def leave(self, turns):
        assert self.n == self.per, (self.n, self.per)
        self.turns, self.n = None, self.start + turns * self.per


class PerGroup:

    def __init__(self, sem, per, primed):
        self.sem, self.per, self.primed = sem, per, primed

    def at(self, layer, g, k=None):
        turn, ahead = layer
        const = (ahead + self.primed) * self.per * G + self.per * g + (self.per if k is None else k)
        if isinstance(turn, int):
            const += turn * self.per * G
        assert const > 0
        return self.sem, const if isinstance(turn, int) else turn * (self.per * G) + const


SCHEDULE = (
    (0.220, "stats1", 0), (0.510, "norm1", 0), (0.780, "turn1", 0), (0.900, "rotate", 0), (0.980, "spread", 0),
    (1.050, "spread", 1), (1.130, "values", 0), (1.380, "scores", 0), (1.390, "keys", 0), (1.400, "scores", 1),
    (1.480, "gate", 0), (1.590, "states", 0), (1.630, "scores", 2), (1.640, "scores", 3), (1.800, "mix", 0),
    (1.840, "gather", 0), (2.070, "heads", 0), (2.090, "square", 0), (2.320, "var", 0), (2.830, "unit", 0),
    (2.900, "scale", 0), (2.970, "out_turn", 0), (3.110, "out", 0), (3.110, "stats2", 0), (3.630, "norm2", 0),
    (3.860, "ffn_turn", 0), (4.020, "ffn_up", 0), (4.210, "ffn_down", 0),)


def layer_order():
    placed = sorted((g + t, what, k, g) for g in range(G) for t, what, k in SCHEDULE)
    return [(what, k, g, int(at < G)) for _, at, what, k, g in sorted((at % G, at, what, k, g) for at, what, k, g in placed)]


LAYER = layer_order()
FIRST_FRONTS = [(what, k, g, 0) for what, k, g, ahead in LAYER if ahead]
LAST_TAILS = [step for step in LAYER if not step[3]]


def four_blocks(nc, x, wa, wb, wl, wd, lnc, const, sel, out):
    with ExitStack() as ctx:
        def sbuf(name, width, dtype=F32):
            return ctx.enter_context(nc.sbuf_tensor(name, [P, width], dtype))

        def sem(name):
            return ctx.enter_context(nc.semaphore(name))

        X = sbuf("X", T * D)
        Wa, Wb, Wl, Wd = sbuf("Wa", WA_W), sbuf("Wb", WB_W), sbuf("Wl", WL_W), sbuf("Wd", WD_W)
        Cs = sbuf("Cs", CS_W)
        Sel = sbuf("Sel", 2 * NSTATE * P, BF16)
        st, mv = sbuf("st", T * 6), sbuf("mv", T * 2)
        ve, rs = sbuf("ve", T), sbuf("rs", T)
        mhalf = sbuf("mhalf", 32)
        eps = sbuf("eps", GT)
        scratch = sbuf("scratch", 32)
        ident = Cs[:, CS["ident"]]
        st3, mv3 = st[:].rearrange("p (t s) -> p t s", s=6), mv[:].rearrange("p (t s) -> p t s", s=2)
        X3 = X[:].rearrange("p (t d) -> p t d", d=D)
        psum = ctx.enter_context(nc.psum_tensor("psum", [P, 8 * GC], F32))
        bank = [psum[:, i * GC:(i + 1) * GC] for i in range(8)]

        ARENA = 37400
        arena = sbuf("arena", ARENA)
        top = [0]

        def take(width):
            top[0] += width
            assert top[0] <= ARENA, top[0]
            return arena[:, top[0] - width:top[0]]

        Xn = take(T * D)
        Xt = take(B * (S + TAPS - 1))
        Xt3 = Xt.rearrange("p (b s) -> p b s", b=B)
        U = take(HALVES * 2048).rearrange("p (h c) -> p h c", h=HALVES)
        Z = take(HALVES * 2048).rearrange("p (h c) -> p h c", h=HALVES)
        Dt = take(HALVES * 2048).rearrange("p (h c) -> p h c", h=HALVES)
        Dtu = take(HALVES * 2048).rearrange("p (h c) -> p h c", h=HALVES)
        Da = take(HALVES * 1024).rearrange("p (h c) -> p h c", h=HALVES)
        Dbu = take(HALVES * 1024).rearrange("p (h c) -> p h c", h=HALVES)
        Hs = take(2 * HALVES * 1024).rearrange("p (r h c) -> p r h c", r=2, h=HALVES)
        Hc = take(HALVES * 1024).rearrange("p (h c) -> p h c", h=HALVES)
        Bc = take(1024).bitcast(BF16)
        Rest, Mid = take(GC), take(GC // 2).bitcast(BF16)
        T1 = take(T * D)
        Crows = take(2 * 1024).rearrange("p (r c) -> p r c", r=2)
        Wk = Crows[:, 0, :].rearrange("p (k c) -> p k c", k=TAPS)
        Wdt, DiagD, Aneg = take(256), take(256), take(2 * NSTATE)
        T13 = T1.rearrange("p (t d) -> p t d", d=D)
        Xn3 = Xn.rearrange("p (t d) -> p t d", d=D)

        top[0] = 0
        Bn, Bt = take(T * D), take(T * D)
        Gates = take(T * LEAVES).rearrange("p (t n) -> p t n", t=T)
        LpA = take(T * LEAVES).rearrange("p (t n) -> p t n", t=T)
        LpB = take(T * LEAVES).rearrange("p (t n) -> p t n", t=T)
        LpT = take(G * 2 * GC).rearrange("p (g h c) -> p g h c", g=G, h=2)
        Wrq, Wlv = take(LEAVES), take(2 * D)
        T2 = take(T * D)
        Bn3, T23 = Bn.rearrange("p (t d) -> p t d", d=D), T2.rearrange("p (t d) -> p t d", d=D)

        top[0] = 0
        R, Hn, Ht = take(T * D), take(T * D), take(T * D)
        Tq = take(2 * 2 * GC).rearrange("p (a c) -> p a c", a=2)
        Tk = take(2 * 2 * GC).rearrange("p (a c) -> p a c", a=2)
        Qr, Kr = take(2 * GC), take(2 * GC)
        Qp = take(2 * CHUNKS * PAIR * CHUNK).rearrange("p (c n) -> p c n", n=PAIR * CHUNK)
        Ka = take(2 * CHUNKS * P).rearrange("p (c n) -> p c n", n=P)
        Kt = take(4 * (SEQ_CHUNKS - 1) * P).rearrange("p (b n) -> p b n", b=4)
        Va = take(2 * CHUNKS * P).rearrange("p (c n) -> p c n", n=P)
        States = take(4 * (SEQ_CHUNKS - 1) * P).rearrange("p (b n) -> p b n", b=4)
        Th, Yt, Gyt = take(2 * GC), take(2 * GC), take(2 * GC)
        Ft = take(2 * 2 * GC)
        Sg = take(T * D)
        Att = take(CHUNKS * PAIR * CHUNK).rearrange("p (c n) -> p c n", n=PAIR * CHUNK)
        Yc, Ys = take(T * D), take(GC)
        gst = take(G * 96)
        Lnc = take(2)
        R3, Hn3 = R.rearrange("p (t d) -> p t d", d=D), Hn.rearrange("p (t d) -> p t d", d=D)

        top[0] = 0
        Dn, Dtr, T3 = take(T * D), take(T * D), take(T * D)
        Hid = take(2 * GC)
        lg, ex, oh, tmp = take(T * EXPERTS), take(T * EXPERTS), take(T * EXPERTS), take(T * EXPERTS)
        red = take(4 * T)
        Oht = take(2048)
        Dn3, T33 = Dn.rearrange("p (t d) -> p t d", d=D), T3.rearrange("p (t d) -> p t d", d=D)

        x_in = [sem(f"x_in{g}") for g in range(G)]
        wa_in, wb_in, wd_in = sem("wa_in"), sem("wb_in"), sem("wd_in")
        const_in, sel_in, lnc_in, stored = sem("const_in"), sem("sel_in"), sem("lnc_in"), sem("stored")
        qkvg_in, out_in, ffn_in = sem("qkvg_in"), sem("out_in"), sem("ffn_in")
        vec, pol, act_steps = sem("vector_steps"), sem("pool_steps"), sem("scalar_steps")
        var_ready, rstd_ready = sem("var_ready"), sem("rstd_ready")
        conv_w, dt_w, dt_wc, a_neg, d_diag = sem("conv_w"), sem("dt_w"), sem("dt_w_copied"), sem("a_neg"), sem("d_diag")
        pads = sem("pads")
        a_normed, a_turned, a_rows = sem("a_normed"), sem("a_turned"), sem("a_rows")
        conv_done, z_done, bc_done, dt_done = sem("conv_done"), sem("z_done"), sem("bc_done"), sem("dt_done")
        u_ready, z_ready, bc_hi, bc_rest, bc_mid, bc_lo, bc_ready = (
            sem("u_ready"), sem("z_ready"), sem("bc_hi"), sem("bc_rest"), sem("bc_mid"), sem("bc_lo"), sem("bc_ready"))
        dtx_ready, exp_ready, ln_ready, log_rest, dt_ready, dtu_ready = (
            sem("dtx_ready"), sem("exp_ready"), sem("ln_ready"), sem("log_rest"), sem("dt_ready"), sem("dtu_ready"))
        b_rows, b_used, c_rows, c_copied = sem("b_rows"), sem("b_used"), sem("c_rows"), sem("c_copied")
        da_ready, scanned, hc_ready, hc_used = sem("da_ready"), sem("scanned"), sem("hc_ready"), sem("hc_used")
        y_gated, y_proj, t1_ready = sem("y_gated"), sem("y_proj"), sem("t1_ready")
        g_normed, g_scaled, o_normed, xa_ready = sem("g_normed"), sem("g_scaled"), sem("o_normed"), sem("xa_ready")
        tree_w, tree_wc = sem("tree_w"), sem("tree_w_copied")
        b_normed, b_turned, b_rows_t, logits, gated, leaves = (
            sem("b_normed"), sem("b_turned"), sem("b_rows_turned"), sem("logits"), sem("gated"), sem("leaves"))
        lp_turned, lp_rows, b_proj, t2_ready, t2_normed, xb_ready = (
            sem("lp_turned"), sem("lp_rows"), sem("b_proj"), sem("t2_ready"), sem("t2_normed"), sem("xb_ready"))
        def per_group(name, per=1, primed=0):
            return PerGroup(sem(name), per, primed)

        r_new, vd_zero, r_normed, xc_ready = sem("r_new"), sem("vd_zero"), sem("r_normed"), sem("xc_ready")
        r_new_in = PerGroup(r_new, 1, 0)
        r_newer = PerGroup(r_new, 1, 1)
        c_normed, c_turned, hn_rows = per_group("c_normed"), per_group("c_turned"), per_group("hn_rows", 1, 1)
        proj, rotated, summed = per_group("proj", 4), per_group("rotated", 4, 1), per_group("summed", 2, 1)
        v_done, v_ready = per_group("v_done"), per_group("v_ready", 1, 1)
        g_done, th_ready, sg_ready = per_group("g_done"), per_group("th_ready"), per_group("sg_ready", 1, 1)
        k_spread, q_spread = per_group("k_spread"), per_group("q_spread")
        k_turned, k_tokens = per_group("k_turned", 2), per_group("k_tokens", 2, 1)
        scores, masked = per_group("scores", 4), per_group("masked", 4, 1)
        state_done, states = per_group("state_done", 2), per_group("states", 2, 1)
        added, yt_rows, y_turned = per_group("added", 1, 1), per_group("yt_rows", 1, 1), per_group("y_turned")
        centred, squared, y_unit = per_group("centred", 1, 1), per_group("squared"), per_group("y_unit")
        gy_ready, gy_turned, gy_rows = per_group("gy_ready"), per_group("gy_turned"), per_group("gy_rows", 1, 1)
        wo_done, r_mid = per_group("wo_done"), per_group("r_mid", 1, 1)
        f_normed, f_turned, f_rows = per_group("f_normed"), per_group("f_turned"), per_group("f_rows", 1, 1)
        w1_done, gelu_ready, w2_done = per_group("w1_done", 2), per_group("gelu_ready", 2, 1), per_group("w2_done")
        primed = (hn_rows, rotated, summed, v_ready, sg_ready, k_tokens, masked, states, added, yt_rows, centred,
                  gy_rows, r_mid, f_rows, gelu_ready)
        FILLS = {
            "turn1": ((0, hn_rows, 1),), "heads": ((0, centred, 1),), "out_turn": ((0, gy_rows, 1),),
            "ffn_turn": ((0, f_rows, 1),),
            "rotate": ((5, rotated, 1), (1, rotated, 2), (4, rotated, 3), (5, rotated, 4)),
            "values": ((4, v_ready, 1),), "gate": ((4, sg_ready, 1),),
            "keys": ((1, k_tokens, 1), (5, k_tokens, 2)), "states": ((5, states, 1), (1, states, 2)),
            "out": ((5, r_mid, 1),), "ffn_up": ((4, gelu_ready, 1), (1, gelu_ready, 2)), "ffn_down": ((1, r_newer, 1),)}
        d_normed, d_turned, d_rows, gate_done, shifted, exps, chosen, oh_turned, oh_rows = (
            sem("d_normed"), sem("d_turned"), sem("d_rows"), sem("gate_done"), sem("shifted"), sem("exps"),
            sem("chosen"), sem("oh_turned"), sem("oh_rows"))
        hidden, h_ready, expert_out, mixed, t3_normed, xd_ready = (
            sem("hidden"), sem("h_ready"), sem("expert_out"), sem("mixed"), sem("t3_normed"), sem("xd_ready"))

        def group(g):
            return slice(g * GC, (g + 1) * GC)

        def tile(t):
            return slice(t * P, (t + 1) * P)

        block = ctx.enter_context(nc.Block())

        @block.sync
        def _(sync):
            x_tiles = x.rearrange("b (h p) d -> p (b h) d", p=P)
            for g in range(G):
                sync.dma_start(X3[:, g * GT:(g + 1) * GT, :], x_tiles[:, g * GT:(g + 1) * GT, :]).then_inc(x_in[g], 16)
                if g == 0:
                    sync.dma_start(Cs[:], const).then_inc(const_in, 16)
                    sync.dma_start(Wa[:], wa).then_inc(wa_in, 16)
            sync.dma_start(Sel[:], sel).then_inc(sel_in, 16)
            sync.dma_start(Wb[:], wb).then_inc(wb_in, 16)
            sync.dma_start(Wd[:], wd).then_inc(wd_in, 16)
            parts = ((slice(WL["qk"].start, WL["g"].stop), qkvg_in), (slice(WL["wo"].start, WL["gn"].stop), out_in),
                     (slice(WL["w1"].start, WL["w2"].stop), ffn_in))
            for cols, landed in parts:
                sync.dma_start(Wl[:, cols], wl[0, :, cols]).then_inc(landed, 16)
            sync.wait_ge(xb_ready, G)
            sync.dma_start(Lnc, lnc).then_inc(lnc_in, 16)
            with sync.Fori(0, LAYERS - 1) as layer:
                nxt = wl[bass.ds(layer + 1, 1)].rearrange("a p c -> (a p) c")
                for done in (proj, v_done, g_done):
                    sync.wait_ge(*done.at((layer, 0), G - 1))
                sync.dma_start(Wl[:, parts[0][0]], nxt[:, parts[0][0]]).then_inc(qkvg_in, 16)
                sync.wait_ge(*wo_done.at((layer, 0), G - 1))
                sync.dma_start(Wl[:, parts[1][0]], nxt[:, parts[1][0]]).then_inc(out_in, 16)
                sync.wait_ge(*w2_done.at((layer, 0), G - 1))
                sync.dma_start(Wl[:, parts[2][0]], nxt[:, parts[2][0]]).then_inc(ffn_in, 16)
            out_tiles = out.rearrange("b (h p) d -> p (b h) d", p=P)
            for g in range(G):
                sync.wait_ge(xd_ready, g + 1)
                sync.dma_start(out_tiles[:, g * GT:(g + 1) * GT, :], X3[:, g * GT:(g + 1) * GT, :]).then_inc(stored, 16)
            sync.wait_ge(stored, 16 * G)

        @block.gpsimd
        def _(pool):
            own = Steps(pool, pol)
            norms = Counter()

            def rstd(g):
                pool.wait_ge(var_ready, norms.next())
                own.put(pool.tensor_tensor(ve[:, g * GT:(g + 1) * GT], mv3[:, g * GT:(g + 1) * GT, 1], eps[:, 0:GT], ALU.add))
                own.settle()
                pool.tensor_tensor(rs[:, g * GT:(g + 1) * GT], ve[:, g * GT:(g + 1) * GT], mhalf[:, 0:GT],
                                   ALU.pow).then_inc(rstd_ready, 1)

            own.put(pool.memset(mhalf[:], -0.5))
            own.put(pool.memset(eps[:], EPS))
            pool.memset(Xt3[:, :, 0:TAPS - 1], 0.0).then_inc(pads, 1)
            for h in range(HALVES):
                pool.memset(Da[:, h].rearrange("p (b s) -> p b s", s=S)[:, :, 0:1], 0.0).then_inc(scanned, 1)
            pool.memset(Crows[:, 1], 0.0).then_inc(hc_ready, 4)
            pool.memset(Bc[:, :], 0.0).then_inc(pads, 1)
            own.settle()
            pool.wait_ge(wa_in, 16)
            for k in range(TAPS):
                last = pool.tensor_tensor(Wk[:, k, :], Wa[:, WA["x"]],
                                          Wa[:, WA["tap"]].rearrange("p (k c) -> p k c", k=TAPS)[:, k, :], ALU.mult)
                if k < TAPS - 1:
                    own.put(last)
            last.then_inc(conv_w, 1)
            pool.wait_ge(const_in, 16)
            for h in range(HALVES):
                pool.tensor_scalar(DiagD[:, tile(h)], ident, Wa[:, WA["dskip"]][:, h:h + 1], None,
                                   ALU.mult).then_inc(d_diag, 1)
            for g in range(G):
                rstd(g)
            for half in range(4):
                q, h = divmod(half, HALVES)
                pool.wait_ge(exp_ready, half + 1)
                if q:
                    pool.wait_ge(hc_used, 2 + 2 * NSTATE)
                    pool.wait_ge(hc_ready, 4 + 2 * NSTATE)
                own.put(pool.tensor_scalar(Hc[:, h], Dbu[:, h], 1.0, -1.0, ALU.add, ALU.add))
                own.settle()
                pool.tensor_tensor(Hc[:, h], Dbu[:, h], Hc[:, h], ALU.subtract).then_inc(log_rest, 1)
                if h == 1:
                    pool.wait_ge(dt_ready, 2 * q + 2)
                    with pool.Fori(0, NSTATE // 2) as pair:
                        for r in range(2):
                            s = pair * 2 + (q * NSTATE + r)
                            pool.wait_ge(c_copied, s + 1)
                            for h in range(HALVES):
                                pool.wait_ge(scanned, s * 2 + (h + 3))
                                pool.wait_ge(hc_used, pair * 4 + (q * (2 * NSTATE + 2) + 2 * r + h + 1))
                                pool.tensor_tensor(Hc[:, h], Hs[:, r, h], Crows[:, r], ALU.mult).then_inc(hc_ready, 1)
            for g in range(G):
                rstd(g)
                pool.wait_ge(g_normed, g + 1)
                t = T13[:, g * GT:(g + 1) * GT, :]
                for col, op in (("ln_g", ALU.mult), ("ln_b", ALU.add)):
                    row = Wa[:, WA[col]].unsqueeze(1).broadcast_to((P, GT, D))
                    ins = pool.tensor_tensor(t, t, row, op)
                    if op == ALU.mult:
                        own.put(ins)
                        own.settle()
                ins.then_inc(g_scaled, 1)
                rstd(g)
                pool.wait_ge(o_normed, g + 1)
                xg = X3[:, g * GT:(g + 1) * GT, :]
                pool.tensor_tensor(xg, xg, t, ALU.add).then_inc(xa_ready, 1)

            for g in range(G):
                rstd(g)
            for g in range(G):
                rstd(g)
                pool.wait_ge(t2_normed, g + 1)
                xg = X3[:, g * GT:(g + 1) * GT, :]
                pool.tensor_tensor(xg, xg, T23[:, g * GT:(g + 1) * GT, :], ALU.add).then_inc(xb_ready, 1)

            pool.memset(Va.rearrange("p c n -> p (c n)"), 0.0).then_inc(vd_zero, 1)
            for i, event in enumerate(primed):
                pool.memset(scratch[:, 1 + i:2 + i], 0.0).then_inc(event.sem, event.per * G)
            for g in range(G):
                rstd(g)
            pool.wait_ge(lnc_in, 16)

            def layer_steps(order, turn):
                for what, part, g, ahead in order:
                    layer = (turn, ahead)
                    half = slice(g % 2 * GC, (g % 2 + 1) * GC)
                    if what in ("stats1", "stats2"):
                        rstd(g)
                    if what == "spread":
                        dst, halves = ((Kr, Tk), (Qr, Tq))[part]
                        pool.wait_ge(*added.at(layer, g - 2))
                        pool.wait_ge(*rotated.at(layer, g, 2 * part + 2))
                        pool.tensor_tensor(dst[:, half], halves[:, 0, half], halves[:, 1, half], ALU.add).then_inc(summed.sem, 1)
                    if what == "var":
                        cols = slice(g * 96 + 64, g * 96 + 96)
                        pool.wait_ge(var_ready, norms.next())
                        pool.tensor_tensor(gst[:, cols], gst[:, cols], mhalf[:], ALU.pow).then_inc(rstd_ready, 1)
                    if what == "scale":
                        pool.wait_ge(*y_unit.at(layer, g))
                        if g == 0:
                            pool.wait_ge(out_in, turn * 16 + 16 * (ahead + 1))
                        y = Yc[:, group(g)].rearrange("p (t d) -> p t d", d=D)
                        gn = Wl[:, WL["gn"]].rearrange("p (a d) -> p a d", a=2)
                        own.put(pool.tensor_tensor(y, y, gn[:, 0:1, :].broadcast_to((P, GT, D)), ALU.mult))
                        own.settle()
                        own.put(pool.tensor_tensor(y, y, gn[:, 1:2, :].broadcast_to((P, GT, D)), ALU.add))
                        own.settle()
                        pool.wait_ge(*sg_ready.at(layer, g))
                        pool.tensor_tensor(Yc[:, group(g)], Yc[:, group(g)], Sg[:, group(g)], ALU.mult).then_inc(gy_ready.sem, 1)

            layer_steps(FIRST_FRONTS, 0)
            with pool.Fori(0, LAYERS - 1) as layer:
                own.enter(layer, PER_LAYER_POOL)
                norms.enter(layer, 3 * G)
                layer_steps(LAYER, layer)
                own.leave(LAYERS - 1)
                norms.leave(LAYERS - 1)
            layer_steps(LAST_TAILS, LAYERS - 1)
            for g in range(G):
                rstd(g)
                pool.wait_ge(r_normed, g + 1)
                xg = X3[:, g * GT:(g + 1) * GT, :]
                pool.tensor_tensor(xg, xg, Hn3[:, g * GT:(g + 1) * GT, :], ALU.add).then_inc(xc_ready, 1)

            for g in range(G):
                rstd(g)
            for g in range(G):
                rstd(g)
                pool.wait_ge(t3_normed, g + 1)
                xg = X3[:, g * GT:(g + 1) * GT, :]
                pool.tensor_tensor(xg, xg, T33[:, g * GT:(g + 1) * GT, :], ALU.add).then_inc(xd_ready, 1)

        @block.scalar
        def _(act):
            own = Steps(act, act_steps)
            act.wait_ge(wa_in, 16)
            own.put(act.activation(Aneg, Wa[:, WA["alog"]], ACT.Exp))
            own.settle()
            act.mul(Aneg, Aneg, -1.0).then_inc(a_neg, 1)

            act.wait_ge(pads, 2)
            for g in range(G):
                act.wait_ge(a_turned, g + 1)
                act.copy(Xt3[:, 2 * g:2 * g + 2, TAPS - 1:], bank[g % 2][:].rearrange("p (b s) -> p b s", b=2)).then_inc(a_rows, 1)
                for h in range(HALVES):
                    act.wait_ge(conv_done, 2 * g + h + 1)
                    act.activation(U[:, h, group(g)], bank[2 + h][:], ACT.Silu,
                                   bias=Wa[:, WA["conv_b"]][:, h:h + 1]).then_inc(u_ready, 1)
                for h in range(HALVES):
                    act.wait_ge(z_done, 2 * g + h + 1)
                    act.activation(Z[:, h, group(g)], bank[4 + h][:], ACT.Silu).then_inc(z_ready, 1)
                act.wait_ge(bc_done, g + 1)
                act.copy(Bc[0:32, group(g)], bank[g % 2][0:32, :]).then_inc(bc_hi, 1)
                act.wait_ge(bc_rest, g + 1)
                act.copy(Mid[0:32, :], Rest[0:32, :]).then_inc(bc_mid, 1)
                act.wait_ge(bc_mid, g + 1)
                act.copy(Bc[32:64, group(g)], Mid[0:32, :]).then_inc(bc_ready, 1)

            act.preload_act_table_set("natural_log_exp_and_others")
            for q in range(2):
                cols = slice(q * 1024, (q + 1) * 1024)
                for h in range(HALVES):
                    act.wait_ge(dtx_ready, 4 * q + 2 + h + 1)
                    if q:
                        act.wait_ge(scanned, 2 + 2 * NSTATE)
                        act.wait_ge(hc_ready, 4 + 2 * NSTATE)
                    own.put(act.activation(Hs[:, 0, h], Dt[:, h, cols], ACT.Abs))
                    own.settle()
                    act.activation(Dbu[:, h], Hs[:, 0, h], ACT.Exp, scale=-1.0).then_inc(exp_ready, 1)
                    act.wait_ge(exp_ready, 2 * q + h + 1)
                    act.activation(Hs[:, 0, h], Dbu[:, h], ACT.Ln, bias=1.0).then_inc(ln_ready, 1)
                act.wait_ge(dtu_ready, 2 * q + 2)
                with act.Fori(0, NSTATE // 2) as pair:
                    for r in range(2):
                        s = pair * 2 + (q * NSTATE + r)
                        for h in range(HALVES):
                            act.wait_ge(scanned, s * 2 + (h + 1))
                            seq = "p (b s) -> p b s"
                            act.activation(Da[:, h].rearrange(seq, s=S)[:, :, 1:], Dt[:, h, cols].rearrange(seq, s=S)[:, :, 1:],
                                           ACT.Exp, scale=Aneg[:, bass.ds(pair * 2 + (r + h * NSTATE), 1)]).then_inc(da_ready, 1)
                        act.wait_ge(c_rows, s + 1)
                        act.wait_ge(hc_ready, s * 2 + 2)
                        act.copy(Crows[:, r], psum[:, 6 * GC:8 * GC]).then_inc(c_copied, 1)

            for g in range(G):
                act.wait_ge(b_turned, g + 1)
                act.copy(Bt[:, group(g)], bank[g % 2][:]).then_inc(b_rows_t, 1)
            for t in range(T // 2):
                act.wait_ge(logits, t + 1)
                act.activation(Gates[:, 2 * t:2 * t + 2, :], bank[2 + t % 2][:], ACT.Sigmoid).then_inc(gated, 1)
            for g in range(G):
                for h in range(2):
                    act.wait_ge(lp_turned, 2 * g + h + 1)
                    act.copy(LpT[:, g, h, :], bank[4 + h][:]).then_inc(lp_rows, 1)

            act.wait_ge(lnc_in, 16)
            act.preload_act_table(ACT.Gelu_apprx_tanh)
            act.wait_ge(vd_zero, 1)
            as3 = "p (t d) -> p t d"

            def layer_steps(order, turn):
                for what, part, g, ahead in order:
                    layer = (turn, ahead)
                    half = slice(g % 2 * GC, (g % 2 + 1) * GC)
                    chunks = slice(g % 2 * CHUNKS, (g % 2 + 1) * CHUNKS)
                    if what == "turn1":
                        act.wait_ge(*c_turned.at(layer, g))
                        act.activation(Ht[:, group(g)], bank[0], ACT.Identity, bias=Lnc[:, 1:2],
                                       scale=Lnc[:, 0:1]).then_inc(hn_rows.sem, 1)
                    if what == "values":
                        act.wait_ge(*v_done.at(layer, g))
                        act.wait_ge(*added.at(layer, g - 2))
                        for a in range(PARITY):
                            half_rows = slice(CHUNK * a, CHUNK * a + CHUNK)
                            dst = Va[half_rows, chunks, :].rearrange("p c (j w) -> p (c j) w", j=PAIR)[:, :, DH * a:DH * a + DH]
                            ins = act.copy(dst, bank[FILLS[what][0][0]][half_rows, :].rearrange("p (c i) -> p c i", i=DH))
                            if a == 0:
                                own.put(ins)
                        ins.then_inc(v_ready.sem, 1)
                    if what == "gate":
                        act.wait_ge(*g_done.at(layer, g))
                        act.activation(Th[:, half], bank[FILLS[what][0][0]], ACT.Tanh, scale=0.5).then_inc(th_ready.sem, 1)
                    if what == "spread":
                        rows, copies, masks, done = ((Kr, Ka, "parity", k_spread), (Qr, Qp, "pair", q_spread))[part]
                        act.wait_ge(*summed.at(layer, g, part + 1))
                        count = (PARITY, PAIR)[part]
                        for i in range(count):
                            ins = act.activation(copies[:, chunks, i * CHUNK:(i + 1) * CHUNK],
                                                 rows[:, half].rearrange("p (c n) -> p c n", n=CHUNK),
                                                 ACT.Identity, scale=Cs[:, CS[masks]][:, i:i + 1])
                            if i < count - 1:
                                own.put(ins)
                        ins.then_inc(done.sem, 1)
                    if what == "keys":
                        for b in range(2):
                            act.wait_ge(*k_turned.at(layer, g, b + 1))
                            act.copy(Kt[:, g % 2 * 2 + b, :], bank[FILLS[what][b][0]][:, 0:(SEQ_CHUNKS - 1) * P]).then_inc(k_tokens.sem, 1)
                    if what == "gather":
                        act.wait_ge(*added.at(layer, g))
                        act.copy(Yt[:, half], bank[6 + g % 2]).then_inc(yt_rows.sem, 1)
                    if what == "square":
                        act.wait_ge(*centred.at(layer, g))
                        act.square(Ys, Yc[:, group(g)]).then_inc(squared.sem, 1)
                    if what == "out_turn":
                        act.wait_ge(*gy_turned.at(layer, g))
                        act.mul(Gyt[:, half], bank[0], 0.5).then_inc(gy_rows.sem, 1)
                    if what == "ffn_turn":
                        act.wait_ge(*f_turned.at(layer, g))
                        act.activation(Ht[:, group(g)], bank[0], ACT.Identity, bias=Lnc[:, 1:2],
                                       scale=Lnc[:, 0:1]).then_inc(f_rows.sem, 1)
                    if what == "ffn_up":
                        for k in range(2):
                            act.wait_ge(*w1_done.at(layer, g, k + 1))
                            act.activation(Ft[:, group(2 * (g % 2) + k)], bank[FILLS[what][k][0]],
                                           ACT.Gelu_apprx_tanh).then_inc(gelu_ready.sem, 1)

            layer_steps(FIRST_FRONTS, 0)
            with act.Fori(0, LAYERS - 1) as layer:
                own.enter(layer, PER_LAYER_SCALAR)
                layer_steps(LAYER, layer)
                own.leave(LAYERS - 1)
            layer_steps(LAST_TAILS, LAYERS - 1)

            for g in range(G):
                act.wait_ge(d_turned, g + 1)
                act.copy(Dtr[:, group(g)], bank[g % 2][:]).then_inc(d_rows, 1)
            act.wait_ge(shifted, 1)
            act.activation(ex, lg, ACT.Exp).then_inc(exps, 1)
            for g in range(G):
                act.wait_ge(oh_turned, g + 1)
                act.copy(Oht[0:EXPERTS, group(g)], bank[g % 2][0:EXPERTS, :]).then_inc(oh_rows, 1)
            for g in range(G):
                for e in range(EXPERTS):
                    i = g * EXPERTS + e
                    act.wait_ge(hidden, i + 1)
                    if i >= 2:
                        act.wait_ge(expert_out, (i - 2) // EXPERTS * (EXPERTS + 1) + (i - 2) % EXPERTS + 2)
                    act.activation(Hid[:, group(i % 2)], bank[2 + i % 2][:], ACT.Gelu,
                                   bias=Wd[:, WD["b1"]][:, e:e + 1]).then_inc(h_ready, 1)

        @block.vector
        def _(dve):
            own = Steps(dve, vec)
            norms = Counter()
            due = {}

            def stats(src3, g, waits=()):
                tiles = range(g * GT, (g + 1) * GT)
                for t in tiles:
                    own.put(dve.bn_stats(st3[:, t, :], src3[:, t, :]))
                own.settle()
                own.put(dve.memset(scratch[:, 0:1], 0.0))
                for t in tiles:
                    ins = dve.bn_aggr(mv3[:, t, :], st3[:, t, :])
                    if t < tiles[-1]:
                        own.put(ins)
                ins.then_inc(var_ready, 1)
                due[g] = norms.next()

            def normalise(dst3, src3, g, done):
                dve.wait_ge(rstd_ready, due.pop(g))
                tiles = range(g * GT, (g + 1) * GT)
                for t in tiles:
                    ins = dve.tensor_scalar(dst3[:, t, :], src3[:, t, :], mv3[:, t, 0:1], rs[:, t:t + 1], ALU.subtract, ALU.mult)
                    if t < tiles[-1]:
                        own.put(ins)
                ins.then_inc(done, 1)

            dve.wait_ge(wa_in, 16)
            dve.wait_ge(const_in, 16)
            dve.wait_ge(dt_w, 1)
            dve.tensor_copy(Wdt, bank[7][:, 0:256]).then_inc(dt_wc, 1)
            for g in range(G + 1):
                if g < G:
                    dve.wait_ge(x_in[g], 16)
                    stats(X3, g)
                if g >= 1:
                    normalise(Xn3, X3, g - 1, a_normed)
            for g in range(G):
                dve.wait_ge(bc_hi, g + 1)
                if g:
                    dve.wait_ge(bc_lo, g)
                dve.tensor_tensor(Rest[0:32, :], bank[g % 2][0:32, :], Bc[0:32, group(g)], ALU.subtract).then_inc(bc_rest, 1)
                dve.wait_ge(bc_mid, g + 1)
                dve.tensor_tensor(Bc[64:96, group(g)], Rest[0:32, :], Mid[0:32, :], ALU.subtract).then_inc(bc_lo, 1)
                for h in range(HALVES):
                    dve.wait_ge(dt_done, 2 * g + h + 1)
                    dve.tensor_scalar(Dt[:, h, group(g)], bank[6 + h][:], Wa[:, WA["b_dt"]][:, h:h + 1], None,
                                      ALU.add).then_inc(dtx_ready, 1)

            for q in range(2):
                cols = slice(q * 1024, (q + 1) * 1024)
                for h in range(HALVES):
                    dve.wait_ge(ln_ready, 2 * q + h + 1)
                    dve.wait_ge(dtx_ready, 8)
                    own.put(dve.scalar_tensor_tensor(Dt[:, h, cols], Dt[:, h, cols], 0.0, Hs[:, 0, h], ALU.max, ALU.add))
                    dve.wait_ge(log_rest, 2 * q + h + 1)
                    own.settle()
                    dve.tensor_tensor(Dt[:, h, cols], Dt[:, h, cols], Hc[:, h], ALU.add).then_inc(dt_ready, 1)
                    dve.wait_ge(dt_ready, 2 * q + h + 1)
                    dve.wait_ge(u_ready, 8)
                    dve.tensor_tensor(Dtu[:, h, cols], Dt[:, h, cols], U[:, h, cols], ALU.mult).then_inc(dtu_ready, 1)
                dve.wait_ge(dtu_ready, 2 * q + 2)
                with dve.Fori(0, NSTATE // 2) as pair:
                    for r in range(2):
                        s = pair * 2 + (q * NSTATE + r)
                        dve.wait_ge(b_rows, s + 1)
                        for h in range(HALVES):
                            dve.wait_ge(scanned, s * 2 + (h + 1))
                            dve.tensor_tensor(Dbu[:, h], Dtu[:, h, cols], psum[:, 4 * GC:6 * GC], ALU.mult).then_inc(b_used, 1)
                        for h in range(HALVES):
                            dve.wait_ge(b_used, s * 2 + (h + 1))
                            dve.wait_ge(da_ready, s * 2 + (h + 1))
                            dve.wait_ge(hc_ready, s * 2 + (h + 1))
                            dve.tensor_tensor_scan(Hs[:, r, h], Da[:, h], Dbu[:, h], 0.0, ALU.mult, ALU.add).then_inc(scanned, 1)
                dve.wait_ge(z_ready, 8)
                for h in range(HALVES):
                    dve.wait_ge(hc_used, (q + 1) * (2 * NSTATE + 2) - 1 + h)
                    zz = Z[:, h, cols]
                    dve.tensor_tensor(zz, psum[:, 2 * h * GC:2 * (h + 1) * GC], zz, ALU.mult).then_inc(y_gated, 1)
            for g in range(G):
                dve.wait_ge(y_proj, g + 1)
                dve.tensor_tensor(T1[:, group(g)], bank[4 + g % 2], Xn[:, group(g)], ALU.add).then_inc(t1_ready, 1)
                dve.wait_ge(t1_ready, g + 1)
                stats(T13, g)
                normalise(T13, T13, g, g_normed)
                dve.wait_ge(g_scaled, g + 1)
                stats(T13, g)
                normalise(T13, T13, g, o_normed)

            dve.wait_ge(tree_w, 1)
            own.put(dve.tensor_copy(Wrq, bank[7][:, 0:256]))
            dve.tensor_copy(Wlv, bank[7][:, 256:512]).then_inc(tree_wc, 1)
            for g in range(G + 1):
                if g < G:
                    dve.wait_ge(xa_ready, g + 1)
                    stats(X3, g)
                if g >= 1:
                    normalise(Bn3, X3, g - 1, b_normed)
            for g in range(G):
                tiles = slice(g * GT, (g + 1) * GT)
                dve.wait_ge(gated, 2 * g + 2)
                first = Gates[:, tiles, 0:1]
                own.put(dve.tensor_scalar(LpA[:, tiles, 0:1], first, -1.0, 1.0, ALU.mult, ALU.add))
                own.put(dve.tensor_copy(LpA[:, tiles, 1:2], first))
                own.settle()
                now, then = LpA, LpB
                for level in range(1, DEPTH):
                    n = 1 << level
                    right, left = then[:, tiles, 1:2 * n:2], then[:, tiles, 0:2 * n:2]
                    own.put(dve.tensor_tensor(right, now[:, tiles, 0:n], Gates[:, tiles, n - 1:2 * n - 1], ALU.mult))
                    own.settle()
                    ins = dve.tensor_tensor(left, now[:, tiles, 0:n], right, ALU.subtract)
                    if level < DEPTH - 1:
                        own.put(ins)
                        own.settle()
                    now, then = then, now
                ins.then_inc(leaves, 1)
            for g in range(G):
                dve.wait_ge(b_proj, g + 1)
                bias = Wb[:, WB["bias"]].unsqueeze(1).broadcast_to((P, GT, D))
                dve.tensor_tensor(T23[:, g * GT:(g + 1) * GT, :], bank[6 + g % 2][:].rearrange("p (t d) -> p t d", d=D),
                                  bias, ALU.add).then_inc(t2_ready, 1)
                dve.wait_ge(t2_ready, g + 1)
                stats(T23, g)
                if g >= 1:
                    normalise(T23, T23, g - 1, t2_normed)
            normalise(T23, T23, G - 1, t2_normed)

            for g in range(G + 1):
                if g < G:
                    dve.wait_ge(xb_ready, g + 1)
                    stats(X3, g)
                if g >= 1:
                    normalise(R3, X3, g - 1, r_new)
            dve.wait_ge(r_new, G)
            as3 = "p (m i) -> p m i"

            def layer_steps(order, turn):
                for what, part, g, ahead in order:
                    layer = (turn, ahead)
                    half = slice(g % 2 * GC, (g % 2 + 1) * GC)
                    sums, mean, var = (gst[:, g * 96 + 32 * k:g * 96 + 32 * (k + 1)] for k in range(3))
                    if what == "stats1":
                        dve.wait_ge(*r_new_in.at(layer, g))
                        stats(R3, g)
                    if what == "norm1":
                        normalise(Hn3, R3, g, c_normed.sem)
                    if what == "rotate":
                        for k in range(4):
                            dve.wait_ge(*proj.at(layer, g, k + 1))
                            if k % 2 == 0:
                                dve.wait_ge(*summed.at(layer, g - 2, k // 2 + 1))
                            dst = (Tk, Tq)[k // 2][:, k % 2, half].rearrange("p (b s) -> p b s", b=2)
                            table = Cs[:, CS[("tk", "tq")[k // 2]]].rearrange("p (a s) -> p a s", a=2)
                            dve.tensor_tensor(dst, bank[FILLS[what][k][0]].rearrange("p (b s) -> p b s", b=2),
                                              table[:, k % 2:k % 2 + 1, :].broadcast_to((P, 2, S)), ALU.mult).then_inc(rotated.sem, 1)
                    if what == "gate":
                        dve.wait_ge(*th_ready.at(layer, g))
                        dve.scalar_tensor_tensor(Sg[:, group(g)], Th[:, half], 1.0, bank[FILLS[what][0][0]], ALU.add, ALU.mult).then_inc(sg_ready.sem, 1)
                    if what == "scores":
                        dve.wait_ge(*scores.at(layer, g, part + 1))
                        if part == 0:
                            dve.wait_ge(*added.at(layer, g - 1))
                        by_query = "p (c q) -> p c q"
                        mask = Cs[:, CS["causal"]].unsqueeze(1).broadcast_to((P, 2 * PAIR, CHUNK))
                        att = Att[:, 2 * part:2 * part + 2, :].rearrange("p c n -> p (c n)").rearrange(by_query, q=CHUNK)
                        dve.tensor_tensor(att, bank[2 + part % 2].rearrange(by_query, q=CHUNK), mask, ALU.mult).then_inc(masked.sem, 1)
                    if what == "states":
                        for b in range(2):
                            dve.wait_ge(*state_done.at(layer, g, b + 1))
                            if b == 0:
                                dve.wait_ge(*added.at(layer, g - 2))
                            width = (SEQ_CHUNKS - 1) * P
                            own_block = Cs[:, CS["same_head"]].unsqueeze(1).broadcast_to((P, SEQ_CHUNKS - 1, P))
                            dve.tensor_tensor(States[:, g % 2 * 2 + b, :].rearrange("p (c f) -> p c f", f=P),
                                              bank[FILLS[what][b][0]][:, 0:width].rearrange("p (c f) -> p c f", f=P),
                                              own_block, ALU.mult).then_inc(states.sem, 1)
                    if what == "heads":
                        dve.wait_ge(*y_turned.at(layer, g))
                        own.put(dve.tensor_reduce(sums, bank[0].rearrange(as3, i=DH), AX, ALU.add))
                        own.settle()
                        own.put(dve.tensor_scalar(mean, sums, 1.0 / DH, None, ALU.mult))
                        own.settle()
                        dve.tensor_tensor(Yc[:, group(g)].rearrange(as3, i=DH), bank[0].rearrange(as3, i=DH),
                                          mean.unsqueeze(2).broadcast_to((P, 32, DH)), ALU.subtract).then_inc(centred.sem, 1)
                    if what == "var":
                        dve.wait_ge(*squared.at(layer, g))
                        own.put(dve.tensor_reduce(var, Ys.rearrange(as3, i=DH), AX, ALU.add))
                        own.settle()
                        dve.tensor_scalar(var, var, 1.0 / DH, EPS, ALU.mult, ALU.add).then_inc(var_ready, 1)
                        due["heads", g] = norms.next()
                    if what == "unit":
                        dve.wait_ge(rstd_ready, due.pop(("heads", g)))
                        y = Yc[:, group(g)].rearrange(as3, i=DH)
                        dve.tensor_tensor(y, y, var.unsqueeze(2).broadcast_to((P, 32, DH)), ALU.mult).then_inc(y_unit.sem, 1)
                    if what == "out":
                        dve.wait_ge(*wo_done.at(layer, g))
                        dve.tensor_tensor(R[:, group(g)], bank[FILLS[what][0][0]], R[:, group(g)], ALU.add).then_inc(r_mid.sem, 1)
                    if what == "stats2":
                        dve.wait_ge(*r_mid.at(layer, g))
                        stats(R3, g)
                    if what == "norm2":
                        normalise(Hn3, R3, g, f_normed.sem)
                    if what == "ffn_down":
                        dve.wait_ge(*w2_done.at(layer, g))
                        dve.tensor_tensor(R[:, group(g)], bank[FILLS[what][0][0]], R[:, group(g)], ALU.add).then_inc(r_new, 1)

            layer_steps(FIRST_FRONTS, 0)
            with dve.Fori(0, LAYERS - 1) as layer:
                assert not due
                own.enter(layer, PER_LAYER_VECTOR)
                norms.enter(layer, 3 * G)
                layer_steps(LAYER, layer)
                own.leave(LAYERS - 1)
                norms.leave(LAYERS - 1)
            assert not due
            layer_steps(LAST_TAILS, LAYERS - 1)
            for g in range(G):
                dve.wait_ge(r_new, G + LAYERS * G)
                stats(R3, g)
                if g >= 1:
                    normalise(Hn3, R3, g - 1, r_normed)
            normalise(Hn3, R3, G - 1, r_normed)

            dve.wait_ge(wd_in, 16)
            for g in range(G + 1):
                if g < G:
                    dve.wait_ge(xc_ready, g + 1)
                    stats(X3, g)
                if g >= 1:
                    normalise(Dn3, X3, g - 1, d_normed)
            by_expert = "p (t e) -> p t e"
            dve.wait_ge(gate_done, 1)
            lg3, ex3, oh3, tmp3 = (v.rearrange(by_expert, e=EXPERTS) for v in (lg, ex, oh, tmp))
            most, total, best, first = (red[:, i * T:(i + 1) * T] for i in range(4))

            def step(ins):
                own.put(ins)
                own.settle()

            def spread(v):
                return v.unsqueeze(2).broadcast_to((P, T, EXPERTS))

            step(dve.tensor_tensor(lg3, bank[2][:, 0:T * EXPERTS].rearrange(by_expert, e=EXPERTS),
                                   Wd[:, WD["bg"]].unsqueeze(1).broadcast_to((P, T, EXPERTS)), ALU.add))
            step(dve.tensor_reduce(most, lg3, AX, ALU.max))
            dve.tensor_tensor(lg3, lg3, spread(most), ALU.subtract).then_inc(shifted, 1)
            dve.wait_ge(exps, 1)
            step(dve.tensor_reduce(total, ex3, AX, ALU.add))
            step(dve.reciprocal(total, total))
            step(dve.tensor_tensor(ex3, ex3, spread(total), ALU.mult))
            step(dve.tensor_reduce(best, ex3, AX, ALU.max))
            step(dve.tensor_tensor(oh3, ex3, spread(best), ALU.is_equal))
            step(dve.tensor_tensor(tmp3, oh3, Cs[:, CS["rank"]].unsqueeze(1).broadcast_to((P, T, EXPERTS)), ALU.mult))
            step(dve.tensor_reduce(first, tmp3, AX, ALU.max))
            dve.tensor_tensor(oh3, tmp3, spread(first), ALU.is_equal).then_inc(chosen, 1)
            dve.wait_ge(chosen, 1)
            for g in range(G + 1):
                if g < G:
                    for e in range(EXPERTS + 1):
                        i = g * (EXPERTS + 1) + e
                        dve.wait_ge(expert_out, i + 1)
                        if e == 0:
                            dve.tensor_copy(T3[:, group(g)], bank[4 + i % 2][:]).then_inc(mixed, 1)
                            continue
                        dve.wait_ge(mixed, i)
                        for k in range(GT):
                            t = g * GT + k
                            ins = dve.scalar_tensor_tensor(T33[:, t, :], bank[4 + i % 2][:, tile(k)], oh3[:, t, e - 1:e],
                                                           T33[:, t, :], ALU.mult, ALU.add)
                            if k < GT - 1:
                                own.put(ins)
                        ins.then_inc(mixed, 1)
                    dve.wait_ge(mixed, (g + 1) * (EXPERTS + 1))
                    stats(T33, g)
                if g >= 1:
                    normalise(T33, T33, g - 1, t3_normed)

        @block.tensor
        def _(pe):
            def turn_tiles(dst, src3, g, width=P):
                for k in range(GT):
                    ins = pe.transpose(dst[0:width, tile(k)], src3[:, g * GT + k, :], ident)
                return ins

            def tokens(dst, rows, weights, rows_of=lambda k: tile(k), width=D):
                for k in range(GT):
                    for i, (r, w) in enumerate(zip(rows, weights)):
                        ins = pe.matmul(dst[:, k * width:(k + 1) * width], r[:, rows_of(k)], w, start=i == 0,
                                        stop=i == len(rows) - 1)
                return ins

            pe.wait_ge(wa_in, 16)
            pe.matmul(bank[7][:, 0:256], Wa[0:RANK, WA["dtin"]], Wa[0:RANK, WA["dtw"]], start=True, stop=True).then_inc(dt_w, 1)
            pe.wait_ge(const_in, 16)
            pe.wait_ge(conv_w, 1)
            pe.wait_ge(dt_wc, 1)
            pe.wait_ge(pads, 2)
            for g in range(G):
                pe.wait_ge(a_normed, g + 1)
                if g >= 2:
                    pe.wait_ge(bc_rest, g - 1)
                turn_tiles(bank[g % 2], Xn3, g).then_inc(a_turned, 1)
                pe.wait_ge(a_rows, g + 1)
                seqs = slice(2 * g, 2 * g + 2)
                for h in range(HALVES):
                    if g:
                        pe.wait_ge(u_ready, 2 * (g - 1) + h + 1)
                    for k in range(TAPS):
                        ins = pe.matmul(bank[2 + h][:], Wk[:, k, tile(h)], Xt3[:, seqs, k:k + S], start=k == 0, stop=k == TAPS - 1)
                    ins.then_inc(conv_done, 1)
                rows = Xt3[:, seqs, TAPS - 1:]
                for h in range(HALVES):
                    if g:
                        pe.wait_ge(z_ready, 2 * (g - 1) + h + 1)
                    pe.matmul(bank[4 + h][:], Wa[:, WA["z"]][:, tile(h)], rows, start=True, stop=True).then_inc(z_done, 1)
                pe.matmul(bank[g % 2][0:32, :], Wa[:, WA["bc"]], rows, start=True, stop=True).then_inc(bc_done, 1)
                for h in range(HALVES):
                    if g:
                        pe.wait_ge(dtx_ready, 2 * (g - 1) + h + 1)
                    pe.matmul(bank[6 + h][:], Wdt[:, tile(h)], rows, start=True, stop=True).then_inc(dt_done, 1)

            pe.wait_ge(sel_in, 16)
            pe.wait_ge(d_diag, HALVES)
            pe.wait_ge(dtx_ready, 8)
            for q in range(2):
                def rows_of_state(first_bank, row, done):
                    for c in range(2):
                        ins = pe.matmul(bank[first_bank + c][:], Sel[:, bass.ds(row * P, P)], Bc[:, group(2 * q + c)],
                                        start=True, stop=True)
                    ins.then_inc(done, 1)

                def add_state(h):
                    for c in range(2):
                        ins = pe.matmul(bank[2 * h + c][:], ident, Hc[:, h, group(c)], start=False, stop=False,
                                        skip_group_check=True)
                    return ins

                pe.wait_ge(u_ready, 8)
                pe.wait_ge(bc_ready, G)
                pe.wait_ge(bc_lo, G)
                for h in range(HALVES):
                    if q:
                        pe.wait_ge(y_gated, h + 1)
                    for c in range(2):
                        ins = pe.matmul(bank[2 * h + c], DiagD[:, tile(h)], U[:, h, group(2 * q + c)], start=True,
                                        stop=False, skip_group_check=True)
                    ins.then_inc(hc_used, 1)
                if q:
                    pe.wait_ge(b_used, 2 * NSTATE)
                rows_of_state(4, 0, b_rows)
                if q:
                    pe.wait_ge(c_copied, NSTATE)
                rows_of_state(6, NSTATE, c_rows)
                base = q * NSTATE
                with pe.Fori(0, NSTATE - 1) as n:
                    pe.wait_ge(b_used, n * 2 + (2 * base + 2))
                    rows_of_state(4, n + 1, b_rows)
                    pe.wait_ge(c_copied, n + (base + 1))
                    rows_of_state(6, n + (1 + NSTATE), c_rows)
                    for h in range(HALVES):
                        pe.wait_ge(hc_ready, n * 2 + (2 * base + 5 + h))
                        add_state(h).then_inc(hc_used, 1)
                for h in range(HALVES):
                    pe.wait_ge(hc_ready, 2 * base + 2 * NSTATE + 3 + h)
                    add_state(h).then_inc(hc_used, 1)
            pe.wait_ge(y_gated, 4)
            for g in range(G):
                if g >= 2:
                    pe.wait_ge(t1_ready, g - 1)
                tokens(bank[4 + g % 2], [Z[:, h, group(g)] for h in range(HALVES)],
                       [Wa[:, WA["out"]][:, tile(h)] for h in range(HALVES)]).then_inc(y_proj, 1)

            pe.wait_ge(wb_in, 16)
            pe.wait_ge(t1_ready, G)
            pe.matmul(bank[7][:, 0:256], Wb[:, WB["q"]], Wb[:, WB["routers"]], start=True, stop=True)
            for h in range(2):
                ins = pe.matmul(bank[7][:, 256 + h * P:256 + (h + 1) * P], Wb[:, WB["values"]][:, tile(h)], Wb[:, WB["wout"]],
                                start=True, stop=True)
            ins.then_inc(tree_w, 1)
            for g in range(G):
                pe.wait_ge(b_normed, g + 1)
                if g >= 2:
                    pe.wait_ge(b_rows_t, g - 1)
                turn_tiles(bank[g % 2], Bn3, g).then_inc(b_turned, 1)
            pe.wait_ge(tree_wc, 1)
            for g in range(G):
                pe.wait_ge(b_rows_t, g + 1)
                for k in range(GT):
                    t = g * GT + k
                    if k % 2 == 0 and t >= 4:
                        pe.wait_ge(gated, t // 2 - 1)
                    ins = pe.matmul(bank[2 + t // 2 % 2][:, (k % 2) * LEAVES:(k % 2 + 1) * LEAVES], Bt[:, tile(t)], Wrq,
                                    start=True, stop=True)
                    if k % 2:
                        ins.then_inc(logits, 1)
            for g in range(G):
                pe.wait_ge(leaves, g + 1)
                for h in range(2):
                    if g:
                        pe.wait_ge(lp_rows, 2 * (g - 1) + h + 1)
                    for k in range(GT):
                        ins = pe.transpose(bank[4 + h][:, tile(k)], LpB[:, g * GT + k, tile(h)], ident)
                    ins.then_inc(lp_turned, 1)
                pe.wait_ge(lp_rows, 2 * g + 2)
                if g >= 2:
                    pe.wait_ge(t2_ready, g - 1)
                tokens(bank[6 + g % 2], [LpT[:, g, h, :] for h in range(2)], [Wlv[:, tile(h)] for h in range(2)]).then_inc(b_proj, 1)

            held = {}

            def claim(what, i, layer, g):
                b, reader, k = FILLS[what][i]
                for event, of, at_group, nth in held.get(b, ()):
                    pe.wait_ge(*event.at(of, at_group, nth))
                held[b] = [(reader, layer, g, k)]
                return bank[b]

            def last_fills(order, turn, shift):
                return {b: (reader, (turn, ahead + shift), g, k) for what, _, g, ahead in order for b, reader, k in FILLS.get(what, ())}

            def layer_steps(order, turn):
                for what, part, g, ahead in order:
                    layer = (turn, ahead)
                    half = slice(g % 2 * GC, (g % 2 + 1) * GC)
                    chunk0, seq0 = g % 2 * CHUNKS, g % 2 * 2
                    if what == "turn1":
                        pe.wait_ge(*c_normed.at(layer, g))
                        turn_tiles(claim(what, 0, layer, g), Hn3, g).then_inc(c_turned.sem, 1)
                    if what == "rotate":
                        pe.wait_ge(*hn_rows.at(layer, g))
                        if g == 0:
                            pe.wait_ge(qkvg_in, turn * 16 + 16 * (ahead + 1))
                        for k in range(4):
                            pe.matmul(claim(what, k, layer, g), Wl[:, WL["qk"]][:, tile(k)], Ht[:, group(g)], start=True,
                                      stop=True).then_inc(proj.sem, 1)
                    if what == "values":
                        dst = claim(what, 0, layer, g)
                        for c in range(CHUNKS):
                            for a in range(PARITY):
                                cols = slice(g * GC + c * CHUNK, g * GC + (c + 1) * CHUNK)
                                ins = pe.matmul(dst[a * CHUNK:(a + 1) * CHUNK, c * CHUNK:(c + 1) * CHUNK], Ht[:, cols],
                                                Wl[:, WL["v"]][:, a * (D // 2):(a + 1) * (D // 2)], start=True, stop=True)
                        ins.then_inc(v_done.sem, 1)
                    if what == "gate":
                        tokens(claim(what, 0, layer, g), [Ht[:, group(g)]], [Wl[:, WL["g"]]]).then_inc(g_done.sem, 1)
                    if what == "keys":
                        pe.wait_ge(*k_spread.at(layer, g))
                        for b in range(2):
                            dst = claim(what, b, layer, g)
                            for c in range(SEQ_CHUNKS - 1):
                                ins = pe.transpose(dst[:, tile(c)], Ka[:, chunk0 + b * SEQ_CHUNKS + c, :], ident)
                            ins.then_inc(k_turned.sem, 1)
                    if what == "scores":
                        if part == 0:
                            pe.wait_ge(*q_spread.at(layer, g))
                        pe.wait_ge(*masked.at(layer, g, part - 1))
                        for c in range(2):
                            i = chunk0 + 2 * part + c
                            ins = pe.matmul(bank[2 + part % 2][:, c * 256:(c + 1) * 256], Ka[:, i, :], Qp[:, i, :], start=True, stop=True)
                        ins.then_inc(scores.sem, 1)
                    if what == "states":
                        pe.wait_ge(*v_ready.at(layer, g))
                        for b in range(2):
                            pe.wait_ge(*k_tokens.at(layer, g, b + 1))
                            dst = claim(what, b, layer, g)
                            for c in range(SEQ_CHUNKS - 1):
                                ins = pe.matmul(dst[:, tile(c)], Kt[:, seq0 + b, tile(c)], Va[:, chunk0 + b * SEQ_CHUNKS + c, :],
                                                start=True, stop=True)
                            ins.then_inc(state_done.sem, 1)
                    if what == "mix":
                        pe.wait_ge(*yt_rows.at(layer, g - 2))
                        for b in range(2):
                            y = bank[6 + g % 2][:, b * S:(b + 1) * S]
                            pe.wait_ge(*states.at(layer, g, b + 1))
                            for c in range(SEQ_CHUNKS - 1):
                                later = slice((c + 1) * CHUNK, S)
                                pe.matmul(y[:, later], States[:, seq0 + b, tile(c)], Qr[:, half][:, b * S:(b + 1) * S][:, later],
                                          start=b == c == 0, stop=False, skip_group_check=True)
                            pe.wait_ge(*masked.at(layer, g, 2 * b + 2))
                            for c in range(SEQ_CHUNKS):
                                for j in range(PAIR):
                                    rows = slice(2 * DH * j, 2 * DH * (j + 1))
                                    ins = pe.matmul(y[rows, c * CHUNK:(c + 1) * CHUNK], Va[:, chunk0 + b * SEQ_CHUNKS + c, rows],
                                                    Att[:, b * SEQ_CHUNKS + c, j * CHUNK:(j + 1) * CHUNK], start=False,
                                                    stop=True, skip_group_check=True)
                        ins.then_inc(added.sem, 1)
                    if what == "heads":
                        pe.wait_ge(*yt_rows.at(layer, g))
                        dst = claim(what, 0, layer, g)
                        for k in range(GT):
                            ins = pe.transpose(dst[:, tile(k)], Yt[:, half][:, tile(k)], ident)
                        ins.then_inc(y_turned.sem, 1)
                    if what == "out_turn":
                        pe.wait_ge(*gy_ready.at(layer, g))
                        turn_tiles(claim(what, 0, layer, g), Yc.rearrange("p (t d) -> p t d", d=D), g).then_inc(gy_turned.sem, 1)
                    if what == "out":
                        pe.wait_ge(*gy_rows.at(layer, g))
                        if g == 0:
                            pe.wait_ge(out_in, turn * 16 + 16 * (ahead + 1))
                        tokens(claim(what, 0, layer, g), [Gyt[:, half]], [Wl[:, WL["wo"]]]).then_inc(wo_done.sem, 1)
                    if what == "ffn_turn":
                        pe.wait_ge(*f_normed.at(layer, g))
                        turn_tiles(claim(what, 0, layer, g), Hn3, g).then_inc(f_turned.sem, 1)
                    if what == "ffn_up":
                        if g == 0:
                            pe.wait_ge(ffn_in, turn * 16 + 16 * (ahead + 1))
                        pe.wait_ge(*f_rows.at(layer, g))
                        for k in range(2):
                            pe.matmul(claim(what, k, layer, g), Wl[:, WL["w1"]][:, tile(k)], Ht[:, group(g)], start=True,
                                      stop=True).then_inc(w1_done.sem, 1)
                    if what == "ffn_down":
                        pe.wait_ge(*gelu_ready.at(layer, g))
                        tokens(claim(what, 0, layer, g), [Ft[:, group(2 * (g % 2) + j)] for j in range(2)],
                               [Wl[:, WL["w2"]][:, tile(j)] for j in range(2)]).then_inc(w2_done.sem, 1)

            pe.wait_ge(xb_ready, G)
            layer_steps(FIRST_FRONTS, 0)
            with pe.Fori(0, LAYERS - 1) as layer:
                before, first = last_fills(LAYER, layer, -1), last_fills(FIRST_FRONTS, layer, 0)
                for b in before:
                    held[b] = [before[b]] + ([first[b]] if b in first and first[b][1:] != before[b][1:] else [])
                layer_steps(LAYER, layer)
            held.update({b: [e] for b, e in last_fills(LAYER, LAYERS - 2, 0).items()})
            layer_steps(LAST_TAILS, LAYERS - 1)

            pe.wait_ge(wd_in, 16)
            for g in range(G):
                pe.wait_ge(d_normed, g + 1)
                if g >= 2:
                    pe.wait_ge(d_rows, g - 1)
                turn_tiles(bank[g % 2], Dn3, g).then_inc(d_turned, 1)
            for g in range(G):
                pe.wait_ge(d_rows, g + 1)
                for k in range(GT):
                    t = g * GT + k
                    ins = pe.matmul(bank[2][:, t * EXPERTS:(t + 1) * EXPERTS], Dtr[:, tile(t)], Wd[:, WD["gate"]], start=True, stop=True)
            ins.then_inc(gate_done, 1)
            pe.wait_ge(chosen, 1)
            for g in range(G):
                if g >= 2:
                    pe.wait_ge(oh_rows, g - 1)
                for k in range(GT):
                    ins = pe.transpose(bank[g % 2][0:EXPERTS, tile(k)], oh[:, (g * GT + k) * EXPERTS:(g * GT + k + 1) * EXPERTS], ident)
                ins.then_inc(oh_turned, 1)

            def second(j):
                g, e = divmod(j, EXPERTS + 1)
                if j >= 2:
                    pe.wait_ge(mixed, j - 1)
                if e == 0:
                    pe.wait_ge(oh_rows, g + 1)
                    tokens(bank[4 + j % 2], [Oht[0:EXPERTS, group(g)]], [Wd[0:EXPERTS, WD["b2"]]]).then_inc(expert_out, 1)
                    return
                i = g * EXPERTS + e - 1
                pe.wait_ge(h_ready, i + 1)
                tokens(bank[4 + j % 2], [Hid[:, group(i % 2)]], [Wd[:, WD["w2"]][:, tile(e - 1)]]).then_inc(expert_out, 1)

            for g in range(G):
                for e in range(EXPERTS):
                    i = g * EXPERTS + e
                    if i >= 2:
                        pe.wait_ge(h_ready, i - 1)
                    pe.matmul(bank[2 + i % 2][:], Wd[:, WD["w1"]][:, tile(e)], Dtr[:, group(g)], start=True, stop=True).then_inc(hidden, 1)
                    if e == 0:
                        if g:
                            second(g * (EXPERTS + 1) - 1)
                        second(g * (EXPERTS + 1))
                    else:
                        second(g * (EXPERTS + 1) + e)
            second(G * (EXPERTS + 1) - 1)


def _pack(width, where, parts):
    out = np.zeros((P, width), np.float32)
    for name, a in parts.items():
        a = a.reshape(a.shape[0], -1)
        out[: a.shape[0], where[name].start : where[name].start + a.shape[1]] = a
    return out


def _columns(v):
    return np.ascontiguousarray(v.reshape(-1, P).T)


def _everywhere(v):
    return np.broadcast_to(v.reshape(1, -1), (P, v.size))


def _rotated(w):
    return np.concatenate([w, w.reshape(D, D // 2, 2)[..., ::-1].reshape(D, D)], 1)


def kernel(**inputs):
    import concourse.bacc as _bacc
    import ml_dtypes
    from concourse.bass_utils import run_bass_kernel_spmd as _run

    a = {k: np.asarray(v) for k, v in inputs.items()}
    win = a["L0_attn_W_in"]
    alog = a["L0_attn_A_log"].reshape(HALVES, P, NSTATE).transpose(1, 0, 2)
    taps = a["L0_attn_conv_w"][:, 0, :].T
    wa = _pack(WA_W, WA, {
        "x": win[:256].T, "z": win[256:512].T, "bc": win[512:544].T, "dtin": win[544:552],
        "dtw": a["L0_attn_W_dt"].T, "tap": _everywhere(taps), "out": a["L0_attn_W_out"].T.reshape(HALVES, P, D).transpose(1, 0, 2),
        "conv_b": _columns(a["L0_attn_conv_b"]), "b_dt": _columns(a["L0_attn_b_dt"]), "alog": alog,
        "dskip": _columns(a["L0_attn_D"]), "ln_g": _everywhere(a["L0_attn_ln_g"]), "ln_b": _everywhere(a["L0_attn_ln_b"])})
    wb = _pack(WB_W, WB, {
        "q": a["L0_ffn_Wq"], "routers": a["L0_ffn_routers"].T, "values": a["L0_ffn_leaf_values"].T,
        "wout": a["L0_ffn_Wout_w"].T, "bias": _everywhere(a["L0_ffn_Wout_b"])})
    wl = np.stack([_pack(WL_W, WL, {
        "qk": np.concatenate([_rotated(a["L1_attn_Wk"][i]), _rotated(a["L1_attn_Wq"][i])], 1),
        "v": a["L1_attn_Wv"][i].reshape(D, PAIR, PARITY, DH).transpose(0, 2, 1, 3), "g": a["L1_attn_Wg"][i], "wo": a["L1_attn_Wo"][i],
        "gn": np.concatenate([_everywhere(a["L1_attn_gn_scale"][i]), _everywhere(a["L1_attn_gn_bias"][i])], 1),
        "w1": a["L1_attn_W1"][i], "w2": a["L1_attn_W2"][i].reshape(2, P, D).transpose(1, 0, 2)})
        for i in range(LAYERS)])
    wd = _pack(WD_W, WD, {
        "w1": a["L1_ffn_W1"].transpose(1, 0, 2), "w2": a["L1_ffn_W2"].transpose(1, 0, 2), "b1": a["L1_ffn_b1"].T,
        "gate": a["L1_ffn_Wg"], "bg": _everywhere(a["L1_ffn_bg"]), "b2": a["L1_ffn_b2"]})
    lnc = np.stack([a["L1_attn_ln_scale"], a["L1_attn_ln_bias"]], 1)
    arrays = {"x": a["L0_attn_x"], "wa": wa, "wb": wb, "wl": wl, "wd": wd, "lnc": lnc, "const": constants(),
              "sel": selectors().astype(ml_dtypes.bfloat16)}
    nc = _bacc.Bacc("TRN2", target_bir_lowering=False, num_devices=1)
    named = {}
    for name, v in arrays.items():
        arrays[name] = v = np.ascontiguousarray(v)
        named[name] = nc.dram_tensor(name, v.shape, mybir.dt.from_np(v.dtype), kind="ExternalInput").ap()
    out = nc.dram_tensor("out", (B, S, D), F32, kind="ExternalOutput").ap()
    four_blocks(nc, out=out, **named)
    r = _run(nc, [arrays], core_ids=[0])
    return r.results[0]["out"]
```

```python
from contextlib import ExitStack

import numpy as np

import concourse.bass as bass
from concourse import mybir

F32 = mybir.dt.float32
BF16 = mybir.dt.bfloat16
ALU = mybir.AluOpType
ACT = mybir.ActivationFunctionType
AX = mybir.AxisListType.X

P = 128
D = 128
B, S = 8, 256
T = B * S // P
G = 4
GT = T // G
GC = GT * P
EPS = 1e-5
NSTATE = 16
HALVES = 2
TAPS = 4
RANK = 8
DEPTH = 8
LEAVES = 1 << DEPTH
LOW_LEVELS = 5
LAYERS = 4
HEADS, DH = 8, 16
CHUNK = 64
CHUNKS = GC // CHUNK
SEQ_CHUNKS = S // CHUNK
PARITY, PAIR = 2, 4
EXPERTS = 8


def offsets(*parts):
    at, out = 0, {}
    for name, width in parts:
        out[name] = slice(at, at + width)
        at += width
    return out, at


WA, WA_W = offsets(("x", 256), ("z", 256), ("bc", 32), ("dtin", P), ("dtw", 256), ("tap", TAPS * 256),
                   ("out", 256), ("conv_b", 2), ("b_dt", 2), ("alog", 2 * NSTATE), ("dskip", 2),
                   ("ln_g", D), ("ln_b", D))
WB, WB_W = offsets(("q", D), ("routers", LEAVES), ("values", LEAVES), ("wout", D), ("bias", D))
WD, WD_W = offsets(("w1", EXPERTS * D), ("w2", EXPERTS * D), ("b1", EXPERTS), ("gate", EXPERTS),
                   ("bg", EXPERTS), ("b2", D))
WL, WL_W = offsets(("qk", 4 * P), ("v", P), ("g", P), ("wo", P), ("gn", 2 * P), ("w1", 2 * P), ("w2", 2 * P))
CS, CS_W = offsets(("ident", P), ("causal", CHUNK), ("same_head", P), ("parity", PARITY), ("pair", PAIR),
                   ("tq", 2 * S), ("tk", 2 * S), ("rank", EXPERTS))
PER_LAYER_VECTOR = 2 * G * (3 * GT - 1) + 3 * G
PER_LAYER_SCALAR = G * (1 + (PARITY - 1) + (PAIR - 1))
PER_LAYER_POOL = 2 * G + 2 * G


def constants():
    c = np.zeros((P, CS_W), np.float32)
    c[:, CS["ident"]] = np.eye(P)
    k = np.arange(P)
    c[:, CS["causal"]] = np.arange(CHUNK)[None] >= k[:, None] % CHUNK
    c[:, CS["same_head"]] = k[:, None] // DH == k[None] // DH
    c[:, CS["parity"]] = k[:, None] // DH % 2 == np.arange(PARITY)
    c[:, CS["pair"]] = k[:, None] // (2 * DH) == np.arange(PAIR)
    pos = np.arange(S, dtype=np.float32)
    freq = (1.0 / 10000.0 ** (np.arange(0, DH, 2, dtype=np.float32) / DH)).astype(np.float32)
    ang = (pos[:, None] * freq[None]).astype(np.float64)
    decay = 1.0 - np.exp(np.linspace(np.log(1 / 32), np.log(1 / 64), HEADS)).astype(np.float32)
    decay = np.log(decay.astype(np.float32)).astype(np.float64)
    tq, tk = np.zeros((P, 2, S)), np.zeros((P, 2, S))
    for row in range(P):
        h, i = divmod(row, DH)
        grow = np.exp(np.arange(S) * decay[h])
        cos, sin = np.cos(ang[:, i // 2]), np.sin(ang[:, i // 2]) * (-1 if i % 2 == 0 else 1)
        tq[row, 0], tq[row, 1] = cos * grow, sin * grow
        tk[row, 0], tk[row, 1] = cos / grow, -sin / grow
    c[:, CS["tq"]] = tq.reshape(P, -1)
    c[:, CS["tk"]] = tk.reshape(P, -1)
    c[:, CS["rank"]] = np.arange(EXPERTS, 0, -1)
    return c


def selectors():
    sel = np.zeros((P, 2 * NSTATE, P), np.float32)
    for s in range(2 * NSTATE):
        for part in range(3):
            sel[s + 32 * part, s] = 1.0
    return sel.reshape(P, -1)


class Steps:

    def __init__(self, eng, sem):
        self.eng, self.sem, self.n, self.turns = eng, sem, 0, None

    def put(self, ins):
        ins.then_inc(self.sem, 1)
        self.n += 1

    def settle(self):
        self.eng.wait_ge(self.sem, self.n if self.turns is None else self.turns + self.n)

    def enter(self, turn, per):
        self.start, self.per = self.n, per
        self.turns, self.n = turn * per + self.n, 0

    def leave(self, turns):
        assert self.n == self.per, (self.n, self.per)
        self.turns, self.n = None, self.start + turns * self.per


class Counter:

    def __init__(self):
        self.n, self.turns = 0, None

    def next(self):
        self.n += 1
        return self.n if self.turns is None else self.turns + self.n

    def enter(self, turn, per):
        self.start, self.per = self.n, per
        self.turns, self.n = turn * per + self.n, 0

    def leave(self, turns):
        assert self.n == self.per, (self.n, self.per)
        self.turns, self.n = None, self.start + turns * self.per


class PerGroup:

    def __init__(self, sem, per, primed):
        self.sem, self.per, self.primed = sem, per, primed

    def at(self, layer, g, k=None):
        turn, ahead = layer
        const = (ahead + self.primed) * self.per * G + self.per * g + (self.per if k is None else k)
        if isinstance(turn, int):
            const += turn * self.per * G
        assert const > 0
        return self.sem, const if isinstance(turn, int) else turn * (self.per * G) + const


SCHEDULE = (
    (0.292, "stats1", 0), (0.531, "norm1", 0), (0.641, "turn1", 0), (0.845, "rotate", 0), (0.931, "spread", 0),
    (1.158, "spread", 1), (1.301, "keys", 0), (1.474, "scores", 0), (1.522, "values", 0), (1.601, "scores", 1),
    (1.655, "gate", 0), (1.693, "scores", 2), (1.771, "states", 0), (1.831, "scores", 3), (1.937, "mix", 0),
    (1.933, "gather", 0), (2.152, "heads", 0), (2.360, "square", 0), (2.578, "var", 0), (2.970, "unit", 0),
    (3.180, "scale", 0), (3.323, "out_turn", 0), (3.494, "out", 0), (3.533, "stats2", 0), (3.645, "norm2", 0),
    (3.843, "ffn_turn", 0), (4.043, "ffn_up", 0), (4.211, "ffn_down", 0),)


def layer_order():
    placed = sorted(((g + t) % G, g + t, what, k, g) for g in range(G) for t, what, k in SCHEDULE)
    return [(what, k, g, int(at < G)) for _, at, what, k, g in placed]


LAYER = layer_order()

TREE_SCHEDULE = (
    (-0.363, "y_proj"), (1.902, "t1"), (4.537, "g_norm"), (4.577, "g_stats"), (5.451, "o_norm"), (6.325, "b_stats"),
    (6.568, "b_norm"), (7.126, "b_turn"), (7.946, "logits"), (7.780, "low_levels"), (8.920, "levels"), (9.756, "lp"),
    (10.296, "b_proj"), (11.612, "t2_stats"), (11.986, "t2_norm"), (12.840, "rx_stats"), (12.992, "rx_norm"),)
FIRST_STEPS_AT, FIRST_STEPS_SCALE = 13.25, 1.00
TREE_STEPS = {what for _, what in TREE_SCHEDULE}
OPENING = [(what, k, g, 0) for _, what, k, g in sorted(
    [(g + t, what, 0, g) for g in range(G) for t, what in TREE_SCHEDULE]
    + [(FIRST_STEPS_AT + FIRST_STEPS_SCALE * (g + t), what, k, g) for g in range(G) for t, what, k in SCHEDULE if g + t < G])]

POWERS = [(what, g) for what, _, g, _ in OPENING
           if what in ("t1", "g_stats", "b_stats", "t2_stats", "rx_stats", "stats1", "stats2", "var")]
POWER_OF = {(norm, g): G + 1 + POWERS.index((what, g)) for g in range(G) for what, norm in (
    ("g_stats", "o_norm"), ("b_stats", "b_norm"), ("t2_stats", "t2_norm"), ("rx_stats", "rx_norm"))}

EXPERT_SCHEDULE = (
    (4.336, "r_stats", 0), (4.723, "r_norm", 0), (4.959, "x_stats", 0), (5.016, "x_norm", 0), (5.195, "d_turn", 0),
    (5.277, "logits", 0), (5.281, "exps", 0), (5.282, "choose", 0), (5.619, "oh_turn", 0), (5.819, "expert", 0),
    (6.993, "t_stats", 0), (7.172, "t_norm", 0),
    ) + tuple((5.529 + 0.109 * e, "hidden", e) for e in range(EXPERTS)) + tuple(
    (5.819 + 0.103 * e, "expert", e + 1) for e in range(EXPERTS))
LAST_TAILS = [(g + t, what, k, g) for g in range(G) for t, what, k in SCHEDULE if g + t >= G]
ENDING = [(what, k, g, 0) for _, what, k, g in sorted(
    LAST_TAILS + [(g + t, what, k, g) for g in range(G) for t, what, k in EXPERT_SCHEDULE])]
EXPERT_STEPS = {what for _, what, _ in EXPERT_SCHEDULE}
HIDDEN = [(g, k) for what, k, g, _ in ENDING if what == "hidden"]
RESULTS = [(g, k) for what, k, g, _ in ENDING if what == "expert"]
HIDDEN_SLOTS = 4


def four_blocks(nc, x, wa, wb, wl, wd, lnc, const, sel, out):
    with ExitStack() as ctx:
        def sbuf(name, width, dtype=F32):
            return ctx.enter_context(nc.sbuf_tensor(name, [P, width], dtype))

        def sem(name):
            return ctx.enter_context(nc.semaphore(name))

        X = sbuf("X", T * D)
        Wa, Wb, Wl, Wd = sbuf("Wa", WA_W), sbuf("Wb", WB_W), sbuf("Wl", WL_W), sbuf("Wd", WD_W)
        Cs = sbuf("Cs", CS_W)
        Sel = sbuf("Sel", 2 * NSTATE * P, BF16)
        st, mv = sbuf("st", T * 6), sbuf("mv", T * 2)
        ve, rs = sbuf("ve", T), sbuf("rs", T)
        shift = sbuf("shift", T)
        mhalf = sbuf("mhalf", 32)
        eps, zeros, ones = sbuf("eps", GT), sbuf("zeros", GT), sbuf("ones", GT)
        Wrq, Wlv = sbuf("Wrq", LEAVES)[:], sbuf("Wlv", 2 * D)[:]
        Lnc = sbuf("Lnc", 2)
        scratch = sbuf("scratch", 32)
        ident = Cs[:, CS["ident"]]
        st3, mv3 = st[:].rearrange("p (t s) -> p t s", s=6), mv[:].rearrange("p (t s) -> p t s", s=2)
        X3 = X[:].rearrange("p (t d) -> p t d", d=D)
        psum = ctx.enter_context(nc.psum_tensor("psum", [P, 8 * GC], F32))
        bank = [psum[:, i * GC:(i + 1) * GC] for i in range(8)]

        ARENA = 37400
        arena = sbuf("arena", ARENA)
        top = [0]

        def take(width):
            top[0] += width
            assert top[0] <= ARENA, top[0]
            return arena[:, top[0] - width:top[0]]

        Xn = take(T * D)
        T1 = take(T * D)
        Z = take(HALVES * 2048).rearrange("p (h c) -> p h c", h=HALVES)
        tree_top = top[0]
        Xt = take(B * (S + TAPS - 1))
        Xt3 = Xt.rearrange("p (b s) -> p b s", b=B)
        U = take(HALVES * 2048).rearrange("p (h c) -> p h c", h=HALVES)
        Dt = take(HALVES * 2048).rearrange("p (h c) -> p h c", h=HALVES)
        Dtu = take(HALVES * 2048).rearrange("p (h c) -> p h c", h=HALVES)
        Da = take(HALVES * 1024).rearrange("p (h c) -> p h c", h=HALVES)
        Dbu = take(HALVES * 1024).rearrange("p (h c) -> p h c", h=HALVES)
        Hs = take(2 * HALVES * 1024).rearrange("p (r h c) -> p r h c", r=2, h=HALVES)
        Hc = take(HALVES * 1024).rearrange("p (h c) -> p h c", h=HALVES)
        Bc = take(1024).bitcast(BF16)
        Rest, Mid = take(GC), take(GC // 2).bitcast(BF16)
        Crows = take(2 * 1024).rearrange("p (r c) -> p r c", r=2)
        Wk = Crows[:, 0, :].rearrange("p (k c) -> p k c", k=TAPS)
        Wdt, DiagD, Aneg = take(256), take(256), take(2 * NSTATE)
        T13 = T1.rearrange("p (t d) -> p t d", d=D)
        Xn3 = Xn.rearrange("p (t d) -> p t d", d=D)

        top[0] = tree_top
        Bn, T2 = Xn, T1
        Bt = take(T * D)
        Gates = take(T * LEAVES).rearrange("p (t n) -> p t n", t=T)
        LpA = take(T * LEAVES).rearrange("p (t n) -> p t n", t=T)
        LpB = take(T * LEAVES).rearrange("p (t n) -> p t n", t=T)
        LpT = take(G * 2 * GC).rearrange("p (g h c) -> p g h c", g=G, h=2)
        Bn3, T23 = Bn.rearrange("p (t d) -> p t d", d=D), T2.rearrange("p (t d) -> p t d", d=D)

        top[0] = 0
        R, Hn, Ht = take(T * D), take(T * D), take(T * D)
        Kt = take(4 * (SEQ_CHUNKS - 1) * P).rearrange("p (b n) -> p b n", b=4)
        States = take(4 * (SEQ_CHUNKS - 1) * P).rearrange("p (b n) -> p b n", b=4)
        Th, Yt, Gyt = take(2 * GC), take(2 * GC), take(2 * GC)
        Ft = take(2 * 2 * GC)
        Sg = take(T * D)
        Att = take(CHUNKS * PAIR * CHUNK).rearrange("p (c n) -> p c n", n=PAIR * CHUNK)
        Yc, Ys = take(T * D), take(GC)
        gst = take(G * 96)
        Qp = take(2 * CHUNKS * PAIR * CHUNK).rearrange("p (c n) -> p c n", n=PAIR * CHUNK)
        Ka = take(2 * CHUNKS * P).rearrange("p (c n) -> p c n", n=P)
        Qr, Kr = take(2 * GC), take(2 * GC)
        Tq = take(2 * 2 * GC).rearrange("p (a c) -> p a c", a=2)
        Tk = take(2 * 2 * GC).rearrange("p (a c) -> p a c", a=2)
        Va = take(2 * CHUNKS * P).rearrange("p (c n) -> p c n", n=P)
        R3, Hn3 = R.rearrange("p (t d) -> p t d", d=D), Hn.rearrange("p (t d) -> p t d", d=D)

        Dn3, Dtr, T3, T33 = Hn3, Ht, R, R3
        Hid = Att.rearrange("p c n -> p (c n)")
        Oht = Tk.rearrange("p a c -> p (a c)")
        lg, ex, oh, tmp = take(T * EXPERTS), take(T * EXPERTS), take(T * EXPERTS), take(T * EXPERTS)
        red = take(4 * T)

        x_in = [sem(f"x_in{g}") for g in range(G)]
        wa_in, wb_in, wd_in = sem("wa_in"), sem("wb_in"), sem("wd_in")
        ident_in, const_in, sel_in, lnc_in, stored = sem("ident_in"), sem("const_in"), sem("sel_in"), sem("lnc_in"), sem("stored")
        qkvg_in, out_in, ffn_in = sem("qkvg_in"), sem("out_in"), sem("ffn_in")
        vec, pol, act_steps = sem("vector_steps"), sem("pool_steps"), sem("scalar_steps")
        var_ready, rstd_ready = sem("var_ready"), sem("rstd_ready")
        conv_w, dt_w, dt_wc, a_neg, d_diag = sem("conv_w"), sem("dt_w"), sem("dt_w_copied"), sem("a_neg"), sem("d_diag")
        pads = sem("pads")
        a_normed, a_turned, a_rows = sem("a_normed"), sem("a_turned"), sem("a_rows")
        conv_done, z_done, bc_done, dt_done = sem("conv_done"), sem("z_done"), sem("bc_done"), sem("dt_done")
        u_ready, z_ready, bc_hi, bc_rest, bc_mid, bc_lo, bc_ready = (
            sem("u_ready"), sem("z_ready"), sem("bc_hi"), sem("bc_rest"), sem("bc_mid"), sem("bc_lo"), sem("bc_ready"))
        dtx_ready, exp_ready, rounded, ln_ready, log_rest, dt_ready, dtu_ready = (
            sem("dtx_ready"), sem("exp_ready"), sem("rounded"), sem("ln_ready"), sem("log_rest"), sem("dt_ready"),
            sem("dtu_ready"))
        b_rows, b_used, c_rows, c_copied = sem("b_rows"), sem("b_used"), sem("c_rows"), sem("c_copied")
        da_ready, scanned, hc_ready, hc_used = sem("da_ready"), sem("scanned"), sem("hc_ready"), sem("hc_used")
        y_gated, y_proj, t1_ready = sem("y_gated"), sem("y_proj"), sem("t1_ready")
        g_scaled, o_normed, xa_ready = sem("g_scaled"), sem("o_normed"), sem("xa_ready")
        tree_w, tree_wc = sem("tree_w"), sem("tree_w_copied")
        b_normed, b_turned, b_rows_t, logits, gated, low_ready, leaves = (
            sem("b_normed"), sem("b_turned"), sem("b_rows_turned"), sem("logits"), sem("gated"), sem("low_ready"), sem("leaves"))
        lp_turned, lp_rows, b_proj, t2_ready, t2_normed, xb_ready = (
            sem("lp_turned"), sem("lp_rows"), sem("b_proj"), sem("t2_ready"), sem("t2_normed"), sem("xb_ready"))

        def per_group(name, per=1, primed=0):
            return PerGroup(sem(name), per, primed)

        r_new, vd_zero, r_normed, xc_ready = sem("r_new"), sem("vd_zero"), sem("r_normed"), sem("xc_ready")
        r_new_in = PerGroup(r_new, 1, 0)
        r_newer = PerGroup(r_new, 1, 1)
        c_normed, c_turned, hn_rows = per_group("c_normed"), per_group("c_turned"), per_group("hn_rows", 1, 1)
        proj, rotated, summed = per_group("proj", 4), per_group("rotated", 4, 1), per_group("summed", 2, 1)
        v_done, v_ready = per_group("v_done"), per_group("v_ready", 1, 1)
        g_done, th_ready, sg_ready = per_group("g_done"), per_group("th_ready"), per_group("sg_ready", 1, 1)
        k_spread, q_spread = per_group("k_spread"), per_group("q_spread")
        k_turned, k_tokens = per_group("k_turned", 2), per_group("k_tokens", 2, 1)
        scores, masked = per_group("scores", 4), per_group("masked", 4, 1)
        state_done, states = per_group("state_done", 2), per_group("states", 2, 1)
        added, yt_rows, y_turned = per_group("added", 1, 1), per_group("yt_rows", 1, 1), per_group("y_turned")
        centred, squared, y_unit = per_group("centred", 1, 1), per_group("squared"), per_group("y_unit")
        gy_ready, gy_turned, gy_rows = per_group("gy_ready"), per_group("gy_turned"), per_group("gy_rows", 1, 1)
        wo_done, r_mid = per_group("wo_done"), per_group("r_mid", 1, 1)
        f_normed, f_turned, f_rows = per_group("f_normed"), per_group("f_turned"), per_group("f_rows", 1, 1)
        w1_done, gelu_ready, w2_done = per_group("w1_done", 2), per_group("gelu_ready", 2, 1), per_group("w2_done")
        primed = (hn_rows, rotated, summed, v_ready, sg_ready, k_tokens, masked, states, added, yt_rows, centred,
                  gy_rows, r_mid, f_rows, gelu_ready)
        FILLS = {
            "turn1": ((0, hn_rows, 1),), "heads": ((0, centred, 1),), "out_turn": ((0, gy_rows, 1),),
            "ffn_turn": ((0, f_rows, 1),),
            "rotate": ((1, rotated, 1), (4, rotated, 2), (5, rotated, 3), (1, rotated, 4)),
            "values": ((4, v_ready, 1),), "gate": ((1, sg_ready, 1),),
            "keys": ((4, k_tokens, 1), (1, k_tokens, 2)), "states": ((4, states, 1), (5, states, 2)),
            "out": ((5, r_mid, 1),), "ffn_up": ((1, gelu_ready, 1), (4, gelu_ready, 2)), "ffn_down": ((5, r_newer, 1),)}
        d_normed, d_turned, d_rows, logits_done, shifted, exps, chosen, oh_turned, oh_rows = (
            per_group("d_normed"), per_group("d_turned"), per_group("d_rows"), per_group("expert_logits"),
            per_group("shifted"), per_group("exps"), per_group("chosen"), per_group("oh_turned"), per_group("oh_rows"))
        t3_normed, xd_ready = sem("t3_normed"), sem("xd_ready")
        hidden, h_ready, expert_out, mixed = (
            [sem(f"{name}{g}") for g in range(G)] for name in ("hidden", "h_ready", "expert_out", "mixed"))
        FILLS.update({"d_turn": ((1, d_rows, 1),), "logits": ((1, shifted, 1),), "oh_turn": ((5, oh_rows, 1),)})

        def group(g):
            return slice(g * GC, (g + 1) * GC)

        def tile(t):
            return slice(t * P, (t + 1) * P)

        def split_levels(eng, own, tiles, low, high):
            for level in range(low, high):
                n = 1 << level
                now, then = (LpA, LpB) if level % 2 else (LpB, LpA)
                right, left = then[:, tiles, 1:2 * n:2], then[:, tiles, 0:2 * n:2]
                own.put(eng.tensor_tensor(right, now[:, tiles, 0:n], Gates[:, tiles, n - 1:2 * n - 1], ALU.mult))
                own.settle()
                ins = eng.tensor_tensor(left, now[:, tiles, 0:n], right, ALU.subtract)
                if level < high - 1:
                    own.put(ins)
                    own.settle()
            return ins

        block = ctx.enter_context(nc.Block())

        @block.sync
        def _(sync):
            x_tiles = x.rearrange("b (h p) d -> p (b h) d", p=P)
            for g in range(G):
                sync.dma_start(X3[:, g * GT:(g + 1) * GT, :], x_tiles[:, g * GT:(g + 1) * GT, :]).then_inc(x_in[g], 16)
                if g == 0:
                    sync.dma_start(ident, const[:, CS["ident"]]).then_inc(ident_in, 16)
                    sync.dma_start(Wa[:], wa).then_inc(wa_in, 16)
            sync.dma_start(Sel[:], sel).then_inc(sel_in, 16)
            rest = slice(CS["ident"].stop, CS_W)
            sync.dma_start(Cs[:, rest], const[:, rest]).then_inc(const_in, 16)
            sync.dma_start(Wb[:], wb).then_inc(wb_in, 16)
            sync.dma_start(Wd[:], wd).then_inc(wd_in, 16)
            parts = ((slice(WL["qk"].start, WL["g"].stop), qkvg_in), (slice(WL["wo"].start, WL["gn"].stop), out_in),
                     (slice(WL["w1"].start, WL["w2"].stop), ffn_in))
            for cols, landed in parts:
                sync.dma_start(Wl[:, cols], wl[0, :, cols]).then_inc(landed, 16)
            sync.dma_start(Lnc[:], lnc).then_inc(lnc_in, 16)
            with sync.Fori(0, LAYERS - 1) as layer:
                nxt = wl[bass.ds(layer + 1, 1)].rearrange("a p c -> (a p) c")
                for done in (proj, v_done, g_done):
                    sync.wait_ge(*done.at((layer, 0), G - 1))
                sync.dma_start(Wl[:, parts[0][0]], nxt[:, parts[0][0]]).then_inc(qkvg_in, 16)
                sync.wait_ge(*wo_done.at((layer, 0), G - 1))
                sync.dma_start(Wl[:, parts[1][0]], nxt[:, parts[1][0]]).then_inc(out_in, 16)
                sync.wait_ge(*w2_done.at((layer, 0), G - 1))
                sync.dma_start(Wl[:, parts[2][0]], nxt[:, parts[2][0]]).then_inc(ffn_in, 16)
            out_tiles = out.rearrange("b (h p) d -> p (b h) d", p=P)
            for g in range(G):
                sync.wait_ge(xd_ready, g + 1)
                sync.dma_start(out_tiles[:, g * GT:(g + 1) * GT, :], X3[:, g * GT:(g + 1) * GT, :]).then_inc(stored, 16)
            sync.wait_ge(stored, 16 * G)

        @block.gpsimd
        def _(pool):
            own = Steps(pool, pol)
            norms = Counter()

            def rstd(g):
                pool.wait_ge(var_ready, norms.next())
                own.put(pool.tensor_tensor(ve[:, g * GT:(g + 1) * GT], mv3[:, g * GT:(g + 1) * GT, 1], eps[:, 0:GT], ALU.add))
                own.settle()
                pool.tensor_tensor(rs[:, g * GT:(g + 1) * GT], ve[:, g * GT:(g + 1) * GT], mhalf[:, 0:GT],
                                   ALU.pow).then_inc(rstd_ready, 1)

            def rstd_and_shift(g):
                tiles = slice(g * GT, (g + 1) * GT)
                pool.wait_ge(var_ready, norms.next())
                own.put(pool.tensor_tensor(ve[:, tiles], mv3[:, tiles, 1], eps[:, 0:GT], ALU.add))
                own.put(pool.tensor_tensor(shift[:, tiles], zeros[:, 0:GT], mv3[:, tiles, 0], ALU.subtract))
                own.settle()
                own.put(pool.tensor_tensor(rs[:, tiles], ve[:, tiles], mhalf[:, 0:GT], ALU.pow))
                own.settle()
                pool.tensor_tensor(shift[:, tiles], shift[:, tiles], rs[:, tiles], ALU.mult).then_inc(rstd_ready, 1)

            own.put(pool.memset(mhalf[:], -0.5))
            own.put(pool.memset(eps[:], EPS))
            own.put(pool.memset(zeros[:], 0.0))
            own.put(pool.memset(ones[:], 1.0))
            pool.memset(Xt3[:, :, 0:TAPS - 1], 0.0).then_inc(pads, 1)
            for h in range(HALVES):
                pool.memset(Da[:, h].rearrange("p (b s) -> p b s", s=S)[:, :, 0:1], 0.0).then_inc(scanned, 1)
            pool.memset(Crows[:, 1], 0.0).then_inc(hc_ready, 4)
            pool.memset(Bc[:, :], 0.0).then_inc(pads, 1)
            for i, event in enumerate(primed):
                pool.memset(scratch[:, 1 + i:2 + i], 0.0).then_inc(event.sem, event.per * G)
            own.settle()
            pool.wait_ge(wa_in, 16)
            for k in range(TAPS):
                last = pool.tensor_tensor(Wk[:, k, :], Wa[:, WA["x"]],
                                          Wa[:, WA["tap"]].rearrange("p (k c) -> p k c", k=TAPS)[:, k, :], ALU.mult)
                if k < TAPS - 1:
                    own.put(last)
            last.then_inc(conv_w, 1)
            pool.wait_ge(ident_in, 16)
            for h in range(HALVES):
                pool.tensor_scalar(DiagD[:, tile(h)], ident, Wa[:, WA["dskip"]][:, h:h + 1], None,
                                   ALU.mult).then_inc(d_diag, 1)
            for g in range(G):
                rstd(g)
            for g in range(G):
                part = group(g % 2)
                for h in range(HALVES):
                    pool.wait_ge(rounded, 2 * g + h + 1)
                    pool.tensor_tensor(Hc[:, h, part], Dbu[:, h, part], Hc[:, h, part], ALU.subtract).then_inc(log_rest, 1)
            pool.wait_ge(dt_ready, 2 * G)
            for q in range(2):
                with pool.Fori(0, NSTATE // 2) as pair:
                    for r in range(2):
                        s = pair * 2 + (q * NSTATE + r)
                        pool.wait_ge(c_copied, s + 1)
                        for h in range(HALVES):
                            pool.wait_ge(scanned, s * 2 + (h + 3))
                            pool.wait_ge(hc_used, pair * 4 + (q * (2 * NSTATE + 2) + 2 * r + h + 1))
                            pool.tensor_tensor(Hc[:, h], Hs[:, r, h], Crows[:, r], ALU.mult).then_inc(hc_ready, 1)
            pool.wait_ge(lnc_in, 16)

            def tree_step(what, g):
                xg = X3[:, g * GT:(g + 1) * GT, :]
                if what == "low_levels":
                    pool.wait_ge(gated, 2 * g + 2)
                    tiles = slice(g * GT, (g + 1) * GT)
                    one = ones[:, 0:GT].unsqueeze(2)
                    own.put(pool.tensor_tensor(LpA[:, tiles, 0:1], one, Gates[:, tiles, 0:1], ALU.subtract))
                    own.put(pool.tensor_copy(LpA[:, tiles, 1:2], Gates[:, tiles, 0:1]))
                    own.settle()
                    split_levels(pool, own, tiles, 1, LOW_LEVELS).then_inc(low_ready, 1)
                if (what, g) == ("low_levels", 0):
                    pool.wait_ge(hc_used, 2 * (2 * NSTATE + 2))
                    pool.wait_ge(y_gated, 2 * HALVES)
                    pool.memset(Va.rearrange("p c n -> p (c n)"), 0.0).then_inc(vd_zero, 1)
                if what == "t1":
                    rstd(g)
                if what in ("g_stats", "b_stats", "t2_stats", "rx_stats"):
                    rstd_and_shift(g)
                if what == "o_norm":
                    pool.wait_ge(o_normed, g + 1)
                    pool.tensor_tensor(xg, xg, T13[:, g * GT:(g + 1) * GT, :], ALU.add).then_inc(xa_ready, 1)
                if what == "t2_norm":
                    pool.wait_ge(t2_normed, g + 1)
                    pool.tensor_tensor(xg, xg, T23[:, g * GT:(g + 1) * GT, :], ALU.add).then_inc(xb_ready, 1)

            def layer_steps(order, turn):
                for what, part, g, ahead in order:
                    layer = (turn, ahead)
                    half = slice(g % 2 * GC, (g % 2 + 1) * GC)
                    if what in ("stats1", "stats2"):
                        rstd(g)
                    if what == "spread":
                        dst, halves = ((Kr, Tk), (Qr, Tq))[part]
                        pool.wait_ge(*added.at(layer, g - 2))
                        pool.wait_ge(*rotated.at(layer, g, 2 * part + 2))
                        pool.tensor_tensor(dst[:, half], halves[:, 0, half], halves[:, 1, half], ALU.add).then_inc(summed.sem, 1)
                    if what == "var":
                        cols = slice(g * 96 + 64, g * 96 + 96)
                        pool.wait_ge(var_ready, norms.next())
                        pool.tensor_tensor(gst[:, cols], gst[:, cols], mhalf[:], ALU.pow).then_inc(rstd_ready, 1)
                    if what == "scale":
                        pool.wait_ge(*y_unit.at(layer, g))
                        if g == 0:
                            pool.wait_ge(out_in, turn * 16 + 16 * (ahead + 1))
                        y = Yc[:, group(g)].rearrange("p (t d) -> p t d", d=D)
                        gn = Wl[:, WL["gn"]].rearrange("p (a d) -> p a d", a=2)
                        own.put(pool.tensor_tensor(y, y, gn[:, 0:1, :].broadcast_to((P, GT, D)), ALU.mult))
                        own.settle()
                        own.put(pool.tensor_tensor(y, y, gn[:, 1:2, :].broadcast_to((P, GT, D)), ALU.add))
                        own.settle()
                        pool.wait_ge(*sg_ready.at(layer, g))
                        pool.tensor_tensor(Yc[:, group(g)], Yc[:, group(g)], Sg[:, group(g)], ALU.mult).then_inc(gy_ready.sem, 1)

            for step in OPENING:
                if step[0] in TREE_STEPS:
                    tree_step(step[0], step[2])
                else:
                    layer_steps([step], 0)
            with pool.Fori(0, LAYERS - 1) as layer:
                own.enter(layer, PER_LAYER_POOL)
                norms.enter(layer, 3 * G)
                layer_steps(LAYER, layer)
                own.leave(LAYERS - 1)
                norms.leave(LAYERS - 1)
            for step in ENDING:
                what, part, g, _ = step
                xg = X3[:, g * GT:(g + 1) * GT, :]
                if what not in EXPERT_STEPS:
                    layer_steps([step], LAYERS - 1)
                if what in ("r_stats", "x_stats", "t_stats"):
                    rstd(g)
                if what == "r_norm":
                    pool.wait_ge(r_normed, g + 1)
                    pool.tensor_tensor(xg, xg, Hn3[:, g * GT:(g + 1) * GT, :], ALU.add).then_inc(xc_ready, 1)
                if what == "t_norm":
                    pool.wait_ge(t3_normed, g + 1)
                    pool.tensor_tensor(xg, xg, T33[:, g * GT:(g + 1) * GT, :], ALU.add).then_inc(xd_ready, 1)

        @block.scalar
        def _(act):
            own = Steps(act, act_steps)
            act.wait_ge(wa_in, 16)
            own.put(act.activation(Aneg, Wa[:, WA["alog"]], ACT.Exp))
            own.settle()
            act.mul(Aneg, Aneg, -1.0).then_inc(a_neg, 1)

            act.wait_ge(pads, 2)

            def input_rows(g):
                act.wait_ge(a_turned, g + 1)
                act.copy(Xt3[:, 2 * g:2 * g + 2, TAPS - 1:], bank[g % 2].rearrange("p (b s) -> p b s", b=2)).then_inc(a_rows, 1)

            input_rows(0)
            for g in range(G):
                act.wait_ge(bc_done, g + 1)
                act.copy(Bc[0:32, group(g)], bank[g % 2][0:32, :]).then_inc(bc_hi, 1)
                act.wait_ge(bc_rest, g + 1)
                act.copy(Mid[0:32, :], Rest[0:32, :]).then_inc(bc_mid, 1)
                act.wait_ge(bc_mid, g + 1)
                act.copy(Bc[32:64, group(g)], Mid[0:32, :]).then_inc(bc_ready, 1)
                if g + 1 < G:
                    input_rows(g + 1)
                act.preload_act_table_set("natural_log_exp_and_others")
                part = group(g % 2)
                for h in range(HALVES):
                    act.wait_ge(dtx_ready, 2 * g + h + 1)
                    own.put(act.activation(Hs[:, 1, h, part], Dt[:, h, group(g)], ACT.Abs))
                own.settle()
                for h in range(HALVES):
                    if g >= 2:
                        act.wait_ge(log_rest, 2 * (g - 2) + h + 1)
                    act.activation(Dbu[:, h, part], Hs[:, 1, h, part], ACT.Exp, scale=-1.0).then_inc(exp_ready, 1)
                for h in range(HALVES):
                    act.wait_ge(exp_ready, 2 * g + h + 1)
                    if g >= 2:
                        act.wait_ge(dt_ready, 2 * (g - 2) + h + 1)
                    act.activation(Hs[:, 0, h, part], Dbu[:, h, part], ACT.Ln, bias=1.0).then_inc(ln_ready, 1)
                for h in range(HALVES):
                    act.wait_ge(conv_done, 2 * g + h + 1)
                    act.activation(U[:, h, group(g)], bank[2 + h], ACT.Silu,
                                   bias=Wa[:, WA["conv_b"]][:, h:h + 1]).then_inc(u_ready, 1)
                for h in range(HALVES):
                    act.wait_ge(z_done, 2 * g + h + 1)
                    act.activation(Z[:, h, group(g)], bank[4 + h], ACT.Silu).then_inc(z_ready, 1)

            act.preload_act_table_set("natural_log_exp_and_others")
            act.wait_ge(dt_ready, 2 * G)
            for q in range(2):
                cols = slice(q * 1024, (q + 1) * 1024)
                with act.Fori(0, NSTATE // 2) as pair:
                    for r in range(2):
                        s = pair * 2 + (q * NSTATE + r)
                        for h in range(HALVES):
                            act.wait_ge(scanned, s * 2 + (h + 1))
                            seq = "p (b s) -> p b s"
                            act.activation(Da[:, h].rearrange(seq, s=S)[:, :, 1:], Dt[:, h, cols].rearrange(seq, s=S)[:, :, 1:],
                                           ACT.Exp, scale=Aneg[:, bass.ds(pair * 2 + (r + h * NSTATE), 1)]).then_inc(da_ready, 1)
                        act.wait_ge(c_rows, s + 1)
                        act.wait_ge(hc_ready, s * 2 + 2)
                        act.copy(Crows[:, r], psum[:, 6 * GC:8 * GC]).then_inc(c_copied, 1)

            def normalise(dst3, src3, what, g, done):
                act.wait_ge(rstd_ready, POWER_OF[what, g])
                for t in range(g * GT, (g + 1) * GT):
                    ins = act.activation(dst3[:, t, :], src3[:, t, :], ACT.Identity, bias=shift[:, t:t + 1], scale=rs[:, t:t + 1])
                ins.then_inc(done, 1)

            def tree_step(what, g):
                if what == "o_norm":
                    normalise(T13, T13, what, g, o_normed)
                if what == "b_norm":
                    normalise(Bn3, X3, what, g, b_normed)
                if what == "t2_norm":
                    normalise(T23, T23, what, g, t2_normed)
                if what == "rx_norm":
                    normalise(R3, X3, what, g, r_new)
                if what == "b_turn":
                    act.wait_ge(b_turned, g + 1)
                    act.copy(Bt[:, group(g)], bank[g % 2]).then_inc(b_rows_t, 1)
                if what == "logits":
                    for t in range(2 * g, 2 * g + 2):
                        act.wait_ge(logits, t + 1)
                        act.activation(Gates[:, 2 * t:2 * t + 2, :], bank[2 + t % 2], ACT.Sigmoid).then_inc(gated, 1)
                if what == "lp":
                    for h in range(2):
                        act.wait_ge(lp_turned, 2 * g + h + 1)
                        act.copy(LpT[:, g, h, :], bank[4 + h]).then_inc(lp_rows, 1)

            act.wait_ge(lnc_in, 16)
            act.wait_ge(const_in, 16)

            def layer_steps(order, turn):
                for what, part, g, ahead in order:
                    layer = (turn, ahead)
                    half = slice(g % 2 * GC, (g % 2 + 1) * GC)
                    chunks = slice(g % 2 * CHUNKS, (g % 2 + 1) * CHUNKS)
                    if what == "turn1":
                        act.wait_ge(*c_turned.at(layer, g))
                        act.activation(Ht[:, group(g)], bank[0], ACT.Identity, bias=Lnc[:, 1:2],
                                       scale=Lnc[:, 0:1]).then_inc(hn_rows.sem, 1)
                    if what == "values":
                        act.wait_ge(vd_zero, 1)
                        act.wait_ge(*v_done.at(layer, g))
                        act.wait_ge(*added.at(layer, g - 2))
                        for a in range(PARITY):
                            half_rows = slice(CHUNK * a, CHUNK * a + CHUNK)
                            dst = Va[half_rows, chunks, :].rearrange("p c (j w) -> p (c j) w", j=PAIR)[:, :, DH * a:DH * a + DH]
                            ins = act.copy(dst, bank[FILLS[what][0][0]][half_rows, :].rearrange("p (c i) -> p c i", i=DH))
                            if a == 0:
                                own.put(ins)
                        ins.then_inc(v_ready.sem, 1)
                    if what == "gate":
                        act.wait_ge(*g_done.at(layer, g))
                        act.activation(Th[:, half], bank[FILLS[what][0][0]], ACT.Tanh, scale=0.5).then_inc(th_ready.sem, 1)
                    if what == "spread":
                        rows, copies, masks, done = ((Kr, Ka, "parity", k_spread), (Qr, Qp, "pair", q_spread))[part]
                        act.wait_ge(*summed.at(layer, g, part + 1))
                        count = (PARITY, PAIR)[part]
                        for i in range(count):
                            ins = act.activation(copies[:, chunks, i * CHUNK:(i + 1) * CHUNK],
                                                 rows[:, half].rearrange("p (c n) -> p c n", n=CHUNK),
                                                 ACT.Identity, scale=Cs[:, CS[masks]][:, i:i + 1])
                            if i < count - 1:
                                own.put(ins)
                        ins.then_inc(done.sem, 1)
                    if what == "keys":
                        for b in range(2):
                            act.wait_ge(*k_turned.at(layer, g, b + 1))
                            act.copy(Kt[:, g % 2 * 2 + b, :], bank[FILLS[what][b][0]][:, 0:(SEQ_CHUNKS - 1) * P]).then_inc(k_tokens.sem, 1)
                    if what == "gather":
                        act.wait_ge(*added.at(layer, g))
                        act.copy(Yt[:, half], bank[6 + g % 2]).then_inc(yt_rows.sem, 1)
                    if what == "square":
                        act.wait_ge(*centred.at(layer, g))
                        act.square(Ys, Yc[:, group(g)]).then_inc(squared.sem, 1)
                    if what == "out_turn":
                        act.wait_ge(*gy_turned.at(layer, g))
                        act.mul(Gyt[:, half], bank[0], 0.5).then_inc(gy_rows.sem, 1)
                    if what == "ffn_turn":
                        act.wait_ge(*f_turned.at(layer, g))
                        act.activation(Ht[:, group(g)], bank[0], ACT.Identity, bias=Lnc[:, 1:2],
                                       scale=Lnc[:, 0:1]).then_inc(f_rows.sem, 1)
                    if what == "ffn_up":
                        for k in range(2):
                            act.wait_ge(*w1_done.at(layer, g, k + 1))
                            act.activation(Ft[:, group(2 * (g % 2) + k)], bank[FILLS[what][k][0]],
                                           ACT.Gelu_apprx_tanh).then_inc(gelu_ready.sem, 1)

            for step in OPENING:
                if step[0] in TREE_STEPS:
                    tree_step(step[0], step[2])
                else:
                    layer_steps([step], 0)
            act.preload_act_table(ACT.Gelu_apprx_tanh)
            with act.Fori(0, LAYERS - 1) as layer:
                own.enter(layer, PER_LAYER_SCALAR)
                layer_steps(LAYER, layer)
                own.leave(LAYERS - 1)

            one = (0, 0)
            for step in ENDING:
                what, part, g, _ = step
                if what not in EXPERT_STEPS:
                    layer_steps([step], LAYERS - 1)
                if what == "d_turn":
                    act.wait_ge(*d_turned.at(one, g))
                    act.copy(Dtr[:, group(g)], bank[FILLS[what][0][0]]).then_inc(d_rows.sem, 1)
                if what == "exps":
                    act.wait_ge(*shifted.at(one, g))
                    own_cols = slice(g * GT * EXPERTS, (g + 1) * GT * EXPERTS)
                    act.activation(ex[:, own_cols], lg[:, own_cols], ACT.Exp).then_inc(exps.sem, 1)
                if what == "oh_turn":
                    act.wait_ge(*oh_turned.at(one, g))
                    act.wait_ge(*added.at((LAYERS - 1, 0), G - 1))
                    act.copy(Oht[0:EXPERTS, group(g)], bank[FILLS[what][0][0]][0:EXPERTS, :]).then_inc(oh_rows.sem, 1)
                if what == "hidden":
                    n = HIDDEN.index((g, part))
                    act.wait_ge(hidden[g], part + 1)
                    if n >= HIDDEN_SLOTS:
                        before, e = HIDDEN[n - HIDDEN_SLOTS]
                        act.wait_ge(expert_out[before], e + 2)
                    else:
                        act.wait_ge(*added.at((LAYERS - 1, 0), G - 1))
                    act.activation(Hid[:, group(n % HIDDEN_SLOTS)], bank[2 + n % 2], ACT.Gelu,
                                   bias=Wd[:, WD["b1"]][:, part:part + 1]).then_inc(h_ready[g], 1)

        @block.vector
        def _(dve):
            own = Steps(dve, vec)
            norms = Counter()
            due = {}

            def stats(src3, g):
                tiles = range(g * GT, (g + 1) * GT)
                for t in tiles:
                    own.put(dve.bn_stats(st3[:, t, :], src3[:, t, :]))
                own.settle()
                own.put(dve.memset(scratch[:, 0:1], 0.0))
                for t in tiles:
                    ins = dve.bn_aggr(mv3[:, t, :], st3[:, t, :])
                    if t < tiles[-1]:
                        own.put(ins)
                ins.then_inc(var_ready, 1)
                due[g] = norms.next()

            def normalise(dst3, src3, g, done):
                dve.wait_ge(rstd_ready, due.pop(g))
                tiles = range(g * GT, (g + 1) * GT)
                for t in tiles:
                    ins = dve.tensor_scalar(dst3[:, t, :], src3[:, t, :], mv3[:, t, 0:1], rs[:, t:t + 1], ALU.subtract, ALU.mult)
                    if t < tiles[-1]:
                        own.put(ins)
                ins.then_inc(done, 1)

            dve.wait_ge(wa_in, 16)
            dve.wait_ge(dt_w, 1)
            dve.tensor_copy(Wdt, bank[7][:, 0:256]).then_inc(dt_wc, 1)
            for g in range(G + 1):
                if g < G:
                    dve.wait_ge(x_in[g], 16)
                    stats(X3, g)
                if g >= 1:
                    normalise(Xn3, X3, g - 1, a_normed)

            def step_size(g):
                part = group(g % 2)
                for h in range(HALVES):
                    dve.wait_ge(exp_ready, 2 * g + h + 1)
                    if g >= 2:
                        dve.wait_ge(dt_ready, 2 * (g - 2) + h + 1)
                    dve.tensor_scalar(Hc[:, h, part], Dbu[:, h, part], 1.0, -1.0, ALU.add, ALU.add).then_inc(rounded, 1)
                for h in range(HALVES):
                    dve.wait_ge(dtx_ready, 2 * g + h + 1)
                    dve.wait_ge(ln_ready, 2 * g + h + 1)
                    own.put(dve.scalar_tensor_tensor(Dt[:, h, group(g)], Dt[:, h, group(g)], 0.0, Hs[:, 0, h, part], ALU.max, ALU.add))
                own.settle()
                for h in range(HALVES):
                    dve.wait_ge(log_rest, 2 * g + h + 1)
                    dve.tensor_tensor(Dt[:, h, group(g)], Dt[:, h, group(g)], Hc[:, h, part], ALU.add).then_inc(dt_ready, 1)
                for h in range(HALVES):
                    dve.wait_ge(dt_ready, 2 * g + h + 1)
                    dve.wait_ge(u_ready, 2 * g + h + 1)
                    dve.tensor_tensor(Dtu[:, h, group(g)], Dt[:, h, group(g)], U[:, h, group(g)], ALU.mult).then_inc(dtu_ready, 1)

            for g in range(G):
                for h in range(HALVES):
                    b_dt = Wa[:, WA["b_dt"]][:, h:h + 1]
                    dve.wait_ge(dt_done, 2 * g + h + 1)
                    dve.tensor_scalar(Dt[:, h, group(g)], bank[6 + h], b_dt, None, ALU.add).then_inc(dtx_ready, 1)
                dve.wait_ge(bc_hi, g + 1)
                if g:
                    dve.wait_ge(bc_lo, g)
                dve.tensor_tensor(Rest[0:32, :], bank[g % 2][0:32, :], Bc[0:32, group(g)], ALU.subtract).then_inc(bc_rest, 1)
                dve.wait_ge(bc_mid, g + 1)
                dve.tensor_tensor(Bc[64:96, group(g)], Rest[0:32, :], Mid[0:32, :], ALU.subtract).then_inc(bc_lo, 1)
                if g:
                    step_size(g - 1)
            step_size(G - 1)
            dve.wait_ge(tree_w, 1)
            own.put(dve.tensor_copy(Wrq, bank[7][:, 0:256]))
            dve.tensor_copy(Wlv, bank[7][:, 256:512]).then_inc(tree_wc, 1)

            dve.wait_ge(dtu_ready, 2 * G)
            for q in range(2):
                cols = slice(q * 1024, (q + 1) * 1024)
                with dve.Fori(0, NSTATE // 2) as pair:
                    for r in range(2):
                        s = pair * 2 + (q * NSTATE + r)
                        dve.wait_ge(b_rows, s + 1)
                        for h in range(HALVES):
                            dve.wait_ge(scanned, s * 2 + (h + 1))
                            dve.tensor_tensor(Dbu[:, h], Dtu[:, h, cols], psum[:, 4 * GC:6 * GC], ALU.mult).then_inc(b_used, 1)
                        for h in range(HALVES):
                            dve.wait_ge(b_used, s * 2 + (h + 1))
                            dve.wait_ge(da_ready, s * 2 + (h + 1))
                            dve.wait_ge(hc_ready, s * 2 + (h + 1))
                            dve.tensor_tensor_scan(Hs[:, r, h], Da[:, h], Dbu[:, h], 0.0, ALU.mult, ALU.add).then_inc(scanned, 1)
                dve.wait_ge(z_ready, 8)
                for h in range(HALVES):
                    dve.wait_ge(hc_used, (q + 1) * (2 * NSTATE + 2) - 1 + h)
                    zz = Z[:, h, cols]
                    dve.tensor_tensor(zz, psum[:, 2 * h * GC:2 * (h + 1) * GC], zz, ALU.mult).then_inc(y_gated, 1)
            def tree_step(what, g):
                tiles = slice(g * GT, (g + 1) * GT)
                if what == "t1":
                    dve.wait_ge(y_proj, g + 1)
                    dve.tensor_tensor(T1[:, group(g)], bank[4 + g % 2], Xn[:, group(g)], ALU.add).then_inc(t1_ready, 1)
                    dve.wait_ge(t1_ready, g + 1)
                    stats(T13, g)
                if what == "g_norm":
                    dve.wait_ge(rstd_ready, due.pop(g))
                    for t in range(g * GT, (g + 1) * GT):
                        own.put(dve.scalar_tensor_tensor(T13[:, t, :], T13[:, t, :], mv3[:, t, 0:1], Wa[:, WA["ln_g"]],
                                                         ALU.subtract, ALU.mult))
                    own.settle()
                    for t in range(g * GT, (g + 1) * GT):
                        ins = dve.scalar_tensor_tensor(T13[:, t, :], T13[:, t, :], rs[:, t:t + 1], Wa[:, WA["ln_b"]],
                                                       ALU.mult, ALU.add)
                    ins.then_inc(g_scaled, 1)
                if what == "g_stats":
                    dve.wait_ge(g_scaled, g + 1)
                    stats(T13, g)
                if what == "o_norm":
                    due.pop(g)
                if what == "b_stats":
                    dve.wait_ge(xa_ready, g + 1)
                    stats(X3, g)
                if what == "b_norm":
                    due.pop(g)
                if what == "levels":
                    dve.wait_ge(low_ready, g + 1)
                    ins = split_levels(dve, own, tiles, LOW_LEVELS, DEPTH)
                    ins.then_inc(leaves, 1)
                if what == "b_proj":
                    dve.wait_ge(b_proj, g + 1)
                    bias = Wb[:, WB["bias"]].unsqueeze(1).broadcast_to((P, GT, D))
                    dve.tensor_tensor(T23[:, tiles, :], bank[6 + g % 2].rearrange("p (t d) -> p t d", d=D),
                                      bias, ALU.add).then_inc(t2_ready, 1)
                if what == "t2_stats":
                    dve.wait_ge(t2_ready, g + 1)
                    stats(T23, g)
                if what == "t2_norm":
                    due.pop(g)
                if what == "rx_stats":
                    dve.wait_ge(xb_ready, g + 1)
                    stats(X3, g)
                if what == "rx_norm":
                    due.pop(g)

            dve.wait_ge(const_in, 16)
            as3 = "p (m i) -> p m i"

            def layer_steps(order, turn):
                for what, part, g, ahead in order:
                    layer = (turn, ahead)
                    half = slice(g % 2 * GC, (g % 2 + 1) * GC)
                    sums, mean, var = (gst[:, g * 96 + 32 * k:g * 96 + 32 * (k + 1)] for k in range(3))
                    if what == "stats1":
                        dve.wait_ge(*r_new_in.at(layer, g))
                        stats(R3, g)
                    if what == "norm1":
                        normalise(Hn3, R3, g, c_normed.sem)
                    if what == "rotate":
                        for k in range(4):
                            dve.wait_ge(*proj.at(layer, g, k + 1))
                            if k % 2 == 0:
                                dve.wait_ge(*summed.at(layer, g - 2, k // 2 + 1))
                            dst = (Tk, Tq)[k // 2][:, k % 2, half].rearrange("p (b s) -> p b s", b=2)
                            table = Cs[:, CS[("tk", "tq")[k // 2]]].rearrange("p (a s) -> p a s", a=2)
                            dve.tensor_tensor(dst, bank[FILLS[what][k][0]].rearrange("p (b s) -> p b s", b=2),
                                              table[:, k % 2:k % 2 + 1, :].broadcast_to((P, 2, S)), ALU.mult).then_inc(rotated.sem, 1)
                    if what == "gate":
                        dve.wait_ge(*th_ready.at(layer, g))
                        dve.scalar_tensor_tensor(Sg[:, group(g)], Th[:, half], 1.0, bank[FILLS[what][0][0]], ALU.add, ALU.mult).then_inc(sg_ready.sem, 1)
                    if what == "scores":
                        dve.wait_ge(*scores.at(layer, g, part + 1))
                        if part == 0:
                            dve.wait_ge(*added.at(layer, g - 1))
                        by_query = "p (c q) -> p c q"
                        mask = Cs[:, CS["causal"]].unsqueeze(1).broadcast_to((P, 2 * PAIR, CHUNK))
                        att = Att[:, 2 * part:2 * part + 2, :].rearrange("p c n -> p (c n)").rearrange(by_query, q=CHUNK)
                        dve.tensor_tensor(att, bank[2 + part % 2].rearrange(by_query, q=CHUNK), mask, ALU.mult).then_inc(masked.sem, 1)
                    if what == "states":
                        for b in range(2):
                            dve.wait_ge(*state_done.at(layer, g, b + 1))
                            if b == 0:
                                dve.wait_ge(*added.at(layer, g - 2))
                            width = (SEQ_CHUNKS - 1) * P
                            own_block = Cs[:, CS["same_head"]].unsqueeze(1).broadcast_to((P, SEQ_CHUNKS - 1, P))
                            dve.tensor_tensor(States[:, g % 2 * 2 + b, :].rearrange("p (c f) -> p c f", f=P),
                                              bank[FILLS[what][b][0]][:, 0:width].rearrange("p (c f) -> p c f", f=P),
                                              own_block, ALU.mult).then_inc(states.sem, 1)
                    if what == "heads":
                        dve.wait_ge(*y_turned.at(layer, g))
                        own.put(dve.tensor_reduce(sums, bank[0].rearrange(as3, i=DH), AX, ALU.add))
                        own.settle()
                        own.put(dve.tensor_scalar(mean, sums, 1.0 / DH, None, ALU.mult))
                        own.settle()
                        dve.tensor_tensor(Yc[:, group(g)].rearrange(as3, i=DH), bank[0].rearrange(as3, i=DH),
                                          mean.unsqueeze(2).broadcast_to((P, 32, DH)), ALU.subtract).then_inc(centred.sem, 1)
                    if what == "var":
                        dve.wait_ge(*squared.at(layer, g))
                        own.put(dve.tensor_reduce(var, Ys.rearrange(as3, i=DH), AX, ALU.add))
                        own.settle()
                        dve.tensor_scalar(var, var, 1.0 / DH, EPS, ALU.mult, ALU.add).then_inc(var_ready, 1)
                        due["heads", g] = norms.next()
                    if what == "unit":
                        dve.wait_ge(rstd_ready, due.pop(("heads", g)))
                        y = Yc[:, group(g)].rearrange(as3, i=DH)
                        dve.tensor_tensor(y, y, var.unsqueeze(2).broadcast_to((P, 32, DH)), ALU.mult).then_inc(y_unit.sem, 1)
                    if what == "out":
                        dve.wait_ge(*wo_done.at(layer, g))
                        dve.tensor_tensor(R[:, group(g)], bank[FILLS[what][0][0]], R[:, group(g)], ALU.add).then_inc(r_mid.sem, 1)
                    if what == "stats2":
                        dve.wait_ge(*r_mid.at(layer, g))
                        stats(R3, g)
                    if what == "norm2":
                        normalise(Hn3, R3, g, f_normed.sem)
                    if what == "ffn_down":
                        dve.wait_ge(*w2_done.at(layer, g))
                        dve.tensor_tensor(R[:, group(g)], bank[FILLS[what][0][0]], R[:, group(g)], ALU.add).then_inc(r_new, 1)

            for step in OPENING:
                if step[0] in TREE_STEPS:
                    tree_step(step[0], step[2])
                else:
                    layer_steps([step], 0)
            with dve.Fori(0, LAYERS - 1) as layer:
                assert not due
                own.enter(layer, PER_LAYER_VECTOR)
                norms.enter(layer, 3 * G)
                layer_steps(LAYER, layer)
                own.leave(LAYERS - 1)
                norms.leave(LAYERS - 1)
            assert not due

            dve.wait_ge(wd_in, 16)
            one = (0, 0)

            def step_of(ins):
                own.put(ins)
                own.settle()

            def spread(v):
                return v.unsqueeze(2).broadcast_to((P, GT, EXPERTS))

            for step in ENDING:
                what, part, g, _ = step
                tiles = slice(g * GT, (g + 1) * GT)
                lg3, ex3, oh3, tmp3 = (v.rearrange("p (t e) -> p t e", e=EXPERTS)[:, tiles, :] for v in (lg, ex, oh, tmp))
                most, total, best, first = (red[:, i * T + g * GT:i * T + (g + 1) * GT] for i in range(4))
                if what not in EXPERT_STEPS:
                    layer_steps([step], LAYERS - 1)
                if what == "r_stats":
                    dve.wait_ge(*r_newer.at((LAYERS - 1, 0), g))
                    stats(R3, g)
                if what == "r_norm":
                    normalise(Hn3, R3, g, r_normed)
                if what == "x_stats":
                    dve.wait_ge(xc_ready, g + 1)
                    stats(X3, g)
                if what == "x_norm":
                    normalise(Dn3, X3, g, d_normed.sem)
                if what == "logits":
                    dve.wait_ge(*logits_done.at(one, g))
                    step_of(dve.tensor_tensor(lg3, bank[FILLS[what][0][0]][:, 0:GT * EXPERTS].rearrange("p (t e) -> p t e", e=EXPERTS),
                                              Wd[:, WD["bg"]].unsqueeze(1).broadcast_to((P, GT, EXPERTS)), ALU.add))
                    step_of(dve.tensor_reduce(most, lg3, AX, ALU.max))
                    dve.tensor_tensor(lg3, lg3, spread(most), ALU.subtract).then_inc(shifted.sem, 1)
                if what == "choose":
                    dve.wait_ge(*exps.at(one, g))
                    step_of(dve.tensor_reduce(total, ex3, AX, ALU.add))
                    step_of(dve.reciprocal(total, total))
                    step_of(dve.tensor_tensor(ex3, ex3, spread(total), ALU.mult))
                    step_of(dve.tensor_reduce(best, ex3, AX, ALU.max))
                    step_of(dve.tensor_tensor(oh3, ex3, spread(best), ALU.is_equal))
                    step_of(dve.tensor_tensor(tmp3, oh3, Cs[:, CS["rank"]].unsqueeze(1).broadcast_to((P, GT, EXPERTS)), ALU.mult))
                    step_of(dve.tensor_reduce(first, tmp3, AX, ALU.max))
                    dve.tensor_tensor(oh3, tmp3, spread(first), ALU.is_equal).then_inc(chosen.sem, 1)
                if what == "expert":
                    dst = bank[6 + RESULTS.index((g, part)) % 2]
                    dve.wait_ge(expert_out[g], part + 1)
                    if part == 0:
                        dve.tensor_copy(T3[:, group(g)], dst).then_inc(mixed[g], 1)
                        continue
                    dve.wait_ge(mixed[g], part)
                    dve.wait_ge(*chosen.at(one, g))
                    for k in range(GT):
                        t = g * GT + k
                        ins = dve.scalar_tensor_tensor(T33[:, t, :], dst[:, tile(k)], oh3[:, k, part - 1:part], T33[:, t, :],
                                                       ALU.mult, ALU.add)
                        if k < GT - 1:
                            own.put(ins)
                    ins.then_inc(mixed[g], 1)
                if what == "t_stats":
                    dve.wait_ge(mixed[g], EXPERTS + 1)
                    stats(T33, g)
                if what == "t_norm":
                    normalise(T33, T33, g, t3_normed)

        @block.tensor
        def _(pe):
            def turn_tiles(dst, src3, g):
                for k in range(GT):
                    ins = pe.transpose(dst[:, tile(k)], src3[:, g * GT + k, :], ident)
                return ins

            def tokens(dst, rows, weights, width=D):
                for k in range(GT):
                    for i, (r, w) in enumerate(zip(rows, weights)):
                        ins = pe.matmul(dst[:, k * width:(k + 1) * width], r[:, tile(k)], w, start=i == 0,
                                        stop=i == len(rows) - 1)
                return ins

            pe.wait_ge(wa_in, 16)
            pe.matmul(bank[7][:, 0:256], Wa[0:RANK, WA["dtin"]], Wa[0:RANK, WA["dtw"]], start=True, stop=True).then_inc(dt_w, 1)
            pe.wait_ge(ident_in, 16)
            pe.wait_ge(dt_wc, 1)
            pe.wait_ge(pads, 2)

            def turn_input(g):
                pe.wait_ge(a_normed, g + 1)
                if g >= 2:
                    pe.wait_ge(bc_rest, g - 1)
                turn_tiles(bank[g % 2], Xn3, g).then_inc(a_turned, 1)

            turn_input(0)
            for g in range(G):
                pe.wait_ge(a_rows, g + 1)
                seqs = slice(2 * g, 2 * g + 2)
                rows = Xt3[:, seqs, TAPS - 1:]
                for h in range(HALVES):
                    if g:
                        pe.wait_ge(dtx_ready, 2 * (g - 1) + h + 1)
                    pe.matmul(bank[6 + h], Wdt[:, tile(h)], rows, start=True, stop=True).then_inc(dt_done, 1)
                pe.matmul(bank[g % 2][0:32, :], Wa[:, WA["bc"]], rows, start=True, stop=True).then_inc(bc_done, 1)
                if g + 1 < G:
                    turn_input(g + 1)
                if g == 0:
                    pe.wait_ge(conv_w, 1)
                for h in range(HALVES):
                    if g:
                        pe.wait_ge(u_ready, 2 * (g - 1) + h + 1)
                    for k in range(TAPS):
                        ins = pe.matmul(bank[2 + h], Wk[:, k, tile(h)], Xt3[:, seqs, k:k + S], start=k == 0, stop=k == TAPS - 1)
                    ins.then_inc(conv_done, 1)
                for h in range(HALVES):
                    if g:
                        pe.wait_ge(z_ready, 2 * (g - 1) + h + 1)
                    pe.matmul(bank[4 + h], Wa[:, WA["z"]][:, tile(h)], rows, start=True, stop=True).then_inc(z_done, 1)

            pe.wait_ge(dtx_ready, 2 * G)
            pe.wait_ge(wb_in, 16)
            pe.matmul(bank[7][:, 0:256], Wb[:, WB["q"]], Wb[:, WB["routers"]], start=True, stop=True)
            for h in range(2):
                ins = pe.matmul(bank[7][:, 256 + h * P:256 + (h + 1) * P], Wb[:, WB["values"]][:, tile(h)], Wb[:, WB["wout"]],
                                start=True, stop=True)
            ins.then_inc(tree_w, 1)

            pe.wait_ge(sel_in, 16)
            pe.wait_ge(d_diag, HALVES)
            pe.wait_ge(z_ready, 2 * G)
            for q in range(2):
                def rows_of_state(first_bank, row, done):
                    for c in range(2):
                        ins = pe.matmul(bank[first_bank + c][:], Sel[:, bass.ds(row * P, P)], Bc[:, group(2 * q + c)],
                                        start=True, stop=True)
                    ins.then_inc(done, 1)

                def add_state(h):
                    for c in range(2):
                        ins = pe.matmul(bank[2 * h + c][:], ident, Hc[:, h, group(c)], start=False, stop=False,
                                        skip_group_check=True)
                    return ins

                pe.wait_ge(bc_ready, G)
                pe.wait_ge(bc_lo, G)
                if q:
                    pe.wait_ge(b_used, 2 * NSTATE)
                rows_of_state(4, 0, b_rows)
                if q:
                    pe.wait_ge(c_copied, NSTATE)
                else:
                    pe.wait_ge(tree_wc, 1)
                rows_of_state(6, NSTATE, c_rows)
                pe.wait_ge(u_ready, 2 * G)
                for h in range(HALVES):
                    if q:
                        pe.wait_ge(y_gated, h + 1)
                    for c in range(2):
                        ins = pe.matmul(bank[2 * h + c], DiagD[:, tile(h)], U[:, h, group(2 * q + c)], start=True,
                                        stop=False, skip_group_check=True)
                    ins.then_inc(hc_used, 1)
                base = q * NSTATE
                pe.wait_ge(b_used, 2 * base + 2)
                rows_of_state(4, 1, b_rows)
                pe.wait_ge(c_copied, base + 1)
                rows_of_state(6, 1 + NSTATE, c_rows)
                pe.wait_ge(hc_ready, 2 * base + 5)
                add_state(0).then_inc(hc_used, 1)
                with pe.Fori(0, NSTATE - 2) as n:
                    pe.wait_ge(b_used, n * 2 + (2 * base + 4))
                    rows_of_state(4, n + 2, b_rows)
                    pe.wait_ge(c_copied, n + (base + 2))
                    rows_of_state(6, n + (2 + NSTATE), c_rows)
                    pe.wait_ge(hc_ready, n * 2 + (2 * base + 6))
                    add_state(1).then_inc(hc_used, 1)
                    pe.wait_ge(hc_ready, n * 2 + (2 * base + 7))
                    add_state(0).then_inc(hc_used, 1)
                for i, h in enumerate((1, 0, 1)):
                    pe.wait_ge(hc_ready, 2 * base + 2 * NSTATE + 2 + i)
                    add_state(h).then_inc(hc_used, 1)
            pe.wait_ge(y_gated, 4)

            def tree_step(what, g):
                if what == "y_proj":
                    if g >= 2:
                        pe.wait_ge(t1_ready, g - 1)
                    tokens(bank[4 + g % 2], [Z[:, h, group(g)] for h in range(HALVES)],
                           [Wa[:, WA["out"]][:, tile(h)] for h in range(HALVES)]).then_inc(y_proj, 1)
                if what == "b_turn":
                    pe.wait_ge(b_normed, g + 1)
                    if g >= 2:
                        pe.wait_ge(b_rows_t, g - 1)
                    turn_tiles(bank[g % 2], Bn3, g).then_inc(b_turned, 1)
                if what == "logits":
                    pe.wait_ge(b_rows_t, g + 1)
                    for k in range(GT):
                        t = g * GT + k
                        if k % 2 == 0 and t >= 4:
                            pe.wait_ge(gated, t // 2 - 1)
                        ins = pe.matmul(bank[2 + t // 2 % 2][:, (k % 2) * LEAVES:(k % 2 + 1) * LEAVES], Bt[:, tile(t)], Wrq,
                                        start=True, stop=True)
                        if k % 2:
                            ins.then_inc(logits, 1)
                if what == "lp":
                    pe.wait_ge(leaves, g + 1)
                    for h in range(2):
                        if g:
                            pe.wait_ge(lp_rows, 2 * (g - 1) + h + 1)
                        else:
                            pe.wait_ge(t1_ready, G)
                        for k in range(GT):
                            ins = pe.transpose(bank[4 + h][:, tile(k)], LpB[:, g * GT + k, tile(h)], ident)
                        ins.then_inc(lp_turned, 1)
                if what == "b_proj":
                    pe.wait_ge(lp_rows, 2 * g + 2)
                    if g >= 2:
                        pe.wait_ge(t2_ready, g - 1)
                    tokens(bank[6 + g % 2], [LpT[:, g, h, :] for h in range(2)], [Wlv[:, tile(h)] for h in range(2)]).then_inc(b_proj, 1)

            held = {}

            def claim(what, i, layer, g):
                b, reader, k = FILLS[what][i]
                for event, of, at_group, nth in held.get(b, ()):
                    pe.wait_ge(*event.at(of, at_group, nth))
                held[b] = [(reader, layer, g, k)]
                return bank[b]

            def last_fills(order, turn, shift):
                return {b: (reader, (turn, ahead + shift), g, k) for what, _, g, ahead in order for b, reader, k in FILLS.get(what, ())}

            def layer_steps(order, turn):
                for what, part, g, ahead in order:
                    layer = (turn, ahead)
                    half = slice(g % 2 * GC, (g % 2 + 1) * GC)
                    chunk0, seq0 = g % 2 * CHUNKS, g % 2 * 2
                    if what == "turn1":
                        pe.wait_ge(*c_normed.at(layer, g))
                        turn_tiles(claim(what, 0, layer, g), Hn3, g).then_inc(c_turned.sem, 1)
                    if what == "rotate":
                        pe.wait_ge(*hn_rows.at(layer, g))
                        if g == 0:
                            pe.wait_ge(qkvg_in, turn * 16 + 16 * (ahead + 1))
                        for k in range(4):
                            pe.matmul(claim(what, k, layer, g), Wl[:, WL["qk"]][:, tile(k)], Ht[:, group(g)], start=True,
                                      stop=True).then_inc(proj.sem, 1)
                    if what == "values":
                        dst = claim(what, 0, layer, g)
                        for c in range(CHUNKS):
                            for a in range(PARITY):
                                cols = slice(g * GC + c * CHUNK, g * GC + (c + 1) * CHUNK)
                                ins = pe.matmul(dst[a * CHUNK:(a + 1) * CHUNK, c * CHUNK:(c + 1) * CHUNK], Ht[:, cols],
                                                Wl[:, WL["v"]][:, a * (D // 2):(a + 1) * (D // 2)], start=True, stop=True)
                        ins.then_inc(v_done.sem, 1)
                    if what == "gate":
                        tokens(claim(what, 0, layer, g), [Ht[:, group(g)]], [Wl[:, WL["g"]]]).then_inc(g_done.sem, 1)
                    if what == "keys":
                        pe.wait_ge(*k_spread.at(layer, g))
                        for b in range(2):
                            dst = claim(what, b, layer, g)
                            for c in range(SEQ_CHUNKS - 1):
                                ins = pe.transpose(dst[:, tile(c)], Ka[:, chunk0 + b * SEQ_CHUNKS + c, :], ident)
                            ins.then_inc(k_turned.sem, 1)
                    if what == "scores":
                        if part == 0:
                            pe.wait_ge(*q_spread.at(layer, g))
                        pe.wait_ge(*masked.at(layer, g, part - 1))
                        for c in range(2):
                            i = chunk0 + 2 * part + c
                            ins = pe.matmul(bank[2 + part % 2][:, c * 256:(c + 1) * 256], Ka[:, i, :], Qp[:, i, :], start=True, stop=True)
                        ins.then_inc(scores.sem, 1)
                    if what == "states":
                        pe.wait_ge(*v_ready.at(layer, g))
                        for b in range(2):
                            pe.wait_ge(*k_tokens.at(layer, g, b + 1))
                            dst = claim(what, b, layer, g)
                            for c in range(SEQ_CHUNKS - 1):
                                ins = pe.matmul(dst[:, tile(c)], Kt[:, seq0 + b, tile(c)], Va[:, chunk0 + b * SEQ_CHUNKS + c, :],
                                                start=True, stop=True)
                            ins.then_inc(state_done.sem, 1)
                    if what == "mix":
                        pe.wait_ge(*yt_rows.at(layer, g - 2))
                        for b in range(2):
                            y = bank[6 + g % 2][:, b * S:(b + 1) * S]
                            pe.wait_ge(*states.at(layer, g, b + 1))
                            for c in range(SEQ_CHUNKS - 1):
                                later = slice((c + 1) * CHUNK, S)
                                pe.matmul(y[:, later], States[:, seq0 + b, tile(c)], Qr[:, half][:, b * S:(b + 1) * S][:, later],
                                          start=b == c == 0, stop=False, skip_group_check=True)
                            pe.wait_ge(*masked.at(layer, g, 2 * b + 2))
                            for c in range(SEQ_CHUNKS):
                                for j in range(PAIR):
                                    rows = slice(2 * DH * j, 2 * DH * (j + 1))
                                    ins = pe.matmul(y[rows, c * CHUNK:(c + 1) * CHUNK], Va[:, chunk0 + b * SEQ_CHUNKS + c, rows],
                                                    Att[:, b * SEQ_CHUNKS + c, j * CHUNK:(j + 1) * CHUNK], start=False,
                                                    stop=True, skip_group_check=True)
                        ins.then_inc(added.sem, 1)
                    if what == "heads":
                        pe.wait_ge(*yt_rows.at(layer, g))
                        dst = claim(what, 0, layer, g)
                        for k in range(GT):
                            ins = pe.transpose(dst[:, tile(k)], Yt[:, half][:, tile(k)], ident)
                        ins.then_inc(y_turned.sem, 1)
                    if what == "out_turn":
                        pe.wait_ge(*gy_ready.at(layer, g))
                        turn_tiles(claim(what, 0, layer, g), Yc.rearrange("p (t d) -> p t d", d=D), g).then_inc(gy_turned.sem, 1)
                    if what == "out":
                        pe.wait_ge(*gy_rows.at(layer, g))
                        if g == 0:
                            pe.wait_ge(out_in, turn * 16 + 16 * (ahead + 1))
                        tokens(claim(what, 0, layer, g), [Gyt[:, half]], [Wl[:, WL["wo"]]]).then_inc(wo_done.sem, 1)
                    if what == "ffn_turn":
                        pe.wait_ge(*f_normed.at(layer, g))
                        turn_tiles(claim(what, 0, layer, g), Hn3, g).then_inc(f_turned.sem, 1)
                    if what == "ffn_up":
                        if g == 0:
                            pe.wait_ge(ffn_in, turn * 16 + 16 * (ahead + 1))
                        pe.wait_ge(*f_rows.at(layer, g))
                        for k in range(2):
                            pe.matmul(claim(what, k, layer, g), Wl[:, WL["w1"]][:, tile(k)], Ht[:, group(g)], start=True,
                                      stop=True).then_inc(w1_done.sem, 1)
                    if what == "ffn_down":
                        pe.wait_ge(*gelu_ready.at(layer, g))
                        tokens(claim(what, 0, layer, g), [Ft[:, group(2 * (g % 2) + j)] for j in range(2)],
                               [Wl[:, WL["w2"]][:, tile(j)] for j in range(2)]).then_inc(w2_done.sem, 1)

            for step in OPENING:
                if step[0] in TREE_STEPS:
                    tree_step(step[0], step[2])
                    continue
                if step[0] == "turn1" and step[2] == 0:
                    pe.wait_ge(b_rows_t, G)
                if step[0] == "rotate" and step[2] == 0:
                    assert OPENING.index(step) > OPENING.index(("b_proj", 0, G - 1, 0))
                    pe.wait_ge(t2_ready, G)
                layer_steps([step], 0)
            with pe.Fori(0, LAYERS - 1) as layer:
                before, first = last_fills(LAYER, layer, -1), last_fills(OPENING, layer, 0)
                for b in before:
                    held[b] = [before[b]] + ([first[b]] if b in first and first[b][1:] != before[b][1:] else [])
                layer_steps(LAYER, layer)
            held.update({b: [e] for b, e in last_fills(LAYER, LAYERS - 2, 0).items()})

            pe.wait_ge(wd_in, 16)
            one = (0, 0)
            for step in ENDING:
                what, part, g, _ = step
                if what not in EXPERT_STEPS:
                    layer_steps([step], LAYERS - 1)
                if what == "d_turn":
                    pe.wait_ge(*d_normed.at(one, g))
                    turn_tiles(claim(what, 0, one, g), Dn3, g).then_inc(d_turned.sem, 1)
                if what == "logits":
                    pe.wait_ge(*d_rows.at(one, g))
                    tokens(claim(what, 0, one, g), [Dtr[:, group(g)]], [Wd[:, WD["gate"]]], EXPERTS).then_inc(logits_done.sem, 1)
                if what == "oh_turn":
                    pe.wait_ge(*chosen.at(one, g))
                    dst = claim(what, 0, one, g)
                    for k in range(GT):
                        ins = pe.transpose(dst[0:EXPERTS, tile(k)], oh[:, (g * GT + k) * EXPERTS:(g * GT + k + 1) * EXPERTS], ident)
                    ins.then_inc(oh_turned.sem, 1)
                if what == "hidden":
                    n = HIDDEN.index((g, part))
                    if n >= 2:
                        before, e = HIDDEN[n - 2]
                        pe.wait_ge(h_ready[before], e + 1)
                    else:
                        pe.wait_ge(*masked.at((LAYERS - 1, 0), G - 1))
                    pe.wait_ge(*d_rows.at(one, g))
                    pe.matmul(bank[2 + n % 2], Wd[:, WD["w1"]][:, tile(part)], Dtr[:, group(g)], start=True,
                              stop=True).then_inc(hidden[g], 1)
                if what == "expert":
                    n = RESULTS.index((g, part))
                    dst = bank[6 + n % 2]
                    if n >= 2:
                        before, e = RESULTS[n - 2]
                        pe.wait_ge(mixed[before], e + 1)
                    else:
                        pe.wait_ge(*yt_rows.at((LAYERS - 1, 0), G - 1))
                    if part == 0:
                        pe.wait_ge(*oh_rows.at(one, g))
                        tokens(dst, [Oht[0:EXPERTS, group(g)]], [Wd[0:EXPERTS, WD["b2"]]]).then_inc(expert_out[g], 1)
                    else:
                        pe.wait_ge(h_ready[g], part)
                        slot = HIDDEN.index((g, part - 1)) % HIDDEN_SLOTS
                        tokens(dst, [Hid[:, group(slot)]], [Wd[:, WD["w2"]][:, tile(part - 1)]]).then_inc(expert_out[g], 1)


def _pack(width, where, parts):
    out = np.zeros((P, width), np.float32)
    for name, a in parts.items():
        a = a.reshape(a.shape[0], -1)
        out[: a.shape[0], where[name].start : where[name].start + a.shape[1]] = a
    return out


def _columns(v):
    return np.ascontiguousarray(v.reshape(-1, P).T)


def _everywhere(v):
    return np.broadcast_to(v.reshape(1, -1), (P, v.size))


def _rotated(w):
    return np.concatenate([w, w.reshape(D, D // 2, 2)[..., ::-1].reshape(D, D)], 1)


def kernel(**inputs):
    import concourse.bacc as _bacc
    import ml_dtypes
    from concourse.bass_utils import run_bass_kernel_spmd as _run

    a = {k: np.asarray(v) for k, v in inputs.items()}
    win = a["L0_attn_W_in"]
    alog = a["L0_attn_A_log"].reshape(HALVES, P, NSTATE).transpose(1, 0, 2)
    taps = a["L0_attn_conv_w"][:, 0, :].T
    wa = _pack(WA_W, WA, {
        "x": win[:256].T, "z": win[256:512].T, "bc": win[512:544].T, "dtin": win[544:552],
        "dtw": a["L0_attn_W_dt"].T, "tap": _everywhere(taps), "out": a["L0_attn_W_out"].T.reshape(HALVES, P, D).transpose(1, 0, 2),
        "conv_b": _columns(a["L0_attn_conv_b"]), "b_dt": _columns(a["L0_attn_b_dt"]), "alog": alog,
        "dskip": _columns(a["L0_attn_D"]), "ln_g": _everywhere(a["L0_attn_ln_g"]), "ln_b": _everywhere(a["L0_attn_ln_b"])})
    wb = _pack(WB_W, WB, {
        "q": a["L0_ffn_Wq"], "routers": a["L0_ffn_routers"].T, "values": a["L0_ffn_leaf_values"].T,
        "wout": a["L0_ffn_Wout_w"].T, "bias": _everywhere(a["L0_ffn_Wout_b"])})
    wl = np.stack([_pack(WL_W, WL, {
        "qk": np.concatenate([_rotated(a["L1_attn_Wk"][i]), _rotated(a["L1_attn_Wq"][i])], 1),
        "v": a["L1_attn_Wv"][i].reshape(D, PAIR, PARITY, DH).transpose(0, 2, 1, 3), "g": a["L1_attn_Wg"][i], "wo": a["L1_attn_Wo"][i],
        "gn": np.concatenate([_everywhere(a["L1_attn_gn_scale"][i]), _everywhere(a["L1_attn_gn_bias"][i])], 1),
        "w1": a["L1_attn_W1"][i], "w2": a["L1_attn_W2"][i].reshape(2, P, D).transpose(1, 0, 2)})
        for i in range(LAYERS)])
    wd = _pack(WD_W, WD, {
        "w1": a["L1_ffn_W1"].transpose(1, 0, 2), "w2": a["L1_ffn_W2"].transpose(1, 0, 2), "b1": a["L1_ffn_b1"].T,
        "gate": a["L1_ffn_Wg"], "bg": _everywhere(a["L1_ffn_bg"]), "b2": a["L1_ffn_b2"]})
    lnc = np.stack([a["L1_attn_ln_scale"], a["L1_attn_ln_bias"]], 1)
    arrays = {"x": a["L0_attn_x"], "wa": wa, "wb": wb, "wl": wl, "wd": wd, "lnc": lnc, "const": constants(),
              "sel": selectors().astype(ml_dtypes.bfloat16)}
    nc = _bacc.Bacc("TRN2", target_bir_lowering=False, num_devices=1)
    named = {}
    for name, v in arrays.items():
        arrays[name] = v = np.ascontiguousarray(v)
        named[name] = nc.dram_tensor(name, v.shape, mybir.dt.from_np(v.dtype), kind="ExternalInput").ap()
    out = nc.dram_tensor("out", (B, S, D), F32, kind="ExternalOutput").ap()
    four_blocks(nc, out=out, **named)
    r = _run(nc, [arrays], core_ids=[0])
    return r.results[0]["out"]
```
